# Optimizing a Trainium2 kernel written in Bass

```python
import numpy as np
import jax
import jax.numpy as jnp

def _softmax(x, axis=-1):
    return jax.nn.softmax(x, axis=axis)

def _gelu(x):
    return jax.nn.gelu(x, approximate=True)

def _silu(x):
    return jax.nn.silu(x)

def _sigmoid(x):
    return jax.nn.sigmoid(x)

def _layernorm(x, axis=-1, eps=1e-05):
    m = jnp.mean(x, axis=axis, keepdims=True)
    v = jnp.var(x, axis=axis, keepdims=True)
    return (x - m) / jnp.sqrt(v + eps)

def _scatter_add(tgt, idx, src, axis=0):
    return tgt.at[idx].add(src)

def _segment_sum(src, seg, n):
    return jax.ops.segment_sum(src, seg, n)
kernel_name = 'mk_decoder_preln_d2_seqx_r8_7d42bb'

def setup_inputs(seed: int=0):
    np.random.seed(seed)
    _w = jnp.asarray

    def _rec_inputs():
        import jax
        import jax.numpy as jnp
        _rk = jax.random.key(seed)
        x = -0.0002928 + 1 * jax.random.normal(jax.random.fold_in(_rk, 1), (2, 512, 128), jnp.float32)
        _lenS = 512 - jax.random.randint(jax.random.fold_in(_rk, 7), (2,), 0, max(1, 512 // 4) + 1, jnp.int32)
        _lenS2 = 77 - jax.random.randint(jax.random.fold_in(_rk, 8), (2,), 0, max(1, 77 // 4) + 1, jnp.int32)
        _ctx_1024P = jax.random.normal(jax.random.fold_in(_rk, 11), (2, 16, 128), jnp.float32)
        _ctx_1024c = jax.random.dirichlet(jax.random.fold_in(_rk, 511), 0.3 * jnp.ones((16,), jnp.float32), (2, 77))
        _ctx_1024t = jnp.einsum('bsk,bkd->bsd', _ctx_1024c, _ctx_1024P)
        _ctx_1024t = _ctx_1024t * jax.lax.rsqrt(jnp.mean(jnp.square(_ctx_1024t)) + 1e-12) * 0.953939
        ctx_1024 = -1.39393e-06 + 0.999914 * (_ctx_1024t + 0.3 * jax.random.normal(jax.random.fold_in(_rk, 611), (2, 77, 128), jnp.float32))
        return (x, ctx_1024)
    x, ctx_1024 = _rec_inputs()

    def _L0_attn_setup():
        import math
        import jax, jax.numpy as jnp
        import numpy as np
        B, S, D, H = (4, 256, 128, 16)
        HD = D // H
        SAMPLING_FACTOR = 5.0
        key = jax.random.key(seed)
        ks = jax.random.split(key, 6)
        std = 1.0 / math.sqrt(D)
        inp = {'x': jax.random.normal(ks[0], (B, S, D), dtype=jnp.float32), 'Wq': jax.random.normal(ks[1], (D, D), dtype=jnp.float32) * std, 'bq': jnp.zeros((D,), dtype=jnp.float32), 'Wk': jax.random.normal(ks[2], (D, D), dtype=jnp.float32) * std, 'bk': jnp.zeros((D,), dtype=jnp.float32), 'Wv': jax.random.normal(ks[3], (D, D), dtype=jnp.float32) * std, 'bv': jnp.zeros((D,), dtype=jnp.float32), 'Wo': jax.random.normal(ks[4], (D, D), dtype=jnp.float32) * std, 'bo': jnp.zeros((D,), dtype=jnp.float32), 'sample_idx': jax.random.randint(ks[5], (S,), 0, S, dtype=jnp.int32)}
        return inp
    _L0_attn_all = _L0_attn_setup()
    _L0_attn_in = {k: v for k, v in _L0_attn_all.items() if k in ('Wq', 'bq', 'Wk', 'bk', 'Wv', 'bv', 'Wo', 'bo', 'sample_idx')}
    del _L0_attn_all

    def _L0_xattn_setup():
        import jax, jax.numpy as jnp
        import numpy as np
        D_MODEL = 128
        NUM_HEADS = 16
        D_K = D_MODEL // NUM_HEADS
        SCALE = float(np.sqrt(D_K))

        def _split_heads(x):
            B, S, _ = x.shape
            return x.reshape(B, S, NUM_HEADS, D_K).transpose(0, 2, 1, 3)
        key = jax.random.key(seed)
        ks = jax.random.split(key, 11)
        B, S, D = (2, 256, D_MODEL)

        def lin(kw):
            lim = float(np.sqrt(6.0 / (D + D)))
            return jax.random.uniform(kw, (D, D), jnp.float32, -lim, lim)
        return {'q': jax.random.normal(ks[0], (B, S, D), jnp.float32), 'k': jax.random.normal(ks[1], (B, S, D), jnp.float32), 'v': jax.random.normal(ks[2], (B, S, D), jnp.float32), 'Wq': lin(ks[3]), 'bq': jnp.zeros((D,), jnp.float32), 'Wk': lin(ks[4]), 'bk': jnp.zeros((D,), jnp.float32), 'Wv': lin(ks[5]), 'bv': jnp.zeros((D,), jnp.float32), 'Wo': lin(ks[6]), 'bo': jnp.zeros((D,), jnp.float32)}
    _L0_xattn_all = _L0_xattn_setup()
    _L0_xattn_in = {k: v for k, v in _L0_xattn_all.items() if k in ('Wq', 'bq', 'Wk', 'bk', 'Wv', 'bv', 'Wo', 'bo')}
    del _L0_xattn_all

    def _L0_ffn_setup():
        import jax, jax.numpy as jnp
        import numpy as np
        B, S, H = (1, 256, 128)
        E, K = (16, 4)
        G, TG = (4, 2)
        I_MOE = 64
        N_SH = 2
        SCALE = 2.5

        def _mlp(x, gw, uw, dw):
            return jax.nn.silu(x @ gw.T) * (x @ uw.T) @ dw.T

        def _route(x2d, router_weight, e_bias):
            T = x2d.shape[0]
            scores = jax.nn.sigmoid(x2d @ router_weight.T)
            sc = scores + e_bias[None, :]
            group_scores = jnp.sum(jax.lax.top_k(sc.reshape(T, G, E // G), 2)[0], axis=-1)
            _, gidx = jax.lax.top_k(group_scores, TG)
            gmask = jnp.zeros((T, G), sc.dtype).at[jnp.arange(T)[:, None], gidx].set(1.0)
            smask = jnp.repeat(gmask, E // G, axis=1)
            masked = jnp.where(smask > 0, sc, 0.0)
            _, tidx = jax.lax.top_k(masked, K)
            tw = jnp.take_along_axis(scores, tidx, axis=1)
            tw = tw / (jnp.sum(tw, axis=-1, keepdims=True) + 1e-20)
            tw = tw * SCALE
            return (tidx, tw)

        def _moe_forward(hidden_states, router_weight, e_bias, gate_w, up_w, down_w, sh_gate_w, sh_up_w, sh_down_w):
            orig_shape = hidden_states.shape
            x = hidden_states.reshape(-1, H)
            T = x.shape[0]
            tidx, tw = _route(x, router_weight, e_bias)
            g = jnp.einsum('th,eih->tei', x, gate_w)
            u = jnp.einsum('th,eih->tei', x, up_w)
            h = jax.nn.silu(g) * u
            yo = jnp.einsum('tei,ehi->teh', h, down_w)
            combine = jnp.zeros((T, E), tw.dtype).at[jnp.arange(T)[:, None], tidx].add(tw)
            routed = jnp.einsum('te,teh->th', combine, yo)
            shared = _mlp(hidden_states.reshape(-1, H), sh_gate_w, sh_up_w, sh_down_w)
            return (routed + shared).reshape(orig_shape)
        key = jax.random.key(seed)
        ks = jax.random.split(key, 9)
        s = 0.02
        return {'hidden_states': jax.random.normal(ks[0], (B, S, H), jnp.float32), 'router_weight': jax.random.normal(ks[1], (E, H), jnp.float32) * s, 'e_bias': jnp.zeros((E,), jnp.float32), 'gate_w': jax.random.normal(ks[2], (E, I_MOE, H), jnp.float32) * s, 'up_w': jax.random.normal(ks[3], (E, I_MOE, H), jnp.float32) * s, 'down_w': jax.random.normal(ks[4], (E, H, I_MOE), jnp.float32) * s, 'sh_gate_w': jax.random.normal(ks[5], (N_SH * I_MOE, H), jnp.float32) * s, 'sh_up_w': jax.random.normal(ks[6], (N_SH * I_MOE, H), jnp.float32) * s, 'sh_down_w': jax.random.normal(ks[7], (H, N_SH * I_MOE), jnp.float32) * s}
    _L0_ffn_all = _L0_ffn_setup()
    _L0_ffn_in = {k: v for k, v in _L0_ffn_all.items() if k in ('router_weight', 'e_bias', 'gate_w', 'up_w', 'down_w', 'sh_gate_w', 'sh_up_w', 'sh_down_w')}
    del _L0_ffn_all

    def _L1_attn_setup():
        import jax, jax.numpy as jnp
        import numpy as np
        D = 128
        H = 16
        N = D // H
        B = 4
        T = 256
        NLAYERS = 12
        LAYER_ID = 6
        EPS = 1e-05 * 64

        def _forward(x, w_r, w_k, w_v, w_g, w_o, time_maa_k, time_maa_v, time_maa_r, time_maa_g, time_decay, time_faaaa, ln_g, ln_b):
            Bs, Ts, C = x.shape
            if Ts % 32 == 0:
                Q = 32
            elif Ts % 128 == 0:
                Q = 128
            else:
                Q = Ts
            nC = Ts // Q
            xs = jnp.pad(x, ((0, 0), (1, 0), (0, 0)))[:, :-1]
            xx = xs - x
            xk = x + xx * time_maa_k
            xv = x + xx * time_maa_v
            xr = x + xx * time_maa_r
            xg = x + xx * time_maa_g
            r = (xr @ w_r.T).reshape(Bs, Ts, H, N).transpose(0, 2, 1, 3)
            k = (xk @ w_k.T).reshape(Bs, Ts, H, N).transpose(0, 2, 3, 1)
            v = (xv @ w_v.T).reshape(Bs, Ts, H, N).transpose(0, 2, 1, 3)
            g = jax.nn.silu(xg @ w_g.T)
            w = jnp.exp(-jnp.exp(time_decay))
            u = time_faaaa
            ws = (w ** Q)[None, :, None, None]
            q = jnp.arange(Q)
            wk = (w[:, None] ** (Q - 1 - q)[None, :])[None, :, None, :]
            wb = (w[:, None] ** q[None, :])[None, :, :, None]
            ii = q[:, None]
            jj = q[None, :]
            e = jnp.maximum(ii - jj - 1, 0)
            Wmat = jnp.where((jj < ii)[None], w[:, None, None] ** e[None], 0.0)
            Wmat = Wmat + jnp.eye(Q, dtype=x.dtype)[None] * u[:, None, None]
            Wmat = Wmat[None]
            rC = r.reshape(Bs, H, nC, Q, N).transpose(2, 0, 1, 3, 4)
            kC = k.reshape(Bs, H, N, nC, Q).transpose(3, 0, 1, 2, 4)
            vC = v.reshape(Bs, H, nC, Q, N).transpose(2, 0, 1, 3, 4)

            def step(state, inp):
                rr, kk, vv = inp
                y = rr @ kk * Wmat @ vv + rr @ state * wb
                state = ws * state + kk * wk @ vv
                return (state, y)
            state0 = jnp.zeros((Bs, H, N, N), x.dtype)
            _, yC = jax.lax.scan(step, state0, (rC, kC, vC))
            y = yC.transpose(1, 2, 0, 3, 4).reshape(Bs, H, Ts, N)
            y = y.transpose(0, 2, 1, 3).reshape(Bs * Ts, H, N)
            mu = y.mean(-1, keepdims=True)
            var = y.var(-1, keepdims=True)
            y = (y - mu) / jnp.sqrt(var + EPS)
            y = y.reshape(Bs, Ts, C) * ln_g + ln_b
            y = y * g
            return y @ w_o.T
        key = jax.random.key(seed)
        ks = jax.random.split(key, 6)
        r01 = LAYER_ID / (NLAYERS - 1)
        r10 = 1.0 - LAYER_ID / NLAYERS
        ddd = np.arange(D, dtype=np.float64) / D
        maa_k = (1.0 - ddd ** r10).astype(np.float32)
        maa_v = (1.0 - (ddd ** r10 + 0.3 * r01)).astype(np.float32)
        maa_r = (1.0 - ddd ** (0.5 * r10)).astype(np.float32)
        maa_g = maa_r.copy()
        hh = np.arange(H, dtype=np.float64)
        decay = (-6.0 + 5.0 * (hh / (H - 1)) ** (0.7 + 1.3 * r01)).astype(np.float32)
        faaaa = (r01 * (1.0 - hh / (H - 1))).astype(np.float32)
        s = 0.02
        return {'x': jax.random.normal(ks[0], (B, T, D), jnp.float32), 'w_r': jax.random.normal(ks[1], (D, D), jnp.float32) * s, 'w_k': jax.random.normal(ks[2], (D, D), jnp.float32) * s, 'w_v': jax.random.normal(ks[3], (D, D), jnp.float32) * s, 'w_g': jax.random.normal(ks[4], (D, D), jnp.float32) * s, 'w_o': jax.random.normal(ks[5], (D, D), jnp.float32) * s, 'time_maa_k': jnp.asarray(maa_k), 'time_maa_v': jnp.asarray(maa_v), 'time_maa_r': jnp.asarray(maa_r), 'time_maa_g': jnp.asarray(maa_g), 'time_decay': jnp.asarray(decay), 'time_faaaa': jnpp if False else jnp.asarray(faaaa), 'ln_g': jnp.ones((D,), jnp.float32), 'ln_b': jnp.zeros((D,), jnp.float32)}
    _L1_attn_all = _L1_attn_setup()
    _L1_attn_in = {k: v for k, v in _L1_attn_all.items() if k in ('w_r', 'w_k', 'w_v', 'w_g', 'w_o', 'time_maa_k', 'time_maa_v', 'time_maa_r', 'time_maa_g', 'time_decay', 'time_faaaa', 'ln_g', 'ln_b')}
    del _L1_attn_all

    def _L1_xattn_setup():
        import jax, jax.numpy as jnp
        import numpy as np
        D_MODEL = 128
        N_HEADS = 16
        D_K = D_MODEL // N_HEADS
        B, S = (4, 256)

        def _xavier(key, out_dim, in_dim):
            limit = float(np.sqrt(6.0 / (in_dim + out_dim)))
            return jax.random.uniform(key, (out_dim, in_dim), jnp.float32, -limit, limit)
        key = jax.random.key(seed)
        ks = jax.random.split(key, 7)
        return {'query': jax.random.normal(ks[0], (B, S, D_MODEL), jnp.float32), 'key': jax.random.normal(ks[1], (B, S, D_MODEL), jnp.float32), 'value': jax.random.normal(ks[2], (B, S, D_MODEL), jnp.float32), 'W_q': _xavier(ks[3], D_MODEL, D_MODEL), 'b_q': jnp.zeros((D_MODEL,), jnp.float32), 'W_k': _xavier(ks[4], D_MODEL, D_MODEL), 'b_k': jnp.zeros((D_MODEL,), jnp.float32), 'W_v': _xavier(ks[5], D_MODEL, D_MODEL), 'b_v': jnp.zeros((D_MODEL,), jnp.float32), 'W_o': _xavier(ks[6], D_MODEL, D_MODEL), 'b_o': jnp.zeros((D_MODEL,), jnp.float32)}
    _L1_xattn_all = _L1_xattn_setup()
    _L1_xattn_in = {k: v for k, v in _L1_xattn_all.items() if k in ('W_q', 'b_q', 'W_k', 'b_k', 'W_v', 'b_v', 'W_o', 'b_o')}
    del _L1_xattn_all

    def _L1_ffn_setup():
        import jax, jax.numpy as jnp
        import numpy as np
        EPS_LN = 1e-05
        EPS_GATE = 1e-08

        def layer_norm(x, gamma, beta):
            mu = jnp.mean(x, axis=-1, keepdims=True)
            var = jnp.mean(jnp.square(x - mu), axis=-1, keepdims=True)
            return (x - mu) * jax.lax.rsqrt(var + EPS_LN) * gamma + beta
        key = jax.random.key(seed)
        ks = jax.random.split(key, 8)
        B, S, D, E, H = (4, 512, 128, 4, 256)
        s_in = 1.0 / np.sqrt(D)
        s_h = 1.0 / np.sqrt(H)
        return {'h': jax.random.normal(ks[0], (B, S, D), dtype=jnp.float32), 'router_w': jax.random.uniform(ks[1], (E, D), jnp.float32, -s_in, s_in), 'rn_g': jnp.ones((D,), jnp.float32), 'rn_b': jnp.zeros((D,), jnp.float32), 'w1': jax.random.uniform(ks[2], (E, D, H), jnp.float32, -s_in, s_in), 'ln_g': jnp.ones((E, H), jnp.float32), 'ln_b': jnp.zeros((E, H), jnp.float32), 'w2': jax.random.uniform(ks[3], (E, H, D), jnp.float32, -s_h, s_h), 'on_g': jnp.ones((D,), jnp.float32), 'on_b': jnp.zeros((D,), jnp.float32)}
    _L1_ffn_all = _L1_ffn_setup()
    _L1_ffn_in = {k: v for k, v in _L1_ffn_all.items() if k in ('router_w', 'rn_g', 'rn_b', 'w1', 'ln_g', 'ln_b', 'w2', 'on_g', 'on_b')}
    del _L1_ffn_all
    return {'x': x, 'ctx_1024': ctx_1024, 'L0_attn_Wq': _L0_attn_in['Wq'], 'L0_attn_bq': _L0_attn_in['bq'], 'L0_attn_Wk': _L0_attn_in['Wk'], 'L0_attn_bk': _L0_attn_in['bk'], 'L0_attn_Wv': _L0_attn_in['Wv'], 'L0_attn_bv': _L0_attn_in['bv'], 'L0_attn_Wo': _L0_attn_in['Wo'], 'L0_attn_bo': _L0_attn_in['bo'], 'L0_attn_sample_idx': _L0_attn_in['sample_idx'], 'L0_xattn_Wq': _L0_xattn_in['Wq'], 'L0_xattn_bq': _L0_xattn_in['bq'], 'L0_xattn_Wk': _L0_xattn_in['Wk'], 'L0_xattn_bk': _L0_xattn_in['bk'], 'L0_xattn_Wv': _L0_xattn_in['Wv'], 'L0_xattn_bv': _L0_xattn_in['bv'], 'L0_xattn_Wo': _L0_xattn_in['Wo'], 'L0_xattn_bo': _L0_xattn_in['bo'], 'L0_ffn_router_weight': _L0_ffn_in['router_weight'], 'L0_ffn_e_bias': _L0_ffn_in['e_bias'], 'L0_ffn_gate_w': _L0_ffn_in['gate_w'], 'L0_ffn_up_w': _L0_ffn_in['up_w'], 'L0_ffn_down_w': _L0_ffn_in['down_w'], 'L0_ffn_sh_gate_w': _L0_ffn_in['sh_gate_w'], 'L0_ffn_sh_up_w': _L0_ffn_in['sh_up_w'], 'L0_ffn_sh_down_w': _L0_ffn_in['sh_down_w'], 'L1_attn_w_r': _L1_attn_in['w_r'], 'L1_attn_w_k': _L1_attn_in['w_k'], 'L1_attn_w_v': _L1_attn_in['w_v'], 'L1_attn_w_g': _L1_attn_in['w_g'], 'L1_attn_w_o': _L1_attn_in['w_o'], 'L1_attn_time_maa_k': _L1_attn_in['time_maa_k'], 'L1_attn_time_maa_v': _L1_attn_in['time_maa_v'], 'L1_attn_time_maa_r': _L1_attn_in['time_maa_r'], 'L1_attn_time_maa_g': _L1_attn_in['time_maa_g'], 'L1_attn_time_decay': _L1_attn_in['time_decay'], 'L1_attn_time_faaaa': _L1_attn_in['time_faaaa'], 'L1_attn_ln_g': _L1_attn_in['ln_g'], 'L1_attn_ln_b': _L1_attn_in['ln_b'], 'L1_xattn_W_q': _L1_xattn_in['W_q'], 'L1_xattn_b_q': _L1_xattn_in['b_q'], 'L1_xattn_W_k': _L1_xattn_in['W_k'], 'L1_xattn_b_k': _L1_xattn_in['b_k'], 'L1_xattn_W_v': _L1_xattn_in['W_v'], 'L1_xattn_b_v': _L1_xattn_in['b_v'], 'L1_xattn_W_o': _L1_xattn_in['W_o'], 'L1_xattn_b_o': _L1_xattn_in['b_o'], 'L1_ffn_router_w': _L1_ffn_in['router_w'], 'L1_ffn_rn_g': _L1_ffn_in['rn_g'], 'L1_ffn_rn_b': _L1_ffn_in['rn_b'], 'L1_ffn_w1': _L1_ffn_in['w1'], 'L1_ffn_ln_g': _L1_ffn_in['ln_g'], 'L1_ffn_ln_b': _L1_ffn_in['ln_b'], 'L1_ffn_w2': _L1_ffn_in['w2'], 'L1_ffn_on_g': _L1_ffn_in['on_g'], 'L1_ffn_on_b': _L1_ffn_in['on_b']}

def reference(x, ctx_1024, L0_attn_Wq, L0_attn_bq, L0_attn_Wk, L0_attn_bk, L0_attn_Wv, L0_attn_bv, L0_attn_Wo, L0_attn_bo, L0_attn_sample_idx, L0_xattn_Wq, L0_xattn_bq, L0_xattn_Wk, L0_xattn_bk, L0_xattn_Wv, L0_xattn_bv, L0_xattn_Wo, L0_xattn_bo, L0_ffn_router_weight, L0_ffn_e_bias, L0_ffn_gate_w, L0_ffn_up_w, L0_ffn_down_w, L0_ffn_sh_gate_w, L0_ffn_sh_up_w, L0_ffn_sh_down_w, L1_attn_w_r, L1_attn_w_k, L1_attn_w_v, L1_attn_w_g, L1_attn_w_o, L1_attn_time_maa_k, L1_attn_time_maa_v, L1_attn_time_maa_r, L1_attn_time_maa_g, L1_attn_time_decay, L1_attn_time_faaaa, L1_attn_ln_g, L1_attn_ln_b, L1_xattn_W_q, L1_xattn_b_q, L1_xattn_W_k, L1_xattn_b_k, L1_xattn_W_v, L1_xattn_b_v, L1_xattn_W_o, L1_xattn_b_o, L1_ffn_router_w, L1_ffn_rn_g, L1_ffn_rn_b, L1_ffn_w1, L1_ffn_ln_g, L1_ffn_ln_b, L1_ffn_w2, L1_ffn_on_g, L1_ffn_on_b):
    import jax
    import jax.numpy as jnp

    def _L0_attn_ref(x, Wq, bq, Wk, bk, Wv, bv, Wo, bo, sample_idx):
        import math
        import jax, jax.numpy as jnp
        import numpy as np
        B, S, D, H = (4, 256, 128, 16)
        HD = D // H
        SAMPLING_FACTOR = 5.0
        batch, seq_len, d_model = x.shape
        scale = math.sqrt(HD)
        u = max(1, min(seq_len, int(SAMPLING_FACTOR * math.log(seq_len + 1))))

        def proj(W, b):
            return (x @ W + b).reshape(batch, seq_len, H, HD).transpose(0, 2, 1, 3)
        Q = proj(Wq, bq)
        K = proj(Wk, bk)
        V = proj(Wv, bv)
        K_sample = K[:, :, sample_idx, :]
        scores_sample = jnp.einsum('bhsd,bhud->bhsu', Q, K_sample) / scale
        M = scores_sample.max(axis=-1) - scores_sample.mean(axis=-1)
        _, top_idx = jax.lax.top_k(M, u)
        Q_reduce = jnp.take_along_axis(Q, top_idx[..., None], axis=2)
        attn_scores = jnp.einsum('bhud,bhsd->bhus', Q_reduce, K) / scale
        attn_probs = jax.nn.softmax(attn_scores, axis=-1)
        context = jnp.einsum('bhus,bhsd->bhud', attn_probs, V)
        V_mean = V.mean(axis=2, keepdims=True)
        out = jnp.broadcast_to(V_mean, (batch, H, seq_len, HD))
        b_idx = jnp.arange(batch)[:, None, None]
        h_idx = jnp.arange(H)[None, :, None]
        out = out.at[b_idx, h_idx, top_idx].set(context)
        out = out.transpose(0, 2, 1, 3).reshape(batch, seq_len, d_model)
        return out @ Wo + bo

    def _L0_xattn_ref(q, k, v, Wq, bq, Wk, bk, Wv, bv, Wo, bo):
        import jax, jax.numpy as jnp
        import numpy as np
        D_MODEL = 128
        NUM_HEADS = 16
        D_K = D_MODEL // NUM_HEADS
        SCALE = float(np.sqrt(D_K))

        def _split_heads(x):
            B, S, _ = x.shape
            return x.reshape(B, S, NUM_HEADS, D_K).transpose(0, 2, 1, 3)
        Q = _split_heads(q @ Wq.T + bq)
        K = _split_heads(k @ Wk.T + bk)
        V = _split_heads(v @ Wv.T + bv)
        scores = jnp.einsum('bhqd,bhkd->bhqk', Q, K) / SCALE
        m = jax.lax.stop_gradient(jnp.max(scores, axis=-1, keepdims=True))
        exp_scores = jnp.exp(scores - m)
        attn = exp_scores / (jnp.sum(exp_scores, axis=-1, keepdims=True) + 1e-09)
        out = jnp.einsum('bhqk,bhkd->bhqd', attn, V)
        B, H, S, dk = out.shape
        out = out.transpose(0, 2, 1, 3).reshape(B, S, H * dk)
        return out @ Wo.T + bo

    def _L0_ffn_ref(hidden_states, router_weight, e_bias, gate_w, up_w, down_w, sh_gate_w, sh_up_w, sh_down_w):
        import jax, jax.numpy as jnp
        import numpy as np
        B, S, H = (1, 256, 128)
        E, K = (16, 4)
        G, TG = (4, 2)
        I_MOE = 64
        N_SH = 2
        SCALE = 2.5

        def _mlp(x, gw, uw, dw):
            return jax.nn.silu(x @ gw.T) * (x @ uw.T) @ dw.T

        def _route(x2d, router_weight, e_bias):
            T = x2d.shape[0]
            scores = jax.nn.sigmoid(x2d @ router_weight.T)
            sc = scores + e_bias[None, :]
            group_scores = jnp.sum(jax.lax.top_k(sc.reshape(T, G, E // G), 2)[0], axis=-1)
            _, gidx = jax.lax.top_k(group_scores, TG)
            gmask = jnp.zeros((T, G), sc.dtype).at[jnp.arange(T)[:, None], gidx].set(1.0)
            smask = jnp.repeat(gmask, E // G, axis=1)
            masked = jnp.where(smask > 0, sc, 0.0)
            _, tidx = jax.lax.top_k(masked, K)
            tw = jnp.take_along_axis(scores, tidx, axis=1)
            tw = tw / (jnp.sum(tw, axis=-1, keepdims=True) + 1e-20)
            tw = tw * SCALE
            return (tidx, tw)

        def _moe_forward(hidden_states, router_weight, e_bias, gate_w, up_w, down_w, sh_gate_w, sh_up_w, sh_down_w):
            orig_shape = hidden_states.shape
            x = hidden_states.reshape(-1, H)
            T = x.shape[0]
            tidx, tw = _route(x, router_weight, e_bias)
            g = jnp.einsum('th,eih->tei', x, gate_w)
            u = jnp.einsum('th,eih->tei', x, up_w)
            h = jax.nn.silu(g) * u
            yo = jnp.einsum('tei,ehi->teh', h, down_w)
            combine = jnp.zeros((T, E), tw.dtype).at[jnp.arange(T)[:, None], tidx].add(tw)
            routed = jnp.einsum('te,teh->th', combine, yo)
            shared = _mlp(hidden_states.reshape(-1, H), sh_gate_w, sh_up_w, sh_down_w)
            return (routed + shared).reshape(orig_shape)
        return _moe_forward(hidden_states, router_weight, e_bias, gate_w, up_w, down_w, sh_gate_w, sh_up_w, sh_down_w)

    def _L1_attn_ref(x, w_r, w_k, w_v, w_g, w_o, time_maa_k, time_maa_v, time_maa_r, time_maa_g, time_decay, time_faaaa, ln_g, ln_b):
        import jax, jax.numpy as jnp
        import numpy as np
        D = 128
        H = 16
        N = D // H
        B = 4
        T = 256
        NLAYERS = 12
        LAYER_ID = 6
        EPS = 1e-05 * 64

        def _forward(x, w_r, w_k, w_v, w_g, w_o, time_maa_k, time_maa_v, time_maa_r, time_maa_g, time_decay, time_faaaa, ln_g, ln_b):
            Bs, Ts, C = x.shape
            if Ts % 32 == 0:
                Q = 32
            elif Ts % 128 == 0:
                Q = 128
            else:
                Q = Ts
            nC = Ts // Q
            xs = jnp.pad(x, ((0, 0), (1, 0), (0, 0)))[:, :-1]
            xx = xs - x
            xk = x + xx * time_maa_k
            xv = x + xx * time_maa_v
            xr = x + xx * time_maa_r
            xg = x + xx * time_maa_g
            r = (xr @ w_r.T).reshape(Bs, Ts, H, N).transpose(0, 2, 1, 3)
            k = (xk @ w_k.T).reshape(Bs, Ts, H, N).transpose(0, 2, 3, 1)
            v = (xv @ w_v.T).reshape(Bs, Ts, H, N).transpose(0, 2, 1, 3)
            g = jax.nn.silu(xg @ w_g.T)
            w = jnp.exp(-jnp.exp(time_decay))
            u = time_faaaa
            ws = (w ** Q)[None, :, None, None]
            q = jnp.arange(Q)
            wk = (w[:, None] ** (Q - 1 - q)[None, :])[None, :, None, :]
            wb = (w[:, None] ** q[None, :])[None, :, :, None]
            ii = q[:, None]
            jj = q[None, :]
            e = jnp.maximum(ii - jj - 1, 0)
            Wmat = jnp.where((jj < ii)[None], w[:, None, None] ** e[None], 0.0)
            Wmat = Wmat + jnp.eye(Q, dtype=x.dtype)[None] * u[:, None, None]
            Wmat = Wmat[None]
            rC = r.reshape(Bs, H, nC, Q, N).transpose(2, 0, 1, 3, 4)
            kC = k.reshape(Bs, H, N, nC, Q).transpose(3, 0, 1, 2, 4)
            vC = v.reshape(Bs, H, nC, Q, N).transpose(2, 0, 1, 3, 4)

            def step(state, inp):
                rr, kk, vv = inp
                y = rr @ kk * Wmat @ vv + rr @ state * wb
                state = ws * state + kk * wk @ vv
                return (state, y)
            state0 = jnp.zeros((Bs, H, N, N), x.dtype)
            _, yC = jax.lax.scan(step, state0, (rC, kC, vC))
            y = yC.transpose(1, 2, 0, 3, 4).reshape(Bs, H, Ts, N)
            y = y.transpose(0, 2, 1, 3).reshape(Bs * Ts, H, N)
            mu = y.mean(-1, keepdims=True)
            var = y.var(-1, keepdims=True)
            y = (y - mu) / jnp.sqrt(var + EPS)
            y = y.reshape(Bs, Ts, C) * ln_g + ln_b
            y = y * g
            return y @ w_o.T
        return _forward(x, w_r, w_k, w_v, w_g, w_o, time_maa_k, time_maa_v, time_maa_r, time_maa_g, time_decay, time_faaaa, ln_g, ln_b)

    def _L1_xattn_ref(query, key, value, W_q, b_q, W_k, b_k, W_v, b_v, W_o, b_o):
        import jax, jax.numpy as jnp
        import numpy as np
        D_MODEL = 128
        N_HEADS = 16
        D_K = D_MODEL // N_HEADS
        B, S = (4, 256)

        def _xavier(key, out_dim, in_dim):
            limit = float(np.sqrt(6.0 / (in_dim + out_dim)))
            return jax.random.uniform(key, (out_dim, in_dim), jnp.float32, -limit, limit)
        b, sq, _ = query.shape
        sk = key.shape[1]
        Q = (query @ W_q.T + b_q).reshape(b, sq, N_HEADS, D_K).transpose(0, 2, 1, 3)
        K = (key @ W_k.T + b_k).reshape(b, sk, N_HEADS, D_K).transpose(0, 2, 1, 3)
        V = (value @ W_v.T + b_v).reshape(b, sk, N_HEADS, D_K).transpose(0, 2, 1, 3)
        scores = jnp.einsum('bhqd,bhkd->bhqk', Q, K) / jnp.sqrt(jnp.float32(D_K))
        attn = jax.nn.softmax(scores, axis=-1)
        out = jnp.einsum('bhqk,bhkd->bhqd', attn, V)
        out = out.transpose(0, 2, 1, 3).reshape(b, sq, D_MODEL)
        return out @ W_o.T + b_o

    def _L1_ffn_ref(h, router_w, rn_g, rn_b, w1, ln_g, ln_b, w2, on_g, on_b):
        import jax, jax.numpy as jnp
        import numpy as np
        EPS_LN = 1e-05
        EPS_GATE = 1e-08

        def layer_norm(x, gamma, beta):
            mu = jnp.mean(x, axis=-1, keepdims=True)
            var = jnp.mean(jnp.square(x - mu), axis=-1, keepdims=True)
            return (x - mu) * jax.lax.rsqrt(var + EPS_LN) * gamma + beta
        D = h.shape[-1]
        h_norm = layer_norm(h, rn_g, rn_b)
        g = jax.nn.softmax(jnp.einsum('bsd,ed->bse', h_norm, router_w), axis=-1)
        top2_w, top2_idx = jax.lax.top_k(g, 2)
        top2_w = top2_w / (jnp.sum(top2_w, axis=-1, keepdims=True) + EPS_GATE)
        hid = jnp.einsum('bsd,edh->bseh', h, w1)
        hid = jax.nn.relu(layer_norm(hid, ln_g, ln_b))
        expert_out = jnp.einsum('bseh,ehd->bsed', hid, w2)
        idx = jnp.broadcast_to(top2_idx[..., None], top2_idx.shape + (D,))
        top2_out = jnp.take_along_axis(expert_out, idx, axis=-2)
        out = jnp.sum(top2_out * top2_w[..., None], axis=-2)
        return layer_norm(out, on_g, on_b)
    x = x + _L0_attn_ref(_layernorm(x, axis=-1), L0_attn_Wq, L0_attn_bq, L0_attn_Wk, L0_attn_bk, L0_attn_Wv, L0_attn_bv, L0_attn_Wo, L0_attn_bo, L0_attn_sample_idx)
    x = x + _L0_xattn_ref(_layernorm(x, axis=-1), ctx_1024, ctx_1024, L0_xattn_Wq, L0_xattn_bq, L0_xattn_Wk, L0_xattn_bk, L0_xattn_Wv, L0_xattn_bv, L0_xattn_Wo, L0_xattn_bo)
    x = x + _L0_ffn_ref(_layernorm(x, axis=-1), L0_ffn_router_weight, L0_ffn_e_bias, L0_ffn_gate_w, L0_ffn_up_w, L0_ffn_down_w, L0_ffn_sh_gate_w, L0_ffn_sh_up_w, L0_ffn_sh_down_w)
    x = x + _L1_attn_ref(_layernorm(x, axis=-1), L1_attn_w_r, L1_attn_w_k, L1_attn_w_v, L1_attn_w_g, L1_attn_w_o, L1_attn_time_maa_k, L1_attn_time_maa_v, L1_attn_time_maa_r, L1_attn_time_maa_g, L1_attn_time_decay, L1_attn_time_faaaa, L1_attn_ln_g, L1_attn_ln_b)
    x = x + _L1_xattn_ref(_layernorm(x, axis=-1), ctx_1024, ctx_1024, L1_xattn_W_q, L1_xattn_b_q, L1_xattn_W_k, L1_xattn_b_k, L1_xattn_W_v, L1_xattn_b_v, L1_xattn_W_o, L1_xattn_b_o)
    x = x + _L1_ffn_ref(_layernorm(x, axis=-1), L1_ffn_router_w, L1_ffn_rn_g, L1_ffn_rn_b, L1_ffn_w1, L1_ffn_ln_g, L1_ffn_ln_b, L1_ffn_w2, L1_ffn_on_g, L1_ffn_on_b)
    return x

_drawn_inputs = setup_inputs


def setup_inputs(seed=0):
    import zlib

    import numpy as np

    out = dict(_drawn_inputs(seed))
    spreads = {'L0_attn_bq': (0.0, 0.1),
     'L0_attn_bk': (0.0, 2.0),
     'L0_attn_bv': (0.0, 0.1),
     'L0_attn_bo': (0.0, 0.1),
     'L0_xattn_bq': (0.0, 0.1),
     'L0_xattn_bk': (0.0, 2.0),
     'L0_xattn_bv': (0.0, 0.1),
     'L0_xattn_bo': (0.0, 0.1),
     'L0_ffn_e_bias': (0.0, 0.284),
     'L1_attn_ln_g': (1.0, 0.546),
     'L1_attn_ln_b': (0.0, 1.431),
     'L1_xattn_b_q': (0.0, 0.1),
     'L1_xattn_b_k': (0.0, 2.0),
     'L1_xattn_b_v': (0.0, 0.1),
     'L1_xattn_b_o': (0.0, 0.1),
     'L1_ffn_rn_g': (1.0, 0.2),
     'L1_ffn_rn_b': (0.0, 0.1),
     'L1_ffn_ln_g': (1.0, 0.2),
     'L1_ffn_ln_b': (0.0, 0.1),
     'L1_ffn_on_g': (1.0, 0.2),
     'L1_ffn_on_b': (0.0, 0.1)}
    factors = {'L0_ffn_router_weight': 4.013,
     'L0_ffn_down_w': 2.867,
     'L1_attn_time_faaaa': 56.02,
     'L0_ffn_sh_gate_w': 2.787,
     'L1_attn_time_maa_k': 3.468}
    for name, (base, spread) in spreads.items():
        noise = np.random.default_rng([zlib.crc32(name.encode()), seed]).standard_normal(out[name].shape)
        drawn = base * np.exp(spread * noise) if base else spread * noise
        out[name] = jnp.asarray(drawn.astype(out[name].dtype))
    for name, factor in factors.items():
        out[name] = (out[name] * factor).astype(out[name].dtype)
    return out
```

```python
from contextlib import ExitStack

import concourse.bass as bass
from concourse import mybir

ALU = mybir.AluOpType
ACT = mybir.ActivationFunctionType
AXX = mybir.AxisListType.X
F32 = mybir.dt.float32
BF16 = mybir.dt.bfloat16
I32 = mybir.dt.int32
U32 = mybir.dt.uint32

P = 128
D = 128
B, S = 2, 512
T = B * S
NT = T // P
CB = S // P
H, HD = 16, 8
NS = 256
TOPK = 31
SLOTS = 32
G = H // 4
NC = 77
HK = H * NC
NB = -(-HK // P)
LB = HK - (NB - 1) * P
VW = D + H
E, EG = 16, 4
NM = 9
FE, FH = 4, 256
HV = 11
ASCALE = HD ** -0.5
NEG = -3.0e38

COLS = ["a_bq", "a_bk", "x0_bq", "x0_bk", "x1_bq", "x1_bk", "maa_k", "maa_v", "maa_r", "maa_g",
        "td", "rn_g", "rn_b"]
COL = {n: i for i, n in enumerate(COLS)}
NCOL = len(COLS) + 16
ROWS = ["a_bv", "a_bo", "x0_bv", "x0_bo", "x1_bv", "x1_bo", "ln_g", "ln_b", "on_g", "on_b"]
ROW = {n: i for i, n in enumerate(ROWS)}
WA = ["a_q", "a_k", "a_v", "a_o"]
WB = ["x0_q", "x0_k", "x0_v", "x0_o", "x1_q", "x1_k", "x1_v", "x1_o"]
WR = ["w_r", "w_k", "w_v", "w_g", "w_o"]


def build(nc, x, sidx, consts, small, selx, bdx, cols, rows, wa, wb, ctxt, wm, rw, wr, tdrow, urow, w1, w2, rwf, ebias, out):
    with ExitStack() as ctx:
        def sb(name, shape, dt=F32):
            return ctx.enter_context(nc.sbuf_tensor(name, shape, dt))

        made = {}

        def s(name):
            if name not in made:
                made[name] = ctx.enter_context(nc.semaphore(name))
            return made[name]

        ps = ctx.enter_context(nc.psum_tensor("ps", [P, 8, 512], F32))

        cst = sb("cst", [P, 6 * P + 512])
        ident, ones, inv_s = cst[:, 0:P], cst[:, P:2 * P], cst[:, 2 * P:3 * P]
        gapT, causal, bdiag = cst[:, 3 * P:4 * P], cst[:, 4 * P:5 * P], cst[:, 5 * P:6 * P]
        iota_row = cst[:, 6 * P:6 * P + 512]
        sm = sb("sm", [P, 16 + 4 + 32 + 256 + 16 + P + 2])
        hmask = sm[:, 0:16]
        iota_pc = sm[:, 16:20]
        slotmask = sm[:, 20:52]
        before16 = sm[:, 52:308].rearrange("p (a b) -> p a b", a=E)
        before4 = sm[:, 308:324].rearrange("p (a b) -> p a b", a=4)
        trow = sm[:, 324:324 + P]
        ncol = sm[:, 324 + P:325 + P]
        colsb = sb("colsb", [P, NCOL])
        rowsb = sb("rowsb", [P, len(ROWS) * P])
        wa_sb = sb("wa_sb", [P, len(WA) * P])
        wb_sb = sb("wb_sb", [P, len(WB) * P])
        wm_sb = sb("wm_sb", [P, 3 * NM * P])
        wr_sb = sb("wr_sb", [P, len(WR) * P])
        w1_sb = sb("w1_sb", [P, FE * FH])
        w2_sb = sb("w2_sb", [P, 8 * P])
        rw_sb = sb("rw_sb", [P, E + FE])
        eb_sb = sb("eb_sb", [P, E])
        sel_sb = sb("sel_sb", [P, 8 * P], BF16)
        bdx_sb = sb("bdx_sb", [P, NB, VW])
        ctxT = sb("ctxT", [P, B, NC])
        tdr = sb("tdr", [P, P])
        ur = sb("ur", [P, H])
        half = sb("half", [P, 64])

        def col(n):
            return colsb[:, COL[n]:COL[n] + 1]

        def row(n):
            return rowsb[:, ROW[n] * P:(ROW[n] + 1) * P]

        def w(n):
            for names, t in ((WA, wa_sb), (WB, wb_sb), (WR, wr_sb)):
                if n in names:
                    i = names.index(n)
                    return t[:, i * P:(i + 1) * P]

        x_tm = sb("x_tm", [P, NT, D])
        xb = sb("xb", [P, NT, D])
        xn_tm = sb("xn_tm", [P, NT, D])
        xnT = sb("xnT", [P, B, S + 1])
        QT = sb("QT", [P, B, S])
        KT = sb("KT", [P, B, S])
        V_tm = sb("V_tm", [P, NT, D])
        attnT = sb("attnT", [P, B, S])
        big = sb("big", [P, 8192])
        aux = sb("aux", [P, 4096])
        st = sb("st", [P, NT, 6])
        mv = sb("mv", [P, NT, 2])
        veps = sb("veps", [P, NT])
        rstd = sb("rstd", [P, NT])
        Kx = sb("Kx", [P, 2, B, NC])
        kbdx_all = sb("kbdx_all", [P, 2 * HK + 2 * NB * P])
        Kbdx = kbdx_all[:, 0:4 * HK].rearrange("p (b h n) -> p b h n", b=2 * B, h=H)
        ctxrep = kbdx_all[:, 2 * HK:2 * HK + 2 * NB * P]
        Vbdx = sb("Vbdx", [P, 2 * B, NB, VW])
        Wtab = sb("Wtab", [P, H, P])
        rpow = sb("rpow", [P, P])
        kpow = sb("kpow", [P, P])
        lamr = sb("lamr", [P, P])
        lamc = sb("lamc", [P, 4])

        def xchunk(c, src):
            return src[:, c // CB, (c % CB) * P:(c % CB + 1) * P]

        def xnchunk(c):
            return xnT[:, c // CB, 1 + (c % CB) * P:1 + (c % CB + 1) * P]

        block = ctx.enter_context(nc.Block())
        x_v = x.rearrange("b (c p) d -> p (b c) d", p=P)
        out_v = out.rearrange("b (c p) d -> p (b c) d", p=P)

        Kbd = big[:, :].rearrange("p (b h s) -> p b h s", b=B, h=H)
        OH = big[:, 0:4096].rearrange("p (c n) -> p c n", c=NT)
        OHT = big[:, 4096:8192].rearrange("p (c n) -> p c n", c=NT)
        ohs = aux[:, 0:1024].rearrange("p (c n) -> p c n", c=CB)
        xsamp = aux[:, 1024:1536].rearrange("p (b n) -> p b n", b=B)
        KsT = aux[:, 1536:2048].rearrange("p (b n) -> p b n", b=B)
        xsel = aux[:, 0:1024].rearrange("p (b n) -> p b n", b=B)
        Qbd = aux[:, 1024:2048].rearrange("p (b h n) -> p b h n", b=B, h=H)
        Pa = aux[:, 2048:3072].rearrange("p (i n) -> p i n", i=2)
        PTa = aux[:, 3072:4096].rearrange("p (i n) -> p i n", i=2)
        sidx_i = sb("sidx_i", [P, NS], I32)
        sidx_f = sb("sidx_f", [P, NS])
        kbar = sb("kbar", [P, B])
        kbarbd = sb("kbarbd", [P, B, H])
        Mx = sb("Mx", [P, CB, B, H])
        MT = sb("MT", [32, 2, S])
        v8 = sb("v8", [32, SLOTS])
        idx = sb("idx", [32, SLOTS], U32)
        idxf = sb("idxf", [32, SLOTS])
        idxT = sb("idxT", [32, 32])
        idxcol = sb("idxcol", [P, 8])
        diag = aux[0:32, 2048:3072].rearrange("p (a n) -> p a n", a=32)
        Vmb = sb("Vmb", [P, B, D])
        Vmc = sb("Vmc", [P, B])
        nmx = sb("nmx", [P, 8])
        nb = sb("nb", [P, 8])
        rsum = sb("rsum", [P, 8])
        rinv = sb("rinv", [P, 8])
        dgt = sb("dgt", [P, 8, 32])
        dg = sb("dg", [P, 8, 32])
        Ssb = aux[:, 0:2 * HK].rearrange("p (i n) -> p i n", i=2)
        PTx = big[:, 0:2 * NB * P].rearrange("p (i n) -> p i n", i=2)
        mxx = sb("mxx", [P, 2, H])
        rsx = sb("rsx", [P, 2, H])
        atm = sb("atm", [P, 4, D])
        sg = sb("sg", [P, NT, E])
        sc = sb("sc", [P, NT, E])
        rt = sb("rt", [P, NT, 64])
        cmp1 = big[:, 0:2048].rearrange("p (c a b) -> p c a b", c=NT, a=E)
        cmp2 = big[:, 2048:4096].rearrange("p (c a b) -> p c a b", c=NT, a=E)
        rank = sb("rank", [P, NT, E])
        den = sb("den", [P, NT])
        comb = sb("comb", [P, NT, E])
        combr = sb("combr", [P, T], BF16)
        cr = aux[0:E, 0:S]
        crb = sb("crb", [E, S], BF16)
        hs = big[:, 4096:8192].rearrange("p (i n) -> p i n", i=8)
        xx = big[:, 0:1024].rearrange("p (b n) -> p b n", b=B)
        mixes = big[:, 1024:5120].rearrange("p (m b n) -> p m b n", m=4, b=B)
        Rbd = big[:, 0:4096].rearrange("p (i h t) -> p i h t", i=2, h=H)
        Pr = big[:, 4096:8192].rearrange("p (i h t) -> p i h t", i=2, h=H)
        Rw = aux[:, 0:1024].rearrange("p (b n) -> p b n", b=B)
        Ktm = aux[:, 1024:2048].rearrange("p (c n) -> p c n", c=NT)
        Gtm = aux[:, 2048:3072].rearrange("p (c n) -> p c n", c=NT)
        yc = aux[:, 3072:4096].rearrange("p (b n) -> p b n", b=B)
        St = sb("St", [P, 2, D])
        Um = sb("Um", [P, D])
        w128 = lamc[:, 2:3]
        gm = sb("gm", [P, 2, 64])
        gv = sb("gv", [P, 2, 64])
        sq = xb[:, :, :].rearrange("p (b c) d -> p b (c d)", b=B)
        hn = big[:, 0:4096].rearrange("p (c n) -> p c n", c=CB)
        hidT = big[:, 4096:8192].rearrange("p (k n) -> p k n", k=8)
        hnT = aux[:, 0:1024].rearrange("p (b n) -> p b n", b=B)
        otm = aux[:, 1024:2048].rearrange("p (c n) -> p c n", c=NT)
        fsm = sb("fsm", [P, NT, FE])
        fw = sb("fw", [P, NT, FE])
        f1 = sb("f1", [P, NT])
        fst = sb("fst", [P, FE, 6])
        fmv = sb("fmv", [P, NT, FE, 2])
        fve = sb("fve", [P, NT, FE])
        frs = sb("frs", [P, NT, FE])
        fnm = sb("fnm", [P, NT, FE])

        @block.sync
        def _(sp):
            for b in range(B):
                sp.dma_start(x_tm[:, b * CB:(b + 1) * CB, :], x_v[:, b * CB:(b + 1) * CB, :]).then_inc(s(f"x_in{b}"), 16)
                if b == 0:
                    sp.dma_start(cst[:, :], consts).then_inc(s("in_first"), 16)
                    sp.dma_start(sidx_i[:, :], sidx).then_inc(s("in_first"), 16)
                    sp.dma_start(sm[:, :], small).then_inc(s("in_first"), 16)
            sp.dma_start(wa_sb[:, :], wa).then_inc(s("in_attn"), 16)
            sp.dma_start(colsb[:, :], cols).then_inc(s("in_attn"), 16)
            sp.dma_start(rowsb[:, :], rows).then_inc(s("in_attn"), 16)
            sp.dma_start(ctxT[:, :, :], ctxt).then_inc(s("in_ctx"), 16)
            sp.dma_start(wb_sb[:, :], wb).then_inc(s("in_ctx"), 16)
            sp.dma_start(bdx_sb[:, :, :], bdx).then_inc(s("in_ctx"), 16)
            sp.dma_start(tdr[:, :], tdrow).then_inc(s("in_ctx"), 16)
            sp.dma_start(ur[:, :], urow).then_inc(s("in_ctx"), 16)
            sp.dma_start(rw_sb[:, 0:E], rw).then_inc(s("in_moe"), 16)
            sp.dma_start(eb_sb[:, :], ebias).then_inc(s("in_moe"), 16)
            sp.dma_start(sel_sb[:, :], selx).then_inc(s("in_moe"), 16)
            sp.dma_start(wm_sb[:, :], wm).then_inc(s("in_moe"), 16)
            sp.dma_start(wr_sb[:, :], wr).then_inc(s("in_last"), 16)
            sp.dma_start(w1_sb[:, :], w1).then_inc(s("in_last"), 16)
            sp.dma_start(w2_sb[:, :], w2).then_inc(s("in_last"), 16)
            sp.dma_start(rw_sb[:, E:E + FE], rwf).then_inc(s("in_last"), 16)
            for b in range(B):
                sp.wait_ge(s("final"), b + 1)
                sp.dma_start(out_v[:, b * CB:(b + 1) * CB, :], xb[:, b * CB:(b + 1) * CB, :]).then_inc(s("stored"), 16)
            sp.wait_ge(s("stored"), 16 * B)

        XSEM = ["x_in", "a_x", "x_x", "m_x", "r_x", "x_x"]

        def wait_x(eng, k, c):
            if k == 0:
                eng.wait_ge(s(f"x_in{c // CB}"), 16)
            else:
                eng.wait_ge(s(XSEM[k]), (NT if k == 5 else 0) + c + 1)

        @block.tensor
        def _(pe):
            mm, tr = nc.tensor.matmul, nc.tensor.transpose

            def ln_transpose(k, sem="xn", out_sem="xnT_ps", bank=6):
                for b in range(B):
                    for j in range(CB):
                        pe.wait_ge(s(sem), NT * k + CB * b + j + 1)
                        i = tr(ps[:, bank + b, j * P:(j + 1) * P], xn_tm[:, CB * b + j, :], ident)
                    i.then_inc(s(out_sem), 1)

            pe.wait_ge(s("in_first"), 16 * 3)
            ln_transpose(0)
            pe.wait_ge(s("ohs"), 1)
            pe.wait_ge(s("in_attn"), 16 * 3)
            for b in range(B):
                for c in range(CB):
                    i = mm(ps[:, b, 0:NS], xn_tm[:, CB * b + c, :], ohs[:, c, :], start=(c == 0), stop=(c == CB - 1))
                i.then_inc(s("xsamp_ps"), 1)
            for b in range(B):
                pe.wait_ge(s("xsamp"), b + 1)
                mm(ps[:, 2 + b, 0:NS], w("a_k"), xsamp[:, b, :], start=True, stop=True).then_inc(s("ks_ps"), 1)
            for b in range(B):
                pe.wait_ge(s("xnT"), b + 1)
                mm(ps[:, 4 + b, :], w("a_q"), xnT[:, b, 1:S + 1], start=True, stop=True).then_inc(s("a_q_ps"), 1)
            for b in range(B):
                mm(ps[:, b, :], w("a_k"), xnT[:, b, 1:S + 1], start=True, stop=True).then_inc(s("a_k_ps"), 1)
            for b in range(B):
                pe.wait_ge(s("ks"), b + 1)
                for j in range(CB):
                    i = mm(ps[:, 2 + b, j * P:(j + 1) * P], xnchunk(CB * b + j), w("a_v"), start=True, stop=True)
                i.then_inc(s("a_v_ps"), 1)

            def pre_groups():
                g = 0
                for l in range(2):
                    pe.wait_ge(s("pre"), g) if g else pe.wait_ge(s("xnT"), 2)
                    mm(ps[:, 6, 0:B * NC], w(f"x{l}_k"), ctxT[:, :, :].rearrange("p b n -> p (b n)"),
                       start=True, stop=True).then_inc(s("pre_ps"), 1)
                    g += 1
                    yield
                for l in range(2):
                    for b in range(B):
                        for q in range(3):
                            pe.wait_ge(s("pre"), g)
                            for n in range(4 * q, min(4 * q + 4, NB)):
                                i = mm(ps[:, 6, (n - 4 * q) * P:(n - 4 * q + 1) * P],
                                       ctxrep[:, b * NB * P + n * P:b * NB * P + (n + 1) * P],
                                       w(f"x{l}_v"), start=True, stop=True)
                            i.then_inc(s("pre_ps"), 1)
                            g += 1
                            yield

            pre = pre_groups()
            pe.wait_ge(s("a_q"), 2)
            pe.wait_ge(s("a_k"), 2)
            pe.wait_ge(s("a_v"), 2)
            for n in range(4 * NT):
                c, hq = n // 4, n % 4
                b, pair = c // CB, 2 * (n % 3)
                if n % (4 * CB) == 0:
                    pe.wait_ge(s("kbd_v"), b + 1)
                    pe.wait_ge(s("kbd_a"), b + 1)
                    pe.wait_ge(s("kbar"), b + 1)
                    for cc in range(CB * b, CB * b + CB):
                        mm(ps[:, 7, cc * H:(cc + 1) * H], xchunk(cc, QT), kbarbd[:, b, :], start=True,
                           stop=True).then_inc(s("mean_ps"), 1)
                if n >= 3:
                    pe.wait_ge(s("mx"), n - 2)
                for v in range(2):
                    i = mm(ps[:, pair + v, :], xchunk(c, QT), Kbd[:, b, 4 * hq + 2 * v:4 * hq + 2 * v + 2, :],
                           start=True, stop=True)
                i.then_inc(s("as_ps"), 1)
                if n == 2:
                    pe.wait_ge(s("in_ctx"), 16 * 5)
                    pe.wait_ge(s("in_ctx"), 16 * 5)
                    pe.wait_ge(s("ctxrep"), 1)
                if n >= 2 and n % 2 == 0:
                    next(pre, None)
            pe.wait_ge(s("m"), 1)
            pe.wait_ge(s("pre"), 14)
            for c in range(CB):
                i = tr(ps[0:32, 6, c * P:(c + 1) * P], Mx[:, c, :, :].rearrange("p b h -> p (b h)"), ident)
            i.then_inc(s("mT_ps"), 1)
            for b in range(B):
                for c in range(CB):
                    mm(ps[:, 2, b * P:(b + 1) * P], inv_s, V_tm[:, CB * b + c, :], start=(c == 0), stop=(c == CB - 1))
                for c in range(CB):
                    i = mm(ps[:, 2, 256 + b:257 + b], V_tm[:, CB * b + c, :], inv_s[:, 0:1], start=(c == 0),
                           stop=(c == CB - 1))
                i.then_inc(s("vm_ps"), 1)
            pe.wait_ge(s("diag"), 1)
            for b in range(B):
                mm(ps[:, b, :], ones[0:32, :], diag[:, H * b:H * (b + 1), :], start=True, stop=True).then_inc(s("ib_ps"), 1)
            pe.wait_ge(s("vm"), B)
            for b in range(B):
                pe.wait_ge(s("oh"), b + 1)
                for c in range(CB):
                    i = mm(ps[:, 2 + b, :], xn_tm[:, CB * b + c, :], OH[:, CB * b + c, :], start=(c == 0), stop=(c == CB - 1))
                i.then_inc(s("xsel_ps"), 1)
            for b in range(B):
                pe.wait_ge(s("xsel"), b + 1)
                mm(ps[:, 4 + b, :], w("a_q"), xsel[:, b, :], start=True, stop=True).then_inc(s("qs_ps"), 1)
            NG = B * G
            for n in range(NG + 2):
                if n < NG:
                    b, g = n // G, n % G
                    pe.wait_ge(s("qbd"), b + 1)
                    pe.wait_ge(s("a_exp"), n - 1) if n >= 2 else pe.wait_ge(s("oh"), B)
                    mm(ps[:, n % 2, :], Qbd[:, b, 4 * g:4 * g + 4, :].rearrange("p h n -> p (h n)"), KT[:, b, :],
                       start=True, stop=True).then_inc(s("ag_ps"), 1)
                m = n - 1
                if 0 <= m < NG:
                    b, g = m // G, m % G
                    pe.wait_ge(s("a_exp"), m + 1)
                    pe.wait_ge(s("pta"), m - 1) if m >= 2 else pe.wait_ge(s("xsel"), B)
                    for c in range(CB):
                        i = tr(ps[:, 2 + m % 2, c * P:(c + 1) * P], Pa[:, m % 2, c * P:(c + 1) * P], ident)
                    i.then_inc(s("pta_ps"), 1)
                    pe.wait_ge(s("pta"), m + 1)
                    pe.wait_ge(s("dg"), m - 1) if m >= 2 else pe.wait_ge(s("qbd"), B)
                    for c in range(CB):
                        i = mm(ps[:, 4 + m % 2, 0:32], PTa[:, m % 2, c * P:(c + 1) * P],
                               V_tm[:, CB * b + c, 32 * g:32 * g + 32], start=(c == 0), stop=(c == CB - 1))
                    i.then_inc(s("pva_ps"), 1)
                m = n - 2
                if m >= 0:
                    b, g = m // G, m % G
                    pe.wait_ge(s("dg"), m + 1)
                    pe.wait_ge(s("oht"), m + 1)
                    i = mm(ps[32 * g:32 * g + 32, 6 + b, :], dg[:, m, :], OHT[:, m, :], start=True, stop=True)
                    if g == G - 1:
                        i.then_inc(s("ao_ps"), 1)
            for b in range(B):
                pe.wait_ge(s("a_at"), b + 1)
                for c in range(CB * b, CB * b + CB):
                    i = mm(ps[:, b, (c % CB) * P:(c % CB + 1) * P], xchunk(c, attnT), w("a_o"), start=True, stop=True)
                i.then_inc(s("a_op_ps"), 1)

            def context(l, k):
                L = f"x{l}"
                ln_transpose(k)
                for b in range(B):
                    pe.wait_ge(s("xnT"), 2 * k + b + 1)
                    mm(ps[:, 4 + b, :], w(f"{L}_q"), xnT[:, b, 1:S + 1], start=True, stop=True).then_inc(s("x_q_ps"), 1)
                pe.wait_ge(s("x_q"), 2 * l + B)
                pe.wait_ge(s("kbdx"), l + 1)
                pe.wait_ge(s("vbdx"), 2 * l + 2)
                for n in range(NT + 3):
                    if n < NT:
                        for u in range(2):
                            m = 2 * n + u
                            if m >= 2:
                                pe.wait_ge(s("x_sub"), 16 * l + m - 1)
                            for v in range(2):
                                i = mm(ps[:, 2 * u + v, 0:4 * NC], xchunk(n, QT),
                                       Kbdx[:, 2 * l + n // CB, 8 * u + 4 * v:8 * u + 4 * v + 4, :], start=True, stop=True)
                            i.then_inc(s("x_s_ps"), 1)
                    c = n - 3
                    if c >= 0:
                        pe.wait_ge(s("x_at"), 8 * l + c + 1)
                        mm(ps[:, 6 + c % 2, 384:512], xchunk(c, attnT), w(f"{L}_o"), start=True,
                           stop=True).then_inc(s("x_op_ps"), 1)
                    c = n - 1
                    if 0 <= c < NT:
                        pe.wait_ge(s("x_exp"), 16 * l + 2 * c + 2)
                        for q in range(3):
                            r = 3 * c + q
                            if r >= 2:
                                pe.wait_ge(s("x_pt"), 24 * l + r - 1)
                            for t in range(4 * q, min(4 * q + 4, NB)):
                                wd = P if t < NB - 1 else LB
                                i = tr(ps[0:wd, 4 + r % 2, (t - 4 * q) * P:(t - 4 * q + 1) * P],
                                       Ssb[:, c % 2, t * P:t * P + wd], ident)
                            i.then_inc(s("x_pt_ps"), 1)
                        pe.wait_ge(s("x_pt"), 24 * l + 3 * c + 3)
                        if c >= 2:
                            pe.wait_ge(s("x_x"), 8 * l + c - 1)
                        for t in range(NB):
                            wd = P if t < NB - 1 else LB
                            i = mm(ps[:, 6 + c % 2, 0:VW], PTx[0:wd, c % 2, t * P:(t + 1) * P],
                                   Vbdx[0:wd, 2 * l + c // CB, t, :], start=(t == 0), stop=(t == NB - 1))
                        i.then_inc(s("x_pv_ps"), 1)
                    c = n - 2
                    if 0 <= c < NT:
                        pe.wait_ge(s("x_atm"), 8 * l + c + 1)
                        tr(ps[:, 6 + c % 2, 256:384], atm[:, c % 4, :], ident).then_inc(s("x_at_ps"), 1)

            context(0, 1)

            pe.wait_ge(s("x_x"), NT)
            ln_transpose(2)
            pe.wait_ge(s("in_moe"), 16 * 4)
            pe.wait_ge(s("in_moe"), 16 * 4)
            for b in range(B):
                pe.wait_ge(s("xnT"), 2 * 2 + b + 1)
                for c in range(CB * b, CB * b + CB):
                    i = mm(ps[:, 4, c * E:(c + 1) * E], xnchunk(c), rw_sb[:, 0:E], start=True, stop=True)
            i.then_inc(s("rl_ps"), 1)

            def gate_up(n):
                b, i = n // NM, n % NM
                if n >= 2:
                    pe.wait_ge(s("m_h1"), n - 1)
                mm(ps[:, n % 2, :], wm_sb[:, i * P:(i + 1) * P], xnT[:, b, 1:S + 1], start=True,
                   stop=True).then_inc(s("g_ps"), 1)
                mm(ps[:, 2 + n % 2, :], wm_sb[:, (NM + i) * P:(NM + i + 1) * P], xnT[:, b, 1:S + 1], start=True,
                   stop=True).then_inc(s("u_ps"), 1)

            def expand(n):
                b, i = n // NM, n % NM
                if i < NM - 1:
                    m = b * (NM - 1) + i
                    pe.wait_ge(s("combT"), 3 * b + 3)
                    if m >= 2:
                        pe.wait_ge(s("m_h2"), m - 1)
                    mm(ps[:, 4 + m % 2, :], sel_sb[:, i * P:(i + 1) * P], combr[:, b * S:(b + 1) * S], start=True,
                       stop=True).then_inc(s("w_ps"), 1)

            def down(n):
                b, i = n // NM, n % NM
                if i < NM - 1:
                    pe.wait_ge(s("m_h2"), b * (NM - 1) + i + 1)
                else:
                    pe.wait_ge(s("m_h1"), n + 1)
                for c in range(CB):
                    r = mm(ps[:, 6 + b, c * P:(c + 1) * P], hs[:, n % 8, c * P:(c + 1) * P],
                           wm_sb[:, (2 * NM + i) * P:(2 * NM + i + 1) * P], start=(i == 0 and c == 0),
                           stop=(i == NM - 1), skip_group_check=True)
                r.then_inc(s("dn_ps"), 1)

            NN = B * NM
            for n in range(2):
                gate_up(n)
            for b in range(B):
                pe.wait_ge(s("comb"), b + 1)
                if b == 1:
                    pe.wait_ge(s("combT"), 3)
                for c in range(CB):
                    i = tr(ps[0:E, 5, c * P:(c + 1) * P], comb[:, CB * b + c, :], ident)
                i.then_inc(s("cT_ps"), 1)
            pe.wait_ge(s("combT"), 6)
            for n in range(NN + 1):
                if n < NN:
                    expand(n)
                if n >= 1:
                    down(n - 1)
                if 1 <= n < NN - 1:
                    gate_up(n + 1)

            pe.wait_ge(s("m_x"), NT)
            ln_transpose(3)
            pe.wait_ge(s("in_last"), 16 * 4)
            for b in range(B):
                pe.wait_ge(s("mix"), 4 * b + 4)
                if b == 1:
                    pe.wait_ge(s("r_pj"), 5)
                    pe.wait_ge(s("r_kt"), 1)
                    pe.wait_ge(s("r_vt"), 1)
                mk, mv_, mr, mg = (mixes[:, i, b, :] for i in range(4))
                mm(ps[:, 0, :], w("w_r"), mr, start=True, stop=True).then_inc(s("r_pj_ps"), 1)
                mm(ps[:, 1, :], w("w_k"), mk, start=True, stop=True).then_inc(s("r_pj_ps"), 1)
                for j in range(CB):
                    i = mm(ps[:, 2, j * P:(j + 1) * P], mk[:, j * P:(j + 1) * P], w("w_k"), start=True, stop=True)
                i.then_inc(s("r_kt_ps"), 1)
                for j in range(CB):
                    i = mm(ps[:, 3, j * P:(j + 1) * P], mv_[:, j * P:(j + 1) * P], w("w_v"), start=True, stop=True)
                i.then_inc(s("r_vt_ps"), 1)
                for j in range(CB):
                    i = mm(ps[:, 4, j * P:(j + 1) * P], mg[:, j * P:(j + 1) * P], w("w_g"), start=True, stop=True)
                i.then_inc(s("r_g_ps"), 1)

            def r_scores(c):
                pe.wait_ge(s("rbd_v"), c + 1)
                pe.wait_ge(s("rbd_p"), c + 1)
                for q in range(4):
                    if c >= 1:
                        pe.wait_ge(s("r_p"), 4 * (c - 1) + q + 1)
                    mm(ps[:, q, :], xchunk(c, KT), Rbd[:, c % 2, 4 * q:4 * q + 4, :], start=True,
                       stop=True).then_inc(s("r_s_ps"), 1)
                if c % CB < CB - 1:
                    if c >= 1:
                        pe.wait_ge(s("um"), c - c // CB)
                    mm(ps[:, 5, 0:P], Ktm[:, c, :], V_tm[:, c, :], start=True, stop=True).then_inc(s("u_st_ps"), 1)

            def r_out(c):
                b, j = c // CB, c % CB
                y = ps[:, 6 + b, j * P:(j + 1) * P]
                if j:
                    pe.wait_ge(s("state"), b * (CB - 1) + j)
                    mm(y, xchunk(c, Rw), St[:, (b * (CB - 1) + j - 1) % 2, :], start=False, stop=False, skip_group_check=True)
                for h in range(H):
                    if h % 4 == 0:
                        pe.wait_ge(s("r_p"), 4 * c + h // 4 + 1)
                    i = mm(y[:, h * HD:(h + 1) * HD], Pr[:, c % 2, h, :], V_tm[:, c, h * HD:(h + 1) * HD],
                           start=(j == 0 and h == 0), stop=(h == H - 1), skip_group_check=True)
                i.then_inc(s("y_ps"), 1)

            pe.wait_ge(s("r_pj"), 10)
            pe.wait_ge(s("r_kt"), 2)
            pe.wait_ge(s("r_vt"), 2)
            pe.wait_ge(s("xnT"), 8)
            for c in range(NT + 1):
                if c < NT:
                    r_scores(c)
                if c >= 1:
                    r_out(c - 1)
            for b in range(B):
                for j in range(CB):
                    pe.wait_ge(s("r_yg"), CB * b + j + 1)
                    i = tr(ps[:, b, j * P:(j + 1) * P], yc[:, b, j * P:(j + 1) * P], ident)
                i.then_inc(s("r_at_ps"), 1)
            for b in range(B):
                pe.wait_ge(s("r_at"), b + 1)
                for c in range(CB * b, CB * b + CB):
                    i = mm(ps[:, 2 + b, (c % CB) * P:(c % CB + 1) * P], xchunk(c, attnT), w("w_o"), start=True, stop=True)
                i.then_inc(s("r_op_ps"), 1)

            context(1, 4)

            pe.wait_ge(s("x_x"), 2 * NT)
            ln_transpose(5)
            ln_transpose(0, sem="hn2", out_sem="hnT_ps", bank=4)
            pe.wait_ge(s("in_last"), 16 * 4)
            pe.wait_ge(s("hnT"), 2)
            pe.wait_ge(s("xnT"), 12)
            for c in range(NT):
                i = mm(ps[:, 6, c * FE:(c + 1) * FE], hnT[:, c // CB, (c % CB) * P:(c % CB + 1) * P],
                       rw_sb[:, E:E + FE], start=True, stop=True)
            i.then_inc(s("fl_ps"), 1)
            pe.wait_ge(s("in_last"), 16 * 4)
            pe.wait_ge(s("in_last"), 16 * 4)

            def f_hidden(c):
                if c >= 2:
                    pe.wait_ge(s("f_hn"), 4 * (c - 1))
                for v in range(2):
                    i = mm(ps[:, 2 * (c % 2) + v, :], xnchunk(c), w1_sb[:, v * 512:(v + 1) * 512], start=True, stop=True)
                i.then_inc(s("f_h_ps"), 1)

            def f_turn(b):
                pe.wait_ge(s("f_hn"), 4 * CB * (b + 1))
                for q in range(8):
                    r = 8 * b + q
                    if r >= 2:
                        pe.wait_ge(s("f_hT"), r - 1)
                    for j in range(CB):
                        i = tr(ps[:, 4 + r % 2, j * P:(j + 1) * P], hn[:, j, q * P:(q + 1) * P], ident)
                    i.then_inc(s("f_hT_ps"), 1)

            def f_down(b):
                pe.wait_ge(s("f_hT"), 8 * (b + 1))
                for j in range(CB):
                    c = CB * b + j
                    if c == 0:
                        pe.wait_ge(s("fsub"), 1)
                    if c >= 2:
                        pe.wait_ge(s("f_cmb"), c - 1)
                    for e in range(FE):
                        for v in range(2):
                            i = mm(ps[:, 6 + c % 2, e * P:(e + 1) * P], hidT[:, 2 * e + v, j * P:(j + 1) * P],
                                   w2_sb[:, (2 * e + v) * P:(2 * e + v + 1) * P], start=(v == 0), stop=(v == 1))
                    i.then_inc(s("f_o_ps"), 1)

            for b in range(B):
                for j in range(CB):
                    f_hidden(CB * b + j)
                f_turn(b)
                f_down(b)

        @block.scalar
        def _(act):
            A = nc.scalar.activation
            act.wait_ge(s("in_attn"), 16 * 3)

            def ln_copy(k):
                for b in range(B):
                    if k == 0 and b == 0:
                        act.wait_ge(s("zero"), 1)
                    act.wait_ge(s("xnT_ps"), 2 * k + b + 1)
                    A(xnT[:, b, 1:S + 1], ps[:, 6 + b, :], ACT.Copy).then_inc(s("xnT"), 1)

            ln_copy(0)
            for b in range(B):
                act.wait_ge(s("xsamp_ps"), b + 1)
                A(xsamp[:, b, :], ps[:, b, 0:NS], ACT.Copy).then_inc(s("xsamp"), 1)
            for b in range(B):
                act.wait_ge(s("ks_ps"), b + 1)
                A(KsT[:, b, :], ps[:, 2 + b, 0:NS], ACT.Identity, bias=col("a_bk")).then_inc(s("ks"), 1)
            for b in range(B):
                act.wait_ge(s("a_q_ps"), b + 1)
                A(QT[:, b, :], ps[:, 4 + b, :], ACT.Identity, bias=col("a_bq")).then_inc(s("a_q"), 1)
            act.wait_ge(s("ks"), B)
            act.wait_ge(s("in_first"), 16 * 3)

            def key_blocks(b):
                for h in range(H // 2, H):
                    i = A(Kbd[:, b, h, :], KsT[:, b, :], ACT.Copy, scale=hmask[:, h:h + 1])
                i.then_inc(s("kbd_a"), 1)

            key_blocks(0)
            for b in range(B):
                act.wait_ge(s("a_k_ps"), b + 1)
                A(KT[:, b, :], ps[:, b, :], ACT.Identity, bias=col("a_bk")).then_inc(s("a_k"), 1)
            key_blocks(1)
            act.wait_ge(s("in_ctx"), 16 * 5)
            A(lamr[:, :], tdr[:, :], ACT.Exp).then_inc(s("lam"), 1)
            A(lamc[:, 0:1], col("td"), ACT.Exp).then_inc(s("lam"), 1)
            g = 0
            for l in range(2):
                act.wait_ge(s("pre_ps"), g + 1)
                A(Kx[:, l, :, :].rearrange("p b n -> p (b n)"), ps[:, 6, 0:B * NC], ACT.Identity,
                  bias=col(f"x{l}_bk")).then_inc(s("pre"), 1)
                g += 1
            for l in range(2):
                for b in range(B):
                    for q in range(3):
                        act.wait_ge(s("pre_ps"), g + 1)
                        m = min(4, NB - 4 * q)
                        A(Vbdx[:, 2 * l + b, 4 * q:4 * q + m, 0:P],
                          ps[:, 6, 0:m * P].rearrange("p (n d) -> p n d", d=P), ACT.Copy).then_inc(s("pre"), 1)
                        g += 1
            act.wait_ge(s("lam_ok"), 4)
            A(rpow[:, :], trow, ACT.Exp, scale=lamc[:, 1:2]).then_inc(s("tabs"), 1)
            A(kpow[:, :], lamr[:, :], ACT.Exp, scale=ncol).then_inc(s("tabs"), 1)
            A(w128, lamc[:, 1:2], ACT.Exp, scale=float(P)).then_inc(s("tabs"), 1)
            act.wait_ge(s("gap"), 1)
            A(Wtab[:, :, :], Wtab[:, :, :], ACT.Exp, scale=-1.0).then_inc(s("wexp"), 1)
            act.wait_ge(s("mT_ps"), 1)
            A(MT[:, 0, :], ps[0:32, 6, :], ACT.Copy).then_inc(s("mT"), 1)
            act.wait_ge(s("vm_ps"), B)
            A(Vmb[:, :, :].rearrange("p b d -> p (b d)"), ps[:, 2, 0:2 * P], ACT.Copy).then_inc(s("vm"), 1)
            A(Vmc[:, :], ps[:, 2, 256:256 + B], ACT.Copy).then_inc(s("vm"), 1)
            for b in range(B):
                act.wait_ge(s("xsel_ps"), b + 1)
                A(xsel[:, b, :], ps[:, 2 + b, :], ACT.Copy).then_inc(s("xsel"), 1)
            for n in range(B * G + 1):
                if n < B * G:
                    act.wait_ge(s("nb"), n + 1)
                    if n >= 2:
                        act.wait_ge(s("pta_ps"), n - 1)
                    A(Pa[:, n % 2, :], ps[:, n % 2, :], ACT.Exp, bias=nb[:, n:n + 1], scale=ASCALE,
                      accum_out=rsum[:, n:n + 1]).then_inc(s("a_exp"), 1)
                m = n - 1
                if m >= 0:
                    act.wait_ge(s("pta_ps"), m + 1)
                    if m >= 2:
                        act.wait_ge(s("pva_ps"), m - 1)
                    A(PTa[:, m % 2, :], ps[:, 2 + m % 2, :], ACT.Copy).then_inc(s("pta"), 1)
            for b in range(B):
                act.wait_ge(s("ao_ps"), b + 1)
                A(attnT[:, b, :], ps[:, 6 + b, :], ACT.Identity, bias=Vmc[:, b:b + 1]).then_inc(s("a_at"), 1)

            def context(l, k):
                L = f"x{l}"
                ln_copy(k)
                for b in range(B):
                    act.wait_ge(s("x_q_ps"), 2 * l + b + 1)
                    A(QT[:, b, :], ps[:, 4 + b, :], ACT.Identity, bias=col(f"{L}_bq")).then_inc(s("x_q"), 1)
                for n in range(NT + 2):
                    c = n - 1
                    if 0 <= c < NT:
                        for q in range(3):
                            r = 3 * c + q
                            act.wait_ge(s("x_pt_ps"), 24 * l + r + 1)
                            if c >= 2 and q == 0:
                                act.wait_ge(s("x_pv_ps"), 8 * l + c - 1)
                            t0, t1 = 4 * q, min(4 * q + 4, NB)
                            if q < 2:
                                A(PTx[:, c % 2, t0 * P:t1 * P], ps[:, 4 + r % 2, :], ACT.Copy).then_inc(s("x_pt"), 1)
                            else:
                                A(PTx[:, c % 2, t0 * P:(t1 - 1) * P], ps[:, 4 + r % 2, 0:P], ACT.Copy)
                                A(PTx[0:LB, c % 2, (t1 - 1) * P:t1 * P], ps[0:LB, 4 + r % 2, P:2 * P],
                                  ACT.Copy).then_inc(s("x_pt"), 1)
                    if n < NT:
                        for u in range(2):
                            act.wait_ge(s("x_sub"), 16 * l + 2 * n + u + 1)
                            v = Ssb[:, n % 2, u * 8 * NC:(u + 1) * 8 * NC]
                            A(v, v, ACT.Exp, scale=ASCALE).then_inc(s("x_exp"), 1)
                    c = n - 2
                    if c >= 0:
                        act.wait_ge(s("x_at_ps"), 8 * l + c + 1)
                        A(xchunk(c, attnT), ps[:, 6 + c % 2, 256:384], ACT.Copy).then_inc(s("x_at"), 1)

            context(0, 1)

            ln_copy(2)
            act.wait_ge(s("rl_ps"), 1)
            A(sg[:, :, :].rearrange("p c e -> p (c e)"), ps[:, 4, 0:NT * E], ACT.Exp, scale=-1.0).then_inc(s("m_en"), 1)

            def silu(n):
                act.wait_ge(s("g_ps"), n + 1)
                if n >= 8:
                    act.wait_ge(s("dn_ps"), n - 7)
                A(hs[:, n % 8, :], ps[:, n % 2, :], ACT.Silu).then_inc(s("m_silu"), 1)

            for n in range(B * NM):
                silu(n)

            ln_copy(3)
            for b in range(B):
                act.wait_ge(s("r_pj_ps"), 2 * b + 1)
                A(QT[:, b, :], ps[:, 0, :], ACT.Copy).then_inc(s("r_pj"), 1)
                act.wait_ge(s("r_pj_ps"), 2 * b + 2)
                A(KT[:, b, :], ps[:, 1, :], ACT.Copy).then_inc(s("r_pj"), 1)
                act.wait_ge(s("r_g_ps"), b + 1)
                A(Gtm[:, CB * b:CB * b + CB, :].rearrange("p c n -> p (c n)"), ps[:, 4, :], ACT.Silu).then_inc(s("r_pj"), 3)
            for b in range(B):
                act.wait_ge(s("r_yc"), b + 1)
                A(sq[:, b, :], yc[:, b, :], ACT.Square).then_inc(s("r_sq"), 1)
            for b in range(B):
                act.wait_ge(s("r_at_ps"), b + 1)
                A(attnT[:, b, :], ps[:, b, :], ACT.Copy).then_inc(s("r_at"), 1)

            context(1, 4)

            ln_copy(5)
            for b in range(B):
                act.wait_ge(s("hnT_ps"), b + 1)
                A(hnT[:, b, :], ps[:, 4 + b, :], ACT.Identity, scale=col("rn_g"), bias=col("rn_b")).then_inc(s("hnT"), 1)
            act.wait_ge(s("fsub"), 1)
            A(fsm[:, :, :], fsm[:, :, :], ACT.Exp).then_inc(s("fexp"), 1)
            for b in range(B):
                for j in range(CB):
                    c = CB * b + j
                    act.wait_ge(s("f_st"), c + 1)
                    if b == 1 and j == 0:
                        act.wait_ge(s("f_hT_ps"), 8)
                    for e in range(FE):
                        A(hn[:, j, e * FH:(e + 1) * FH], ps[:, 2 * (c % 2) + e // 2, (e % 2) * FH:(e % 2 + 1) * FH],
                          ACT.Identity, scale=frs[:, c, e:e + 1], bias=fnm[:, c, e:e + 1]).then_inc(s("f_hn"), 1)
                for q in range(8):
                    act.wait_ge(s("f_hT_ps"), 8 * b + q + 1)
                    if b == 1 and q == 0:
                        act.wait_ge(s("f_o_ps"), CB)
                    A(hidT[:, q, :], ps[:, 4 + (8 * b + q) % 2, :], ACT.Relu, scale=colsb[:, len(COLS) + q:len(COLS) + q + 1],
                      bias=colsb[:, len(COLS) + 8 + q:len(COLS) + 9 + q]).then_inc(s("f_hT"), 1)

        @block.vector
        def _(dve):
            V = nc.vector
            chain = [0]

            def link(ins):
                chain[0] += 1
                ins.then_inc(s("dve_chain"), 1)
                dve.wait_ge(s("dve_chain"), chain[0])

            def layernorm(k):
                for b in range(B):
                    cs = range(CB * b, CB * b + CB)
                    for c in cs:
                        wait_x(dve, k, c)
                        i = V.bn_stats(st[:, c, :], x_tm[:, c, :])
                    link(i)
                    for c in cs:
                        i = V.bn_aggr(mv[:, c, :], st[:, c, :])
                    link(i)
                    V.tensor_scalar(veps[:, CB * b:CB * b + CB], mv[:, CB * b:CB * b + CB, 1], 1e-5, None,
                                    ALU.add).then_inc(s("veps"), 1)
                for b in range(B):
                    dve.wait_ge(s("rstd"), 2 * k + b + 1)
                    for c in range(CB * b, CB * b + CB):
                        V.tensor_scalar(xn_tm[:, c, :], x_tm[:, c, :], mv[:, c, 0:1], rstd[:, c:c + 1],
                                        ALU.subtract, ALU.mult).then_inc(s("xn"), 1)

            def add_residual(bank, b, sem, ops):
                dve.wait_ge(s(ops), b + 1)
                cs = slice(CB * b, CB * b + CB)
                V.tensor_tensor(x_tm[:, cs, :], ps[:, bank, :].rearrange("p (c d) -> p c d", c=CB), xb[:, cs, :],
                                ALU.add).then_inc(s(sem), CB)

            dve.wait_ge(s("in_first"), 16 * 3)
            dve.wait_ge(s("in_first"), 16 * 3)
            link(V.tensor_copy(sidx_f[:, :], sidx_i[:, :]))
            for c in range(CB):
                i = V.tensor_scalar(ohs[:, c, :], sidx_f[:, :], iota_pc[:, c:c + 1], None, ALU.is_equal)
            i.then_inc(s("ohs"), 1)
            layernorm(0)
            for b in range(B):
                dve.wait_ge(s("ks"), b + 1)
                V.tensor_tensor(Kbd[:, b, 0:8, :], KsT[:, b, :].unsqueeze(1).broadcast_to([P, 8, NS]),
                                hmask[:, 0:8].unsqueeze(2).broadcast_to([P, 8, NS]), ALU.mult).then_inc(s("kbd_v"), 1)
                link(V.reduce_sum(kbar[:, b:b + 1], KsT[:, b, :], AXX))
                V.tensor_scalar(kbarbd[:, b, :], hmask, kbar[:, b:b + 1], 1.0 / NS, ALU.mult, ALU.mult).then_inc(s("kbar"), 1)
                if b == 0:
                    dve.wait_ge(s("in_attn"), 16 * 3)
            for b in range(B):
                dve.wait_ge(s("a_v_ps"), b + 1)
                V.tensor_tensor(V_tm[:, CB * b:CB * b + CB, :], ps[:, 2 + b, :].rearrange("p (c d) -> p c d", c=CB),
                                row("a_bv").unsqueeze(1).broadcast_to([P, CB, D]), ALU.add).then_inc(s("a_v"), 1)
            for n in range(4 * NT):
                c, hq = n // 4, n % 4
                pair = 2 * (n % 3)
                dve.wait_ge(s("as_ps"), n + 1)
                V.tensor_reduce(Mx[:, c % CB, c // CB, 4 * hq:4 * hq + 4],
                                ps[:, pair:pair + 2, :].rearrange("p v (h n) -> p (v h) n", n=NS),
                                AXX, ALU.max).then_inc(s("mx"), 1)
            dve.wait_ge(s("mx"), 4 * NT)
            dve.wait_ge(s("mean_ps"), NT)
            V.tensor_tensor(Mx[:, :, :, :], Mx[:, :, :, :],
                            ps[:, 7, 0:NT * H].rearrange("p (b c h) -> p c b h", b=B, c=CB), ALU.subtract).then_inc(s("m"), 1)
            dve.wait_ge(s("mT"), 1)
            for r in range(4):
                cur, nxt = MT[:, r % 2, :], MT[:, 1 - r % 2, :]
                v = v8[:, 8 * r:8 * r + 8]
                link(V.max(v, cur))
                link(V.max_index(idx[:, 8 * r:8 * r + 8], v, cur))
                if r < 3:
                    link(V.match_replace(nxt, v, cur, NEG))
            link(V.tensor_copy(idxf[:, :], idx[:, :]))
            V.tensor_tensor(diag[:, :, :], idxf[:, :].unsqueeze(1).broadcast_to([32, 32, SLOTS]),
                            ident[0:32, 0:32].unsqueeze(2).broadcast_to([32, 32, SLOTS]), ALU.mult).then_inc(s("diag"), 1)
            link(V.transpose(idxT[:, :], idxf[:, :]))
            for j in range(4):
                i = V.tensor_copy(idxcol[32 * j:32 * j + 32, :], idxT[:, j::4])
            link(i)
            for b in range(B):
                dve.wait_ge(s("ib_ps"), b + 1)
                for c in range(CB):
                    i = V.tensor_scalar(OH[:, CB * b + c, :], ps[:, b, :], iota_pc[:, c:c + 1], None, ALU.is_equal)
                i.then_inc(s("oh"), 1)
            for b in range(B):
                dve.wait_ge(s("qs_ps"), b + 1)
                V.scalar_tensor_tensor(out=Qbd[:, b, :, :], in0=ps[:, 4 + b, :].rearrange("p (h n) -> p h n", h=H),
                                       scalar=col("a_bq"), in1=hmask.unsqueeze(2).broadcast_to([P, H, SLOTS]),
                                       op0=ALU.add, op1=ALU.mult).then_inc(s("qbd"), 1)

            def place(n):
                V.tensor_scalar(OHT[:, n, :], iota_row, idxcol[:, n:n + 1], None, ALU.is_equal).then_inc(s("oht"), 1)

            place(0)
            place(1)
            for n in range(B * G + 1):
                if n < B * G:
                    dve.wait_ge(s("ag_ps"), n + 1)
                    link(V.tensor_reduce(nmx[:, n:n + 1], ps[:, n % 2, :], AXX, ALU.max))
                    V.tensor_scalar(nb[:, n:n + 1], nmx[:, n:n + 1], -ASCALE, None, ALU.mult).then_inc(s("nb"), 1)
                if n + 2 < B * G:
                    place(n + 2)
                m = n - 1
                if m >= 0:
                    b, g = m // G, m % G
                    dve.wait_ge(s("a_exp"), m + 1)
                    link(V.reciprocal(rinv[:, m:m + 1], rsum[:, m:m + 1]))
                    dve.wait_ge(s("pva_ps"), m + 1)
                    dve.wait_ge(s("vm"), B)
                    link(V.scalar_tensor_tensor(out=dgt[:, m, :], in0=ps[:, 4 + m % 2, 0:32], scalar=rinv[:, m:m + 1],
                                                in1=Vmb[:, b, 32 * g:32 * g + 32], op0=ALU.mult, op1=ALU.subtract))
                    V.tensor_tensor(dg[:, m, :], dgt[:, m, :], slotmask, ALU.mult).then_inc(s("dg"), 1)
            for b in range(B):
                dve.wait_ge(s("xb"), b + 1)
                add_residual(b, b, "a_x", "a_op_ps")

            def context(l, k, xbk):
                L = f"x{l}"
                layernorm(k)
                for n in range(NT + 3):
                    if n < NT:
                        for u in range(2):
                            dve.wait_ge(s("x_s_ps"), 16 * l + 2 * n + u + 1)
                            src = ps[:, 2 * u:2 * u + 2, 0:4 * NC].rearrange("p v (h n) -> p v h n", n=NC)
                            m8 = mxx[:, n % 2, 8 * u:8 * u + 8]
                            link(V.tensor_reduce(m8.rearrange("p (v h) -> p v h", v=2), src, AXX, ALU.max))
                            if n >= 2 and u == 0:
                                dve.wait_ge(s("x_pt_ps"), 24 * l + 3 * (n - 1))
                            V.tensor_tensor(Ssb[:, n % 2, u * 8 * NC:(u + 1) * 8 * NC].rearrange("p (v h n) -> p v h n", v=2, h=4),
                                            src, m8.rearrange("p (v h) -> p v h", v=2).unsqueeze(3).broadcast_to([P, 2, 4, NC]),
                                            ALU.subtract).then_inc(s("x_sub"), 1)
                    c = n - 3
                    if c >= 0:
                        dve.wait_ge(s("x_op_ps"), 8 * l + c + 1)
                        dve.wait_ge(s("xb"), xbk + c // CB + 1)
                        V.tensor_tensor(x_tm[:, c, :], ps[:, 6 + c % 2, 384:512], xb[:, c, :], ALU.add).then_inc(s("x_x"), 1)
                    c = n - 1
                    if 0 <= c < NT:
                        dve.wait_ge(s("x_pv_ps"), 8 * l + c + 1)
                        bank = ps[:, 6 + c % 2, :]
                        link(V.tensor_scalar(rsx[:, 0, :], bank[:, D:VW], 1e-9 if l == 0 else 0.0, None, ALU.add))
                        link(V.reciprocal(rsx[:, 1, :], rsx[:, 0, :]))
                        V.tensor_tensor(atm[:, c % 4, :].rearrange("p (h d) -> p h d", h=H),
                                        bank[:, 0:D].rearrange("p (h d) -> p h d", h=H),
                                        rsx[:, 1, :].unsqueeze(2).broadcast_to([P, H, HD]), ALU.mult).then_inc(s("x_atm"), 1)

            context(0, 1, 2)

            layernorm(2)
            dve.wait_ge(s("wmask"), 1)
            dve.wait_ge(s("in_ctx"), 16 * 5)
            for h in range(H):
                i = V.scalar_tensor_tensor(out=Wtab[:, h, :], in0=ident, scalar=ur[:, h:h + 1], in1=Wtab[:, h, :],
                                           op0=ALU.mult, op1=ALU.add)
            i.then_inc(s("wtab"), 1)
            dve.wait_ge(s("m_en"), 1)
            dve.wait_ge(s("in_moe"), 16 * 4)
            link(V.tensor_scalar(sg[:, :, :], sg[:, :, :], 1.0, None, ALU.add))
            link(V.reciprocal(sg[:, :, :], sg[:, :, :]))
            link(V.tensor_tensor(sc[:, :, :], sg[:, :, :], eb_sb[:, :].unsqueeze(1).broadcast_to([P, NT, E]), ALU.add))
            s4 = sc[:, :, :].rearrange("p c (g e) -> p c g e", g=EG)

            def r4(i):
                return rt[:, :, 4 * i:4 * i + 4]

            V.tensor_tensor(r4(0), s4[:, :, :, 0], s4[:, :, :, 1], ALU.max)
            V.tensor_tensor(r4(1), s4[:, :, :, 0], s4[:, :, :, 1], ALU.min)
            V.tensor_tensor(r4(2), s4[:, :, :, 2], s4[:, :, :, 3], ALU.max)
            link(V.tensor_tensor(r4(3), s4[:, :, :, 2], s4[:, :, :, 3], ALU.min))
            V.tensor_tensor(r4(4), r4(0), r4(2), ALU.max)
            V.tensor_tensor(r4(5), r4(0), r4(2), ALU.min)
            link(V.tensor_tensor(r4(6), r4(1), r4(3), ALU.max))
            link(V.tensor_tensor(r4(5), r4(5), r4(6), ALU.max))
            link(V.tensor_tensor(r4(7), r4(4), r4(5), ALU.add))

            def rank_of(vals, cnt, dst, before, t1, t2):
                me = vals.unsqueeze(3).broadcast_to([P, NT, cnt, cnt])
                other = vals.unsqueeze(2).broadcast_to([P, NT, cnt, cnt])
                bm = before.unsqueeze(1).broadcast_to([P, NT, cnt, cnt])
                V.tensor_tensor(t1, other, me, ALU.is_gt)
                link(V.tensor_tensor(t2, other, me, ALU.is_equal))
                link(V.tensor_tensor(t2, t2, bm, ALU.mult))
                link(V.tensor_tensor(t1, t1, t2, ALU.add))
                link(V.reduce_sum(dst, t1, AXX))

            c1 = rt[:, :, 32:48].rearrange("p c (a b) -> p c a b", a=4)
            c2 = rt[:, :, 48:64].rearrange("p c (a b) -> p c a b", a=4)
            rank_of(r4(7), 4, r4(0), before4, c1, c2)
            link(V.tensor_scalar(r4(1), r4(0), 1.5, None, ALU.is_lt))
            link(V.tensor_tensor(sc[:, :, :].rearrange("p c (g e) -> p c g e", g=EG), s4,
                                 r4(1).unsqueeze(3).broadcast_to([P, NT, EG, 4]), ALU.mult))
            rank_of(sc[:, :, :], E, rank[:, :, :], before16, cmp1, cmp2)
            link(V.tensor_scalar(rank[:, :, :], rank[:, :, :], 3.5, None, ALU.is_lt))
            link(V.tensor_tensor(rank[:, :, :], rank[:, :, :], sg[:, :, :], ALU.mult))
            link(V.reduce_sum(den[:, :], rank[:, :, :], AXX))
            link(V.tensor_scalar(den[:, :], den[:, :], 1e-20, None, ALU.add))
            link(V.reciprocal(den[:, :], den[:, :]))
            link(V.tensor_scalar(den[:, :], den[:, :], 2.5, None, ALU.mult))
            V.tensor_tensor(comb[:, :, :], rank[:, :, :], den[:, :].unsqueeze(2).broadcast_to([P, NT, E]),
                            ALU.mult).then_inc(s("comb"), 2)
            dve.wait_ge(s("zero"), 2)
            for b in range(B):
                src, bs = ps[0:E, 5, :], slice(b * S, (b + 1) * S)
                dve.wait_ge(s("cT_ps"), b + 1)
                V.tensor_copy(combr[0:E, bs], src).then_inc(s("combT"), 1)
                dve.wait_ge(s("combT"), 3 * b + 1)
                link(V.tensor_tensor(cr[0:E, :], src, combr[0:E, bs], ALU.subtract))
                V.tensor_copy(combr[32:32 + E, bs], cr[0:E, :]).then_inc(s("combT"), 1)
                link(V.tensor_copy(crb[0:E, :], cr[0:E, :]))
                V.tensor_tensor(combr[64:64 + E, bs], cr[0:E, :], crb[0:E, :], ALU.subtract).then_inc(s("combT"), 1)
            for n in range(B * NM):
                b, i = n // NM, n % NM
                dve.wait_ge(s("m_silu"), n + 1)
                dve.wait_ge(s("u_ps"), n + 1)
                V.tensor_tensor(hs[:, n % 8, :], hs[:, n % 8, :], ps[:, 2 + n % 2, :], ALU.mult).then_inc(s("m_h1"), 1)
                if i < NM - 1:
                    m = b * (NM - 1) + i
                    dve.wait_ge(s("m_h1"), n + 1)
                    dve.wait_ge(s("w_ps"), m + 1)
                    V.tensor_tensor(hs[:, n % 8, :], hs[:, n % 8, :], ps[:, 4 + m % 2, :], ALU.mult).then_inc(s("m_h2"), 1)
            for b in range(B):
                dve.wait_ge(s("dn_ps"), NM * (b + 1))
                cs = slice(CB * b, CB * b + CB)
                V.tensor_tensor(x_tm[:, cs, :], ps[:, 6 + b, :].rearrange("p (c d) -> p c d", c=CB), x_tm[:, cs, :],
                                ALU.add).then_inc(s("m_x"), CB)

            layernorm(3)
            for b in range(B):
                dve.wait_ge(s("xnT"), 2 * 3 + b + 1)
                link(V.tensor_tensor(xx[:, b, :], xnT[:, b, 0:S], xnT[:, b, 1:S + 1], ALU.subtract))
                for i, n in enumerate(("maa_k", "maa_v", "maa_r", "maa_g")):
                    V.scalar_tensor_tensor(out=mixes[:, i, b, :], in0=xx[:, b, :], scalar=col(n), in1=xnT[:, b, 1:S + 1],
                                           op0=ALU.mult, op1=ALU.add).then_inc(s("mix"), 1)
            dve.wait_ge(s("tabs"), 3)
            for b in range(B):
                cs = slice(CB * b, CB * b + CB)
                dve.wait_ge(s("r_kt_ps"), b + 1)
                V.tensor_tensor(Ktm[:, cs, :], ps[:, 2, :].rearrange("p (c d) -> p c d", c=CB),
                                kpow[:, :].unsqueeze(1).broadcast_to([P, CB, D]), ALU.mult).then_inc(s("r_kt"), 1)
                dve.wait_ge(s("r_vt_ps"), b + 1)
                V.tensor_copy(V_tm[:, cs, :], ps[:, 3, :].rearrange("p (c d) -> p c d", c=CB)).then_inc(s("r_vt"), 1)
                dve.wait_ge(s("r_pj"), 5 * b + 1)
                V.tensor_tensor(Rw[:, b, :].rearrange("p (c t) -> p c t", c=CB), QT[:, b, :].rearrange("p (c t) -> p c t", c=CB),
                                rpow[:, :].unsqueeze(1).broadcast_to([P, CB, P]), ALU.mult).then_inc(s("rw"), 1)
            dve.wait_ge(s("r_g_ps"), B)
            for c in range(NT + 1):
                if c < NT:
                    if c >= 2:
                        dve.wait_ge(s("r_s_ps"), 4 * (c - 1))
                    V.tensor_tensor(Rbd[:, c % 2, 0:HV, :], xchunk(c, QT).unsqueeze(1).broadcast_to([P, HV, P]),
                                    hmask[:, 0:HV].unsqueeze(2).broadcast_to([P, HV, P]), ALU.mult).then_inc(s("rbd_v"), 1)
                m = c - 1
                if m < 0:
                    continue
                b, j = m // CB, m % CB
                for q in range(4):
                    dve.wait_ge(s("r_s_ps"), 4 * m + q + 1)
                    if m >= 2 and q == 0:
                        dve.wait_ge(s("y_ps"), m - 1)
                    V.tensor_tensor(Pr[:, m % 2, 4 * q:4 * q + 4, :], ps[:, q, :].rearrange("p (h t) -> p h t", h=4),
                                    Wtab[:, 4 * q:4 * q + 4, :], ALU.mult).then_inc(s("r_p"), 1)
                if j < CB - 1:
                    k = b * (CB - 1) + j
                    dve.wait_ge(s("u_st_ps"), k + 1)
                    if k >= 2:
                        dve.wait_ge(s("y_ps"), m)
                    if k:
                        dve.wait_ge(s("state"), k)
                    V.tensor_tensor(Um[:, :], ps[:, 5, 0:P], bdiag, ALU.mult).then_inc(s("um"), 1)
                    dve.wait_ge(s("um"), k + 1)
                    if j == 0:
                        V.tensor_copy(St[:, k % 2, :], Um[:, :]).then_inc(s("state"), 1)
                    else:
                        dve.wait_ge(s("state"), k)
                        V.scalar_tensor_tensor(out=St[:, k % 2, :], in0=St[:, (k - 1) % 2, :], scalar=w128, in1=Um[:, :],
                                               op0=ALU.mult, op1=ALU.add).then_inc(s("state"), 1)
            for b in range(B):
                y = ps[:, 6 + b, :].rearrange("p (g d) -> p g d", d=HD)
                ys = yc[:, b, :].rearrange("p (g d) -> p g d", d=HD)
                dve.wait_ge(s("y_ps"), CB * (b + 1))
                link(V.reduce_sum(gm[:, b, :], y, AXX))
                link(V.tensor_scalar(gm[:, b, :], gm[:, b, :], 1.0 / HD, None, ALU.mult))
                V.tensor_tensor(ys, y, gm[:, b, :].unsqueeze(2).broadcast_to([P, 64, HD]), ALU.subtract).then_inc(s("r_yc"), 1)
            for b in range(B):
                dve.wait_ge(s("r_sq"), b + 1)
                link(V.reduce_sum(gv[:, b, :], sq[:, b, :].rearrange("p (g d) -> p g d", d=HD), AXX))
                V.tensor_scalar(gv[:, b, :], gv[:, b, :], 1.0 / HD, 64e-5, ALU.mult, ALU.add).then_inc(s("r_var"), 1)
            for b in range(B):
                ys = yc[:, b, :].rearrange("p (g d) -> p g d", d=HD)
                yr = yc[:, b, :].rearrange("p (c d) -> p c d", c=CB)
                dve.wait_ge(s("r_rstd"), b + 1)
                link(V.tensor_tensor(ys, ys, gm[:, b, :].unsqueeze(2).broadcast_to([P, 64, HD]), ALU.mult))
                link(V.tensor_tensor(yr, yr, row("ln_g").unsqueeze(1).broadcast_to([P, CB, D]), ALU.mult))
                link(V.tensor_tensor(yr, yr, row("ln_b").unsqueeze(1).broadcast_to([P, CB, D]), ALU.add))
                V.tensor_tensor(yr, yr, Gtm[:, CB * b:CB * b + CB, :], ALU.mult).then_inc(s("r_yg"), CB)
            for b in range(B):
                dve.wait_ge(s("r_op_ps"), b + 1)
                cs = slice(CB * b, CB * b + CB)
                V.tensor_tensor(x_tm[:, cs, :], ps[:, 2 + b, :].rearrange("p (c d) -> p c d", c=CB), x_tm[:, cs, :],
                                ALU.add).then_inc(s("r_x"), CB)

            context(1, 4, 4)

            layernorm(5)
            for b in range(B):
                cs = range(CB * b, CB * b + CB)
                dve.wait_ge(s("xn"), 5 * NT + CB * (b + 1))
                for c in cs:
                    i = V.bn_stats(st[:, c, :], xn_tm[:, c, :])
                link(i)
                for c in cs:
                    i = V.bn_aggr(mv[:, c, :], st[:, c, :])
                link(i)
                V.tensor_scalar(veps[:, CB * b:CB * b + CB], mv[:, CB * b:CB * b + CB, 1], 1e-5, None,
                                ALU.add).then_inc(s("veps"), 1)
            dve.wait_ge(s("xnT_ps"), 12)
            for b in range(B):
                dve.wait_ge(s("rstd"), 2 * 6 + b + 1)
                for c in range(CB * b, CB * b + CB):
                    V.tensor_scalar(xn_tm[:, c, :], xn_tm[:, c, :], mv[:, c, 0:1], rstd[:, c:c + 1],
                                    ALU.subtract, ALU.mult).then_inc(s("hn2"), 1)
            dve.wait_ge(s("fl_ps"), 1)
            lg = ps[:, 6, 0:NT * FE].rearrange("p (c e) -> p c e", e=FE)
            link(V.tensor_reduce(f1[:, :], lg, AXX, ALU.max))
            V.tensor_tensor(fsm[:, :, :], lg, f1[:, :].unsqueeze(2).broadcast_to([P, NT, FE]),
                            ALU.subtract).then_inc(s("fsub"), 1)
            dve.wait_ge(s("fexp"), 1)
            link(V.reduce_sum(f1[:, :], fsm[:, :, :], AXX))
            link(V.reciprocal(f1[:, :], f1[:, :]))
            link(V.tensor_tensor(fsm[:, :, :], fsm[:, :, :], f1[:, :].unsqueeze(2).broadcast_to([P, NT, FE]), ALU.mult))
            rank_of(fsm[:, :, :], FE, fw[:, :, :], before4, c1, c2)
            link(V.tensor_scalar(fw[:, :, :], fw[:, :, :], 1.5, None, ALU.is_lt))
            link(V.tensor_tensor(fw[:, :, :], fw[:, :, :], fsm[:, :, :], ALU.mult))
            link(V.reduce_sum(f1[:, :], fw[:, :, :], AXX))
            link(V.tensor_scalar(f1[:, :], f1[:, :], 1e-8, None, ALU.add))
            link(V.reciprocal(f1[:, :], f1[:, :]))
            link(V.tensor_tensor(fw[:, :, :], fw[:, :, :], f1[:, :].unsqueeze(2).broadcast_to([P, NT, FE]), ALU.mult))

            def f_stats(c):
                dve.wait_ge(s("f_h_ps"), c + 1)
                for e in range(FE):
                    i = V.bn_stats(fst[:, e, :], ps[:, 2 * (c % 2) + e // 2, (e % 2) * FH:(e % 2 + 1) * FH])
                link(i)
                for e in range(FE):
                    i = V.bn_aggr(fmv[:, c, e, :], fst[:, e, :])
                link(i)
                V.tensor_scalar(fve[:, c, :], fmv[:, c, :, 1], 1e-5, None, ALU.add).then_inc(s("f_ve"), 1)

            def f_shift(c):
                dve.wait_ge(s("f_rs"), c + 1)
                V.scalar_tensor_tensor(out=fnm[:, c, :], in0=fmv[:, c, :, 0], scalar=-1.0, in1=frs[:, c, :],
                                       op0=ALU.mult, op1=ALU.mult).then_inc(s("f_st"), 1)

            def f_combine(c):
                dve.wait_ge(s("f_o_ps"), c + 1)
                bank = ps[:, 6 + c % 2, :]
                link(V.tensor_scalar(otm[:, c, :], bank[:, 0:P], fw[:, c, 0:1], None, ALU.mult))
                for e in range(1, FE):
                    i = V.scalar_tensor_tensor(out=otm[:, c, :], in0=bank[:, e * P:(e + 1) * P], scalar=fw[:, c, e:e + 1],
                                               in1=otm[:, c, :], op0=ALU.mult, op1=ALU.add)
                    if e < FE - 1:
                        link(i)
                i.then_inc(s("f_cmb"), 1)

            for b in range(B):
                for j in range(CB):
                    f_stats(CB * b + j)
                    f_shift(CB * b + j)
                for j in range(CB):
                    f_combine(CB * b + j)
            for b in range(B):
                cs = range(CB * b, CB * b + CB)
                sl = slice(CB * b, CB * b + CB)
                dve.wait_ge(s("f_cmb"), CB * (b + 1))
                for c in cs:
                    i = V.bn_stats(st[:, c, :], otm[:, c, :])
                link(i)
                for c in cs:
                    i = V.bn_aggr(mv[:, c, :], st[:, c, :])
                link(i)
                V.tensor_scalar(veps[:, sl], mv[:, sl, 1], 1e-5, None, ALU.add).then_inc(s("veps"), 1)
            for b in range(B):
                sl = slice(CB * b, CB * b + CB)
                dve.wait_ge(s("rstd"), 2 * 7 + b + 1)
                for c in range(CB * b, CB * b + CB):
                    i = V.tensor_scalar(otm[:, c, :], otm[:, c, :], mv[:, c, 0:1], rstd[:, c:c + 1], ALU.subtract, ALU.mult)
                link(i)
                link(V.tensor_tensor(otm[:, sl, :], otm[:, sl, :], row("on_g").unsqueeze(1).broadcast_to([P, CB, D]), ALU.mult))
                link(V.tensor_tensor(otm[:, sl, :], otm[:, sl, :], row("on_b").unsqueeze(1).broadcast_to([P, CB, D]), ALU.add))
                V.tensor_tensor(xb[:, sl, :], otm[:, sl, :], x_tm[:, sl, :], ALU.add).then_inc(s("final"), 1)

        @block.gpsimd
        def _(pool):
            Gp = nc.gpsimd

            def inv_std(k):
                for b in range(B):
                    pool.wait_ge(s("veps"), 2 * k + b + 1)
                    sl = slice(CB * b, CB * b + CB)
                    Gp.tensor_tensor(rstd[:, sl], veps[:, sl], half[:, 0:CB], ALU.pow).then_inc(s("rstd"), 1)

            def with_bias(k, name):
                for b in range(B):
                    wait_x(pool, k, CB * b + CB - 1)
                    sl = slice(CB * b, CB * b + CB)
                    Gp.tensor_tensor(xb[:, sl, :], x_tm[:, sl, :], row(name).unsqueeze(1).broadcast_to([P, CB, D]),
                                     ALU.add).then_inc(s("xb"), 1)

            Gp.memset(half[:, :], -0.5).then_inc(s("half"), 1)
            Gp.memset(xnT[:, :, 0:1], 0.0).then_inc(s("zero"), 1)
            pool.wait_ge(s("half"), 1)
            inv_std(0)
            pool.wait_ge(s("in_ctx"), 16 * 5)
            for b in range(B):
                i = Gp.tensor_copy(ctxrep[:, b * NB * P:b * NB * P + HK].rearrange("p (h n) -> p h n", h=H),
                                   ctxT[:, b, :].unsqueeze(1).broadcast_to([P, H, NC]))
                i = Gp.memset(ctxrep[:, b * NB * P + HK:(b + 1) * NB * P], 0.0)
            i.then_inc(s("ctxrep"), 1)
            pool.wait_ge(s("in_attn"), 16 * 3)
            with_bias(0, "a_bo")
            pool.wait_ge(s("lam"), 2)
            Gp.tensor_scalar(lamr[:, :], lamr[:, :], 3.0e38, None, ALU.min).then_inc(s("lam_ok"), 1)
            Gp.tensor_scalar(lamc[:, 0:1], lamc[:, 0:1], 3.0e38, None, ALU.min).then_inc(s("lam_ok"), 1)
            pool.wait_ge(s("lam_ok"), 2)
            Gp.tensor_scalar(lamc[:, 1:2], lamc[:, 0:1], -1.0, None, ALU.mult).then_inc(s("lam_ok"), 2)

            def keys(l):
                for b in range(B):
                    i = Gp.tensor_tensor(Kbdx[:, 2 * l + b, :, :], Kx[:, l, b, :].unsqueeze(1).broadcast_to([P, H, NC]),
                                         hmask.unsqueeze(2).broadcast_to([P, H, NC]), ALU.mult)
                i.then_inc(s("kbdx"), 1)

            pool.wait_ge(s("pre"), 2)
            pool.wait_ge(s("in_first"), 16 * 3)
            keys(0)
            pool.wait_ge(s("in_ctx"), 16 * 5)
            for l in range(2):
                for b in range(B):
                    pool.wait_ge(s("pre"), 2 + 3 * (2 * l + b + 1))
                    v = Vbdx[:, 2 * l + b, :, :]
                    Gp.tensor_tensor(v[:, :, 0:P], v[:, :, 0:P], row(f"x{l}_bv").unsqueeze(1).broadcast_to([P, NB, P]),
                                     ALU.add).then_inc(s("vb"), 1)
                    Gp.tensor_copy(v[:, :, P:VW], bdx_sb[:, :, P:VW])
                    pool.wait_ge(s("vb"), 2 * l + b + 1)
                    Gp.tensor_tensor(v[:, :, 0:P], v[:, :, 0:P], bdx_sb[:, :, 0:P], ALU.mult).then_inc(s("vbdx"), 1)
            keys(1)
            Gp.tensor_tensor(Wtab[:, :, :], gapT.unsqueeze(1).broadcast_to([P, H, P]),
                             lamr[:, ::HD].unsqueeze(2).broadcast_to([P, H, P]), ALU.mult).then_inc(s("gap"), 1)
            pool.wait_ge(s("wexp"), 1)
            Gp.tensor_tensor(Wtab[:, :, :], Wtab[:, :, :], causal.unsqueeze(1).broadcast_to([P, H, P]),
                             ALU.mult).then_inc(s("wmask"), 1)
            Gp.memset(combr[:, :], 0.0).then_inc(s("zero"), 1)
            inv_std(1)
            with_bias(1, "x0_bo")
            inv_std(2)
            inv_std(3)
            pool.wait_ge(s("r_g_ps"), B)
            for c in range(NT):
                pool.wait_ge(s("r_pj"), 5 * (c // CB) + 1)
                if c >= 2:
                    pool.wait_ge(s("r_s_ps"), 4 * (c - 1))
                Gp.tensor_tensor(Rbd[:, c % 2, HV:H, :], xchunk(c, QT).unsqueeze(1).broadcast_to([P, H - HV, P]),
                                 hmask[:, HV:H].unsqueeze(2).broadcast_to([P, H - HV, P]), ALU.mult).then_inc(s("rbd_p"), 1)
            for b in range(B):
                pool.wait_ge(s("r_var"), b + 1)
                Gp.tensor_tensor(gm[:, b, :], gv[:, b, :], half[:, :], ALU.pow).then_inc(s("r_rstd"), 1)
            inv_std(4)
            with_bias(4, "x1_bo")
            inv_std(5)
            inv_std(6)
            for c in range(NT):
                pool.wait_ge(s("f_ve"), c + 1)
                Gp.tensor_tensor(frs[:, c, :], fve[:, c, :], half[:, 0:FE], ALU.pow).then_inc(s("f_rs"), 1)
            inv_std(7)


def kernel(**inputs):
    import numpy as np
    import ml_dtypes
    import concourse.bacc as bacc
    from concourse.bass_utils import run_bass_kernel_spmd

    a = {n: np.asarray(v) for n, v in inputs.items()}
    f = np.float32
    p = np.arange(P)

    def every(v):
        return np.broadcast_to(v, (P,) + v.shape)

    def side(parts):
        return np.concatenate(parts, axis=1)

    same_head = (p[:, None] // HD == p[None, :] // HD).astype(f)
    gap = np.maximum(p[None, :] - p[:, None] - 1, 0).astype(f)
    causal = (p[None, :] > p[:, None]).astype(f)
    consts = side([np.eye(P, dtype=f), np.ones((P, P), f), np.full((P, P), 1.0 / S, f), gap, causal, same_head,
                   every(np.arange(S, dtype=f))])
    before16 = (np.arange(E)[None, :] < np.arange(E)[:, None]).astype(f).reshape(-1)
    before4 = (np.arange(4)[None, :] < np.arange(4)[:, None]).astype(f).reshape(-1)
    small = side([(p[:, None] // HD == np.arange(H)[None, :]).astype(f),
                  (p[:, None] + P * np.arange(CB)[None, :]).astype(f),
                  ((p[:, None] // SLOTS == np.arange(32)[None, :] // HD) & (p[:, None] % SLOTS < TOPK)).astype(f),
                  every(before16), every(before4), every(np.arange(P, dtype=f)),
                  (p[:, None] - (P - 1)).astype(f), np.zeros((P, 1), f)])
    r = p[:, None] + P * np.arange(NB)[None, :]
    cols_v = np.arange(VW)
    bdx = ((r[:, :, None] < HK) & (r[:, :, None] // NC == np.where(cols_v < D, cols_v // HD, cols_v - D))).astype(f)
    unit = np.arange(P)
    selx = np.zeros((P, 8, P), f)
    for m in range(8):
        for part in range(3):
            selx[32 * part + 2 * m + unit // 64, m, unit] = 1
    selx = selx.reshape(P, -1).astype(ml_dtypes.bfloat16)

    A0, X0, F0, R1, X1, F1 = "L0_attn_", "L0_xattn_", "L0_ffn_", "L1_attn_", "L1_xattn_", "L1_ffn_"
    td_row = np.repeat(a[R1 + "time_decay"], HD)
    cols = np.stack([a[A0 + "bq"], a[A0 + "bk"], a[X0 + "bq"], a[X0 + "bk"], a[X1 + "b_q"], a[X1 + "b_k"],
                     a[R1 + "time_maa_k"], a[R1 + "time_maa_v"], a[R1 + "time_maa_r"], a[R1 + "time_maa_g"],
                     td_row, a[F1 + "rn_g"], a[F1 + "rn_b"]], axis=1)
    cols = side([cols, a[F1 + "ln_g"].reshape(8, P).T, a[F1 + "ln_b"].reshape(8, P).T])
    rows = every(np.concatenate([a[A0 + "bv"], a[A0 + "bo"], a[X0 + "bv"], a[X0 + "bo"], a[X1 + "b_v"], a[X1 + "b_o"],
                                 a[R1 + "ln_g"], a[R1 + "ln_b"], a[F1 + "on_g"], a[F1 + "on_b"]]))
    wa = side([a[A0 + n] for n in ("Wq", "Wk", "Wv", "Wo")])
    wb = side([a[X0 + n].T for n in ("Wq", "Wk", "Wv", "Wo")] + [a[X1 + n].T for n in ("W_q", "W_k", "W_v", "W_o")])
    wr = side([a[R1 + n].T for n in ("w_r", "w_k", "w_v", "w_g", "w_o")])
    wm = side([a[F0 + "gate_w"].reshape(-1, D).T, a[F0 + "sh_gate_w"].T, a[F0 + "up_w"].reshape(-1, D).T,
               a[F0 + "sh_up_w"].T,
               a[F0 + "down_w"].transpose(0, 2, 1).reshape(8, P, D).transpose(1, 0, 2).reshape(P, -1),
               a[F0 + "sh_down_w"].T])
    w1 = a[F1 + "w1"].transpose(1, 0, 2).reshape(D, -1)
    w2 = a[F1 + "w2"].reshape(8, P, D).transpose(1, 0, 2).reshape(P, -1)
    given = {
        "x": a["x"], "sidx": every(a[A0 + "sample_idx"]), "consts": consts, "small": small, "selx": selx, "bdx": bdx,
        "cols": cols, "rows": rows, "wa": wa, "wb": wb, "ctxt": a["ctx_1024"].transpose(2, 0, 1), "wm": wm,
        "rw": a[F0 + "router_weight"].T, "wr": wr, "tdrow": every(td_row), "urow": every(a[R1 + "time_faaaa"]),
        "w1": w1, "w2": w2, "rwf": a[F1 + "router_w"].T, "ebias": every(a[F0 + "e_bias"]),
    }
    nc = bacc.Bacc("TRN2", target_bir_lowering=False, num_devices=1)
    arrays, args = {}, []
    for n, v in given.items():
        arrays[f"{n}_dram"] = np.ascontiguousarray(v)
        args.append(nc.dram_tensor(f"{n}_dram", v.shape, mybir.dt.from_np(v.dtype), kind="ExternalInput").ap())
    args.append(nc.dram_tensor("out_dram", (B, S, D), F32, kind="ExternalOutput").ap())
    build(nc, *args)
    return run_bass_kernel_spmd(nc, [arrays], core_ids=[0]).results[0]["out_dram"]
```

```python
from contextlib import ExitStack

import concourse.bass as bass
from concourse import mybir

ALU = mybir.AluOpType
ACT = mybir.ActivationFunctionType
AXX = mybir.AxisListType.X
F32 = mybir.dt.float32
BF16 = mybir.dt.bfloat16
F32R = mybir.dt.float32r
I32 = mybir.dt.int32
U32 = mybir.dt.uint32

P = 128
D = 128
B, S = 2, 512
T = B * S
NT = T // P
CB = S // P
H, HD = 16, 8
NS = 256
TOPK = 31
SLOTS = 32
G = H // 4
NC = 77
NCP = NC + 1
HK = H * NC
NB = -(-HK // P)
LB = HK - (NB - 1) * P
VW = D + H
E, EG = 16, 4
NM = 9
FE, FH = 4, 256
NEG = -3.0e38
NHS = 7
RB = 2 * NEG / 3
ASCALE = HD ** -0.5

COLS = ["a_bq", "a_bk", "x0_bq", "x0_bk", "x1_bq", "x1_bk", "maa_k", "maa_v", "maa_r", "maa_g",
        "td", "rn_g", "rn_b", "hn_g", "hn_b"]
COL = {n: i for i, n in enumerate(COLS)}
NCOL = len(COLS) + 16
ROWS = ["a_bv", "a_bo", "x0_bv", "x0_bo", "x1_bv", "x1_bo", "on_g", "on_b"]
ROW = {n: i for i, n in enumerate(ROWS)}
WA = ["a_q", "a_k", "a_v", "a_o"]
WB = ["x0_q", "x0_k", "x0_v", "x0_o", "x1_q", "x1_k", "x1_v", "x1_o"]
WR = ["w_r", "w_k", "w_v", "w_g", "w_o"]


def build(nc, x, sidx, consts, small, selx, bdx, cols, rows, wa, wb, ctxt, wm, rw, wr, tdrow, urow, w1, w2, rwf, ebias, out):
    with ExitStack() as ctx:
        def sb(name, shape, dt=F32):
            return ctx.enter_context(nc.sbuf_tensor(name, shape, dt))

        made = {}

        def s(name):
            if name not in made:
                made[name] = ctx.enter_context(nc.semaphore(name))
            return made[name]

        ps = ctx.enter_context(nc.psum_tensor("ps", [P, 8, 512], F32))

        cst = sb("cst", [P, 6 * P + 512])
        ident, ones, inv_s = cst[:, 0:P], cst[:, P:2 * P], cst[:, 2 * P:3 * P]
        gapT, causal, bdiag = cst[:, 3 * P:4 * P], cst[:, 4 * P:5 * P], cst[:, 5 * P:6 * P]
        iota_row = cst[:, 6 * P:6 * P + 512]
        sm = sb("sm", [P, 16 + 4 + 32 + 256 + 16 + P + 2 + 4])
        hmask = sm[:, 0:16]
        iota_pc = sm[:, 16:20]
        slotmask = sm[:, 20:52]
        before16 = sm[:, 52:308].rearrange("p (a b) -> p a b", a=E)
        before4 = sm[:, 308:324].rearrange("p (a b) -> p a b", a=4)
        trow = sm[:, 324:324 + P]
        ncol = sm[:, 324 + P:325 + P]
        quad = sm[:, 326 + P:330 + P]
        colsb = sb("colsb", [P, NCOL])
        rowsb = sb("rowsb", [P, len(ROWS) * P])
        wa_sb = sb("wa_sb", [P, len(WA) * P])
        wb_sb = sb("wb_sb", [P, len(WB) * P])
        wm_sb = sb("wm_sb", [P, 3 * NM * P])
        wr_sb = sb("wr_sb", [P, len(WR) * P])
        w1_sb = wm_sb[:, 0:FE * FH]
        w2_sb = wm_sb[:, FE * FH:FE * FH + 8 * P]
        rw_sb = sb("rw_sb", [P, E + FE])
        eb_sb = sb("eb_sb", [P, E])
        ctxT = sb("ctxT", [P, B, NCP])
        tdr = sb("tdr", [P, P])
        ur = sb("ur", [P, H])
        half = sb("half", [P, 64])

        def col(n):
            return colsb[:, COL[n]:COL[n] + 1]

        def row(n):
            return rowsb[:, ROW[n] * P:(ROW[n] + 1) * P]

        def w(n):
            for names, t in ((WA, wa_sb), (WB, wb_sb), (WR, wr_sb)):
                if n in names:
                    i = names.index(n)
                    return t[:, i * P:(i + 1) * P]

        x_tm = sb("x_tm", [P, NT, D])
        xn_tm = sb("xn_tm", [P, NT, D])
        xnT = sb("xnT", [P, B, S + 1])
        KT = sb("KT", [P, B, S])
        V_tm = sb("V_tm", [P, NT, D])
        attnT = sb("attnT", [P, B, S])
        big = sb("big", [P, 8192])
        sel_sb = KT[:, 0, :].bitcast(BF16)
        QT = big[:, 7168:8192].rearrange("p (b n) -> p b n", b=B)
        aux = sb("aux", [P, 4096])
        st = sb("st", [P, NT, 6])
        mv = sb("mv", [P, NT, 2])
        veps = sb("veps", [P, NT])
        rstd = sb("rstd", [P, NT])
        Qh = sb("Qh", [P, B, S], F32R)
        Ql = sb("Ql", [P, B, S], F32R)
        Qp = sb("Qp", [P, G, T], F32R)
        bd = sb("bd", [P, 4096], F32R)
        sel4 = sb("sel4", [P, 4, G * P], F32R)
        QH, QL, KH, KL = range(4)
        terms = {QH: slice(0, 2), QL: slice(2, 4), KH: slice(0, 4, 2), KL: slice(1, 4, 2)}
        Kx = sb("Kx", [P, B * NCP])
        Kxh = sb("Kxh", [P, B * NCP], F32R)
        Kxl = sb("Kxl", [P, B * NCP], F32R)
        Kxh2 = sb("Kxh2", [P, B * NS], F32R)
        Kxl2 = sb("Kxl2", [P, B * NS], F32R)
        Kbp = sb("Kbp", [P, G, 4, B * NCP], F32R)
        Vbdx = sb("Vbdx", [P, B, NB, VW])
        ctxrep = big[:, 0:B * NB * P]
        bdx_sb = big[:, B * NB * P:B * NB * P + NB * VW].rearrange("p (n v) -> p n v", n=NB)
        Wtab = sb("Wtab", [P, H, P])
        rpow = sb("rpow", [P, P])
        kpow = sb("kpow", [P, P])
        lamr = sb("lamr", [P, P])
        lamc = sb("lamc", [P, 4])

        def xchunk(c, src):
            return src[:, c // CB, (c % CB) * P:(c % CB + 1) * P]

        def xnchunk(c):
            return xnT[:, c // CB, 1 + (c % CB) * P:1 + (c % CB + 1) * P]

        block = ctx.enter_context(nc.Block())
        x_v = x.rearrange("b (c p) d -> p (b c) d", p=P)
        out_v = out.rearrange("b (c p) d -> p (b c) d", p=P)

        bda = bd[:, :].rearrange("p (i j n) -> p i j n", i=4, j=4)
        Ksh = Kxh2[:, :].rearrange("p (b n) -> p b n", b=B)
        Ksl = Kxl2[:, :].rearrange("p (b n) -> p b n", b=B)
        OH = big[:, 0:4096].rearrange("p (c n) -> p c n", c=NT)
        OHT = big[:, 4096:8192].rearrange("p (c n) -> p c n", c=NT)
        ohs = aux[:, 0:1024].rearrange("p (c n) -> p c n", c=CB)
        xsamp = aux[:, 1024:1536].rearrange("p (b n) -> p b n", b=B)
        KsT = aux[:, 1536:2048].rearrange("p (b n) -> p b n", b=B)
        xsel = aux[:, 0:1024].rearrange("p (b n) -> p b n", b=B)
        Qbd = aux[:, 1024:2048].rearrange("p (b h n) -> p b h n", b=B, h=H)
        Pa = aux[:, 2048:3072].rearrange("p (i n) -> p i n", i=2)
        PTa = aux[:, 3072:4096].rearrange("p (i n) -> p i n", i=2)
        sidx_i = aux[:, 3072:3072 + NS].bitcast(I32)
        sidx_f = aux[:, 3072 + NS:3072 + 2 * NS]
        kbar = sb("kbar", [P, B])
        kbarbd = sb("kbarbd", [P, B, H])
        Mx = sb("Mx", [P, CB, B, H])
        MT = attnT[0:32, :, :]
        v8 = sb("v8", [32, SLOTS])
        idx = sb("idx", [32, SLOTS], U32)
        idxf = sb("idxf", [32, SLOTS])
        idxT = sb("idxT", [32, 32])
        idxcol = sb("idxcol", [P, 8])
        diag = aux[0:32, 2048:3072].rearrange("p (a n) -> p a n", a=32)
        Vmb = sb("Vmb", [P, B, D])
        Vmc = sb("Vmc", [P, B])
        nmx = sb("nmx", [P, 8])
        nb = sb("nb", [P, 8])
        rsum = sb("rsum", [P, 8])
        rinv = sb("rinv", [P, 8])
        dgt = attnT[:, 1, 0:256].rearrange("p (n d) -> p n d", n=8)
        dg = attnT[:, 1, 256:512].rearrange("p (n d) -> p n d", n=8)
        Ssb = aux[:, 0:2 * HK].rearrange("p (i n) -> p i n", i=2)
        PTx = big[:, 8192 - NHS * S:8192 - NHS * S + 2 * NB * P].rearrange("p (i n) -> p i n", i=2)
        mxx = sb("mxx", [P, 2, H])
        rsx = sb("rsx", [P, 2, H])
        atm = big[:, 7424:7936].rearrange("p (c n) -> p c n", c=4)
        sg = sb("sg", [P, NT, E])
        sc = sb("sc", [P, NT, E])
        rt = aux[:, 2048:2560].rearrange("p (c n) -> p c n", c=NT)
        masked = sb("masked", [P, NT, E + 4])
        struck = sb("struck", [P, NT, E + 4])
        top8 = sb("top8", [P, NT, 8])
        rank = sb("rank", [P, NT, E])
        den = sb("den", [P, NT])
        comb = sb("comb", [P, NT, E])
        combr = aux[:, 2560:3072].bitcast(BF16)
        cr = aux[0:E, 0:S]
        crb = sb("crb", [E, S], BF16)
        hs = big[:, 8192 - NHS * S:8192].rearrange("p (i n) -> p i n", i=NHS)
        xx = big[:, 0:1024].rearrange("p (b n) -> p b n", b=B)
        mixes = big[:, 1024:5120].rearrange("p (m b n) -> p m b n", m=4, b=B)
        Rbd = bd[:, :].rearrange("p (i g j t) -> p i g j t", i=2, g=G, j=4)
        Pr = big[:, 4096:8192].rearrange("p (i h t) -> p i h t", i=2, h=H)
        Rw = aux[:, 0:1024].rearrange("p (b n) -> p b n", b=B)
        Ktm = aux[:, 1024:2048].rearrange("p (c n) -> p c n", c=NT)
        GT = aux[:, 2048:3072].rearrange("p (b n) -> p b n", b=B)
        Vx = big[:, 0:4096].rearrange("p (i h n) -> p i h n", i=2, h=H)
        gv = big[:, 0:1024].rearrange("p (b n) -> p b n", b=B)
        gn = big[:, 1024:2048].rearrange("p (b n) -> p b n", b=B)
        gy = big[:, 2048:3072].rearrange("p (b n) -> p b n", b=B)
        RT = aux[:, 3072:4096].rearrange("p (b n) -> p b n", b=B)
        KTr = attnT
        Kh, Kl = Qh, Ql
        yc = aux[:, 3072:4096].rearrange("p (b n) -> p b n", b=B)
        St = sb("St", [P, 2, D])
        Um = sb("Um", [P, D])
        w128 = lamc[:, 2:3]
        sq = xn_tm[:, :, :].rearrange("p (b c) d -> p b (c d)", b=B)
        hn = [t.rearrange("p (c n) -> p c n", n=FE * FH) for t in
              (big[:, 0:4096], Wtab[:, :, :].rearrange("p h n -> p (h n)"),
               Vbdx[:, :, :, :].rearrange("p b n v -> p (b n v)")[:, 0:2 * FE * FH])]
        hn = [hn[0][:, c, :] for c in range(CB)] + [hn[1 + c // 2][:, c % 2, :] for c in range(CB)]
        hidT = big[:, 4096:8192].rearrange("p (k n) -> p k n", k=8)
        hnT = aux[:, 0:1024].rearrange("p (b n) -> p b n", b=B)
        otm = aux[:, 1024:2048].rearrange("p (c n) -> p c n", c=NT)
        fsm = sb("fsm", [P, NT, FE])
        fw = sb("fw", [P, NT, FE])
        f1 = sb("f1", [P, NT])
        fst = sb("fst", [P, FE, 6])
        fmv = sb("fmv", [P, NT, FE, 2])
        fve = sb("fve", [P, NT, FE])
        frs = sb("frs", [P, NT, FE])
        fnm = sb("fnm", [P, NT, FE])

        @block.sync
        def _(sp):
            for b in range(B):
                sp.dma_start(x_tm[:, b * CB:(b + 1) * CB, :], x_v[:, b * CB:(b + 1) * CB, :]).then_inc(s(f"x_in{b}"), 16)
                if b == 0:
                    sp.dma_start(cst[:, :], consts).then_inc(s("in_first"), 16)
                    sp.dma_start(sidx_i, sidx).then_inc(s("in_first"), 16)
                    sp.dma_start(sm[:, :], small).then_inc(s("in_first"), 16)
            sp.dma_start(wa_sb[:, :], wa).then_inc(s("in_attn"), 16)
            sp.dma_start(colsb[:, :], cols).then_inc(s("in_attn"), 16)
            sp.dma_start(rowsb[:, :], rows).then_inc(s("in_attn"), 16)
            sp.dma_start(ctxT[:, :, :], ctxt).then_inc(s("in_ctx"), 16)
            sp.dma_start(wb_sb[:, :], wb).then_inc(s("in_ctx"), 16)
            sp.dma_start(bdx_sb, bdx).then_inc(s("in_ctx"), 16)
            sp.dma_start(tdr[:, :], tdrow).then_inc(s("in_ctx"), 16)
            sp.dma_start(ur[:, :], urow).then_inc(s("in_ctx"), 16)
            sp.dma_start(rw_sb[:, 0:E], rw).then_inc(s("in_moe"), 16)
            sp.dma_start(eb_sb[:, :], ebias).then_inc(s("in_moe"), 16)
            sp.dma_start(wm_sb[:, :], wm).then_inc(s("in_moe"), 16)
            sp.dma_start(wr_sb[:, :], wr).then_inc(s("in_last"), 16)
            sp.dma_start(rw_sb[:, E:E + FE], rwf).then_inc(s("in_last"), 16)
            sp.wait_ge(s("x_up"), NT)
            sp.dma_start(sel_sb, selx).then_inc(s("in_sel"), 16)
            sp.dma_start(bdx_sb, bdx).then_inc(s("in_sel"), 16)
            sp.wait_ge(s("dn_ps"), B * NM)
            sp.dma_start(w1_sb, w1).then_inc(s("in_late"), 16)
            sp.dma_start(w2_sb, w2).then_inc(s("in_late"), 16)
            for b in range(B):
                sp.wait_ge(s("final"), b + 1)
                sp.dma_start(out_v[:, b * CB:(b + 1) * CB, :], otm[:, b * CB:(b + 1) * CB, :]).then_inc(s("stored"), 16)
            sp.wait_ge(s("stored"), 16 * B)

        def wait_x(eng, k, c):
            if k == 0:
                eng.wait_ge(s(f"x_in{c // CB}"), 16)
            else:
                eng.wait_ge(s("x_up"), NT * (k - 1) + c + 1)

        @block.tensor
        def _(pe):
            mm, tr = nc.tensor.matmul, nc.tensor.transpose

            def ln_transpose(k, sem="xn", out_sem="xnT_ps", bank=6):
                for b in range(B):
                    for j in range(CB):
                        pe.wait_ge(s(sem), NT * k + CB * b + j + 1)
                        i = tr(ps[:, bank + b, j * P:(j + 1) * P], xn_tm[:, CB * b + j, :], ident)
                    i.then_inc(s(out_sem), 1)

            pe.wait_ge(s("in_first"), 16 * 3)
            ln_transpose(0)
            pe.wait_ge(s("ohs"), 1)
            pe.wait_ge(s("in_attn"), 16 * 3)
            for b in range(B):
                for c in range(CB):
                    i = mm(ps[:, b, 0:NS], xn_tm[:, CB * b + c, :], ohs[:, c, :], start=(c == 0), stop=(c == CB - 1))
                i.then_inc(s("xsamp_ps"), 1)
            for b in range(B):
                pe.wait_ge(s("xsamp"), b + 1)
                mm(ps[:, 2 + b, 0:NS], w("a_k"), xsamp[:, b, :], start=True, stop=True).then_inc(s("ks_ps"), 1)
            for b in range(B):
                pe.wait_ge(s("xnT"), b + 1)
                mm(ps[:, 4 + b, :], w("a_q"), xnT[:, b, 1:S + 1], start=True, stop=True).then_inc(s("a_q_ps"), 1)
            for b in range(B):
                mm(ps[:, b, :], w("a_k"), xnT[:, b, 1:S + 1], start=True, stop=True).then_inc(s("a_k_ps"), 1)
            for b in range(B):
                pe.wait_ge(s("ks"), b + 1)
                for j in range(CB):
                    i = mm(ps[:, 2 + b, j * P:(j + 1) * P], xnchunk(CB * b + j), w("a_v"), start=True, stop=True)
                i.then_inc(s("a_v_ps"), 1)

            def pre_groups(l, banks):
                n0, nb = 9 * l, len(banks)
                mm(ps[:, banks[0], 0:B * NCP], w(f"x{l}_k"), ctxT[:, :, :].rearrange("p b n -> p (b n)"),
                   start=True, stop=True).then_inc(s("pre_ps"), 1)
                yield
                pe.wait_ge(s("ctxrep"), l + 1)
                order = [("v", r) for r in range(nb - 1)] + [("k", 0), ("k", 1)] + [("v", r) for r in range(nb - 1, 6)]
                for m, (kind, r) in enumerate(order):
                    bank = banks[(m + 1) % nb]
                    if m + 1 >= nb:
                        pe.wait_ge(s("pre"), n0 + m + 2 - nb)
                    if kind == "k":
                        pe.wait_ge(s("kx"), l + 1)
                        for v in range(2):
                            o = ps[:, bank, v * B * NCP:(v + 1) * B * NCP]
                            q = 2 * r + v
                            mm(o, sel4[:, KH, q * P:(q + 1) * P], Kxh[:, :], start=True, stop=False)
                            i = mm(o, sel4[:, KL, q * P:(q + 1) * P], Kxl[:, :], start=False, stop=True)
                    else:
                        b, q = r // 3, r % 3
                        for n in range(4 * q, min(4 * q + 4, NB)):
                            i = mm(ps[:, bank, (n - 4 * q) * P:(n - 4 * q + 1) * P],
                                   ctxrep[:, b * NB * P + n * P:b * NB * P + (n + 1) * P], w(f"x{l}_v"), start=True, stop=True)
                    i.then_inc(s("pre_ps"), 1)
                    yield

            pre = pre_groups(0, (6,))

            def a_pack(b, g):
                m = G * b + g
                if m >= 2:
                    pe.wait_ge(s("a_qp"), m - 1)
                o = ps[:, 4 + m % 2, :]
                mm(o, sel4[:, QH, g * P:(g + 1) * P], Qh[:, b, :], start=True, stop=False)
                mm(o, sel4[:, QL, g * P:(g + 1) * P], Ql[:, b, :], start=False, stop=True).then_inc(s("a_pk_ps"), 1)

            def a_keys(m):
                b, gg = m // 2, m % 2
                if m:
                    pe.wait_ge(s("a_bd"), 2 * m)
                for g in (2 * gg, 2 * gg + 1):
                    o = ps[:, 7, (g % 2) * NS:(g % 2 + 1) * NS]
                    mm(o, sel4[:, KH, g * P:(g + 1) * P], Ksh[:, b, :], start=True, stop=False)
                    i = mm(o, sel4[:, KL, g * P:(g + 1) * P], Ksl[:, b, :], start=False, stop=True)
                i.then_inc(s("a_kp_ps"), 1)

            pe.wait_ge(s("sel"), 1)
            pe.wait_ge(s("ksl"), B)
            a_keys(0)
            pe.wait_ge(s("a_ql"), B)
            pe.wait_ge(s("a_q"), 2)
            a_pack(0, 0)
            a_pack(0, 1)
            a_keys(1)
            for m in range(2, 2 * G):
                a_pack(m // G, m % G)
            pe.wait_ge(s("a_k"), 2)
            pe.wait_ge(s("a_v"), 2)
            pe.wait_ge(s("in_ctx"), 16 * 5)
            NU = B * G * CB
            for n in range(NU):
                m, j = n // CB, n % CB
                b, g = m // G, m % G
                pair = 2 * (n % 3)
                if j == 0:
                    pe.wait_ge(s("a_bd"), m + 1)
                    pe.wait_ge(s("a_qp"), m + 1)
                if n == 2:
                    pe.wait_ge(s("a_qp"), 2 * G)
                if n >= 3:
                    pe.wait_ge(s("mx"), n - 2)
                for v in range(2):
                    i = mm(ps[:, pair + v, :], Qp[:, g, b * S + j * P:b * S + (j + 1) * P],
                           bda[:, m % 4, 2 * v:2 * v + 2, :], start=True, stop=True)
                i.then_inc(s("as_ps"), 1)
                if n in (7, 13):
                    a_keys(2 + (n > 7))
                elif n > 2:
                    next(pre, None)
            for _ in pre:
                pass
            pe.wait_ge(s("a_bd"), 2 * G)
            pe.wait_ge(s("kbar"), B)
            for c in range(NT):
                i = mm(ps[:, 7, c * H:(c + 1) * H], xchunk(c, QT), kbarbd[:, c // CB, :], start=True, stop=True)
            i.then_inc(s("mean_ps"), 1)
            pe.wait_ge(s("m"), 1)
            pe.wait_ge(s("pre"), 9)
            for c in range(CB):
                i = tr(ps[0:32, 6, c * P:(c + 1) * P], Mx[:, c, :, :].rearrange("p b h -> p (b h)"), ident)
            i.then_inc(s("mT_ps"), 1)
            for b in range(B):
                for c in range(CB):
                    mm(ps[:, 2, b * P:(b + 1) * P], inv_s, V_tm[:, CB * b + c, :], start=(c == 0), stop=(c == CB - 1))
                for c in range(CB):
                    i = mm(ps[:, 2, 256 + b:257 + b], V_tm[:, CB * b + c, :], inv_s[:, 0:1], start=(c == 0),
                           stop=(c == CB - 1))
                i.then_inc(s("vm_ps"), 1)
            pe.wait_ge(s("diag"), 1)
            for b in range(B):
                mm(ps[:, b, :], ones[0:32, :], diag[:, H * b:H * (b + 1), :], start=True, stop=True).then_inc(s("ib_ps"), 1)
            pe.wait_ge(s("vm"), B)
            for b in range(B):
                pe.wait_ge(s("oh"), b + 1)
                for c in range(CB):
                    i = mm(ps[:, 2 + b, :], xn_tm[:, CB * b + c, :], OH[:, CB * b + c, :], start=(c == 0), stop=(c == CB - 1))
                i.then_inc(s("xsel_ps"), 1)
            for b in range(B):
                pe.wait_ge(s("xsel"), b + 1)
                mm(ps[:, 4 + b, :], w("a_q"), xsel[:, b, :], start=True, stop=True).then_inc(s("qs_ps"), 1)
            NG = B * G
            for n in range(NG + 3):
                if n < NG:
                    b, g = n // G, n % G
                    pe.wait_ge(s("qbd"), b + 1)
                    pe.wait_ge(s("a_exp"), n - 1) if n >= 2 else pe.wait_ge(s("oh"), B)
                    mm(ps[:, n % 2, :], Qbd[:, b, 4 * g:4 * g + 4, :].rearrange("p h n -> p (h n)"), KT[:, b, :],
                       start=True, stop=True).then_inc(s("ag_ps"), 1)
                m = n - 1
                if 0 <= m < NG:
                    b, g = m // G, m % G
                    pe.wait_ge(s("a_exp"), m + 1)
                    pe.wait_ge(s("pta"), m - 1) if m >= 2 else pe.wait_ge(s("xsel"), B)
                    for c in range(CB):
                        i = tr(ps[:, 2 + m % 2, c * P:(c + 1) * P], Pa[:, m % 2, c * P:(c + 1) * P], ident)
                    i.then_inc(s("pta_ps"), 1)
                m = n - 2
                if 0 <= m < NG:
                    b, g = m // G, m % G
                    pe.wait_ge(s("pta"), m + 1)
                    pe.wait_ge(s("dg"), m - 1) if m >= 2 else pe.wait_ge(s("qbd"), B)
                    for c in range(CB):
                        i = mm(ps[:, 4 + m % 2, 0:32], PTa[:, m % 2, c * P:(c + 1) * P],
                               V_tm[:, CB * b + c, 32 * g:32 * g + 32], start=(c == 0), stop=(c == CB - 1))
                    i.then_inc(s("pva_ps"), 1)
                m = n - 3
                if m >= 0:
                    b, g = m // G, m % G
                    pe.wait_ge(s("dg"), m + 1)
                    pe.wait_ge(s("oht"), m + 1)
                    i = mm(ps[32 * g:32 * g + 32, 6 + b, :], dg[:, m, :], OHT[:, m, :], start=True, stop=True)
                    if g == G - 1:
                        i.then_inc(s("ao_ps"), 1)
            for b in range(B):
                pe.wait_ge(s("a_at"), b + 1)
                for c in range(CB * b, CB * b + CB):
                    i = mm(ps[:, b, (c % CB) * P:(c % CB + 1) * P], xchunk(c, attnT), w("a_o"), start=True, stop=True)
                i.then_inc(s("a_op_ps"), 1)

            def context(l, k):
                L = f"x{l}"
                ln_transpose(k)
                for b in range(B):
                    pe.wait_ge(s("xnT"), 2 * k + b + 1)
                    mm(ps[:, 4 + b, :], w(f"{L}_q"), xnT[:, b, 1:S + 1], start=True, stop=True).then_inc(s("x_q_ps"), 1)
                for m in range(2 * G):
                    b, g = m // G, m % G
                    pe.wait_ge(s("x_ql"), 2 * l + b + 1)
                    if m >= G:
                        pe.wait_ge(s(("x_qp_a", "x_qp_v")[m % 2]), 4 * l + (m - G) // 2 + 1)
                    o = ps[:, m % 4, :]
                    mm(o, sel4[:, QH, g * P:(g + 1) * P], Qh[:, b, :], start=True, stop=False)
                    mm(o, sel4[:, QL, g * P:(g + 1) * P], Ql[:, b, :], start=False, stop=True).then_inc(s("x_pk_ps"), 1)
                pe.wait_ge(s("x_qp_a"), 4 * l + 4)
                pe.wait_ge(s("x_qp_v"), 4 * l + 4)
                pe.wait_ge(s("pre"), 9 * (l + 1))
                pe.wait_ge(s("vbdx"), 2 * l + 2)
                for n in range(NT + 4):
                    if n < NT:
                        for u in range(2):
                            m = 2 * n + u
                            if m >= 2:
                                pe.wait_ge(s("x_sub"), 16 * l + m - 1)
                            for v in range(2):
                                g, b = 2 * u + v, n // CB
                                i = mm(ps[:, g, 0:4 * NCP], Qp[:, g, n * P:(n + 1) * P],
                                       Kbp[:, g, :, b * NCP:(b + 1) * NCP], start=True, stop=True)
                            i.then_inc(s("x_s_ps"), 1)
                    c = n - 4
                    if c >= 0:
                        pe.wait_ge(s("x_at"), 8 * l + c + 1)
                        mm(ps[:, 6 + c % 2, 384:512], xchunk(c, attnT), w(f"{L}_o"), start=True,
                           stop=True).then_inc(s("x_op_ps"), 1)
                    c = n - 1
                    if 0 <= c < NT:
                        pe.wait_ge(s("x_exp"), 16 * l + 2 * c + 2)
                        for q in range(3):
                            r = 3 * c + q
                            if r >= 2:
                                pe.wait_ge(s("x_pt"), 24 * l + r - 1)
                            for t in range(4 * q, min(4 * q + 4, NB)):
                                wd = P if t < NB - 1 else LB
                                i = tr(ps[0:wd, 4 + r % 2, (t - 4 * q) * P:(t - 4 * q + 1) * P],
                                       Ssb[:, c % 2, t * P:t * P + wd], ident)
                            i.then_inc(s("x_pt_ps"), 1)
                    c = n - 2
                    if 0 <= c < NT:
                        pe.wait_ge(s("x_pt"), 24 * l + 3 * c + 3)
                        if c >= 2:
                            pe.wait_ge(s("x_up"), (1 + 3 * l) * NT + c - 1)
                        for t in range(NB):
                            wd = P if t < NB - 1 else LB
                            i = mm(ps[:, 6 + c % 2, 0:VW], PTx[0:wd, c % 2, t * P:(t + 1) * P],
                                   Vbdx[0:wd, c // CB, t, :], start=(t == 0), stop=(t == NB - 1))
                        i.then_inc(s("x_pv_ps"), 1)
                    c = n - 3
                    if 0 <= c < NT:
                        pe.wait_ge(s("x_atm"), 8 * l + c + 1)
                        tr(ps[:, 6 + c % 2, 256:384], atm[:, c % 4, :], ident).then_inc(s("x_at_ps"), 1)

            context(0, 1)

            pe.wait_ge(s("x_up"), 2 * NT)
            ln_transpose(2)
            pe.wait_ge(s("in_moe"), 16 * 3)
            pe.wait_ge(s("in_moe"), 16 * 3)
            for b in range(B):
                pe.wait_ge(s("xnT"), 2 * 2 + b + 1)
                for c in range(CB * b, CB * b + CB):
                    i = mm(ps[:, 4, c * E:(c + 1) * E], xnchunk(c), rw_sb[:, 0:E], start=True, stop=True)
            i.then_inc(s("rl_ps"), 1)

            def gate_up(n):
                b, i = n // NM, n % NM
                if n >= 2:
                    pe.wait_ge(s("m_h1"), n - 1)
                mm(ps[:, n % 2, :], wm_sb[:, i * P:(i + 1) * P], xnT[:, b, 1:S + 1], start=True,
                   stop=True).then_inc(s("g_ps"), 1)
                mm(ps[:, 2 + n % 2, :], wm_sb[:, (NM + i) * P:(NM + i + 1) * P], xnT[:, b, 1:S + 1], start=True,
                   stop=True).then_inc(s("u_ps"), 1)

            def expand(n):
                b, i = n // NM, n % NM
                if i < NM - 1:
                    m = b * (NM - 1) + i
                    pe.wait_ge(s("combT"), 3 * b + 3)
                    if m >= 2:
                        pe.wait_ge(s("m_h2"), m - 1)
                    mm(ps[:, 4 + m % 2, :], sel_sb[:, i * P:(i + 1) * P], combr[:, b * S:(b + 1) * S], start=True,
                       stop=True).then_inc(s("w_ps"), 1)

            def down(n):
                b, i = n // NM, n % NM
                if i < NM - 1:
                    pe.wait_ge(s("m_h2"), b * (NM - 1) + i + 1)
                else:
                    pe.wait_ge(s("m_h1"), n + 1)
                for c in range(CB):
                    r = mm(ps[:, 6 + b, c * P:(c + 1) * P], hs[:, n % NHS, c * P:(c + 1) * P],
                           wm_sb[:, (2 * NM + i) * P:(2 * NM + i + 1) * P], start=(i == 0 and c == 0),
                           stop=(i == NM - 1), skip_group_check=True)
                r.then_inc(s("dn_ps"), 1)

            NN = B * NM
            for n in range(2):
                gate_up(n)
            for _ in pre_groups(1, (5, 6, 7)):
                pass
            pe.wait_ge(s("pre"), 18)
            for b in range(B):
                pe.wait_ge(s("comb"), b + 1)
                if b == 1:
                    pe.wait_ge(s("combT"), 3)
                for c in range(CB):
                    i = tr(ps[0:E, 5, c * P:(c + 1) * P], comb[:, CB * b + c, :], ident)
                i.then_inc(s("cT_ps"), 1)
            pe.wait_ge(s("combT"), 6)
            pe.wait_ge(s("in_sel"), 16 * 2)
            for n in range(NN + 1):
                if n < NN:
                    expand(n)
                if n >= 1:
                    down(n - 1)
                if 1 <= n < NN - 1:
                    gate_up(n + 1)

            pe.wait_ge(s("x_up"), 3 * NT)
            ln_transpose(3)
            pe.wait_ge(s("in_last"), 16 * 2)
            for b in range(B):
                pe.wait_ge(s("mix"), 4 * b + 4)
                if b == 1:
                    pe.wait_ge(s("r_pj"), 1)
                    pe.wait_ge(s("r_g"), 1)
                    pe.wait_ge(s("r_kv"), 3)
                mk, mv_, mr, mg = (mixes[:, i, b, :] for i in range(4))
                mm(ps[:, 0, :], w("w_r"), mr, start=True, stop=True).then_inc(s("r_pj_ps"), 1)
                mm(ps[:, 1, :], w("w_k"), mk, start=True, stop=True).then_inc(s("r_pj_ps"), 1)
                for j in range(CB):
                    i = mm(ps[:, 2, j * P:(j + 1) * P], mk[:, j * P:(j + 1) * P], w("w_k"), start=True, stop=True)
                i.then_inc(s("r_pj_ps"), 1)
                for j in range(CB):
                    i = mm(ps[:, 3, j * P:(j + 1) * P], mv_[:, j * P:(j + 1) * P], w("w_v"), start=True, stop=True)
                i.then_inc(s("r_pj_ps"), 1)
                mm(ps[:, 4, :], w("w_g"), mg, start=True, stop=True).then_inc(s("r_pj_ps"), 1)

            def r_pack(m):
                b, g = m // G, m % G
                if m >= 2:
                    pe.wait_ge(s("r_kp"), m - 1)
                o = ps[:, 2 + m % 2, :]
                mm(o, sel4[:, KH, g * P:(g + 1) * P], Kh[:, b, :], start=True, stop=False)
                mm(o, sel4[:, KL, g * P:(g + 1) * P], Kl[:, b, :], start=False, stop=True).then_inc(s("r_pk_ps"), 1)

            def r_rows(c):
                pe.wait_ge(s("r_rl"), B)
                if c:
                    pe.wait_ge(s("rbd"), c)
                for g in range(G):
                    o = ps[:, 4, g * P:(g + 1) * P]
                    mm(o, sel4[:, QH, g * P:(g + 1) * P], xchunk(c, Qh), start=True, stop=False)
                    i = mm(o, sel4[:, QL, g * P:(g + 1) * P], xchunk(c, Ql), start=False, stop=True)
                i.then_inc(s("r_rows_ps"), 1)

            def r_scores(c):
                pe.wait_ge(s("rbd"), c + 1)
                for q in range(4):
                    if c >= 1:
                        pe.wait_ge(s("r_p"), 4 * (c - 1) + q + 1)
                    mm(ps[:, q, :], Qp[:, q, c * P:(c + 1) * P], Rbd[:, c % 2, q, :, :], start=True,
                       stop=True).then_inc(s("r_s_ps"), 1)
                if c % CB < CB - 1:
                    if c >= 1:
                        pe.wait_ge(s("um"), c - c // CB)
                    mm(ps[:, 5, 0:P], Ktm[:, c, :], V_tm[:, c, :], start=True, stop=True).then_inc(s("u_st_ps"), 1)

            def r_out(c):
                b, j = c // CB, c % CB
                y = ps[:, 6 + b, j * P:(j + 1) * P]
                if j:
                    pe.wait_ge(s("state"), b * (CB - 1) + j)
                    mm(y, St[:, (b * (CB - 1) + j - 1) % 2, :], xchunk(c, Rw), start=False, stop=False, skip_group_check=True)
                pe.wait_ge(s("vx"), c + 1)
                for h in range(H):
                    if h % 4 == 0:
                        pe.wait_ge(s("r_p"), 4 * c + h // 4 + 1)
                    i = mm(y, Vx[:, c % 2, h, :], Pr[:, c % 2, h, :], start=(j == 0 and h == 0), stop=(h == H - 1),
                           skip_group_check=True)
                i.then_inc(s("y_ps"), 1)

            pe.wait_ge(s("r_pj"), 2)
            pe.wait_ge(s("r_g"), 2)
            pe.wait_ge(s("r_kv"), 3 * B)
            pe.wait_ge(s("xnT"), 8)
            for m in range(2 * G):
                r_pack(m)
            pe.wait_ge(s("r_kp"), 2 * G)
            r_rows(0)
            for c in range(NT + 1):
                if c < NT:
                    r_scores(c)
                if c + 1 < NT:
                    r_rows(c + 1)
                if c >= 1:
                    r_out(c - 1)
            for b in range(B):
                pe.wait_ge(s("r_y"), b + 1)
                mm(ps[:, b, :], bdiag, yc[:, b, :], start=True, stop=True).then_inc(s("r_mean_ps"), 1)
            for b in range(B):
                pe.wait_ge(s("r_sq"), b + 1)
                mm(ps[:, 2 + b, :], bdiag, sq[:, b, :], start=True, stop=True).then_inc(s("r_var_ps"), 1)
            for b in range(B):
                pe.wait_ge(s("r_yg"), b + 1)
                for c in range(CB * b, CB * b + CB):
                    i = mm(ps[:, 4 + b, (c % CB) * P:(c % CB + 1) * P], xchunk(c, yc), w("w_o"), start=True, stop=True)
                i.then_inc(s("r_op_ps"), 1)

            context(1, 4)

            pe.wait_ge(s("x_up"), 5 * NT)
            ln_transpose(5)
            pe.wait_ge(s("in_late"), 16 * 2)
            pe.wait_ge(s("xnT"), 12)

            def f_hidden(c):
                if c >= 2:
                    pe.wait_ge(s("f_hn"), 3 * (c - 1))
                    pe.wait_ge(s("f_hv"), c - 1)
                for v in range(2):
                    i = mm(ps[:, 2 * (c % 2) + v, :], xnchunk(c), w1_sb[:, v * 512:(v + 1) * 512], start=True, stop=True)
                i.then_inc(s("f_h_ps"), 1)

            def f_turn(b, qs):
                pe.wait_ge(s("f_hn"), 3 * CB * (b + 1))
                pe.wait_ge(s("f_hv"), CB * (b + 1))
                for q in qs:
                    r = 8 * b + q
                    if r >= 2:
                        pe.wait_ge(s("f_hT"), r - 1)
                    for j in range(CB):
                        i = tr(ps[:, 4 + r % 2, j * P:(j + 1) * P], hn[CB * b + j][:, q * P:(q + 1) * P], ident)
                    i.then_inc(s("f_hT_ps"), 1)

            def f_down(b):
                pe.wait_ge(s("f_hT"), 8 * (b + 1))
                for j in range(CB):
                    c = CB * b + j
                    if c == 0:
                        pe.wait_ge(s("fsub"), 1)
                    if c >= 2:
                        pe.wait_ge(s("f_cmb"), c - 1)
                    for e in range(FE):
                        for v in range(2):
                            i = mm(ps[:, 6 + c % 2, e * P:(e + 1) * P], hidT[:, 2 * e + v, j * P:(j + 1) * P],
                                   w2_sb[:, (2 * e + v) * P:(2 * e + v + 1) * P], start=(v == 0), stop=(v == 1))
                    i.then_inc(s("f_o_ps"), 1)

            f_hidden(0)
            f_hidden(1)
            ln_transpose(0, sem="hn2", out_sem="hnT_ps", bank=4)
            pe.wait_ge(s("in_last"), 16 * 2)
            pe.wait_ge(s("hnT"), 2)
            for c in range(NT):
                i = mm(ps[:, 6, c * FE:(c + 1) * FE], hnT[:, c // CB, (c % CB) * P:(c % CB + 1) * P],
                       rw_sb[:, E:E + FE], start=True, stop=True)
            i.then_inc(s("fl_ps"), 1)
            f_hidden(2)
            f_hidden(3)
            for j in range(0, CB, 2):
                f_hidden(CB + j)
                f_hidden(CB + j + 1)
                f_turn(0, range(2 * j, 2 * j + 4))
            f_down(0)
            f_turn(1, range(8))
            f_down(1)

        @block.scalar
        def _(act):
            A = nc.scalar.activation
            act.wait_ge(s("in_attn"), 16 * 3)

            def ln_copy(k):
                for b in range(B):
                    if k == 0 and b == 0:
                        act.wait_ge(s("filled"), 2)
                    act.wait_ge(s("xnT_ps"), 2 * k + b + 1)
                    A(xnT[:, b, 1:S + 1], ps[:, 6 + b, :], ACT.Copy).then_inc(s("xnT"), 1)

            ln_copy(0)
            for b in range(B):
                act.wait_ge(s("xsamp_ps"), b + 1)
                A(xsamp[:, b, :], ps[:, b, 0:NS], ACT.Copy).then_inc(s("xsamp"), 1)
            for b in range(B):
                act.wait_ge(s("ks_ps"), b + 1)
                A(KsT[:, b, :], ps[:, 2 + b, 0:NS], ACT.Identity, bias=col("a_bk")).then_inc(s("ks"), 1)
            for b in range(B):
                act.wait_ge(s("ks"), b + 1)
                A(Ksh[:, b, :], KsT[:, b, :], ACT.Copy).then_inc(s("ksh"), 1)
            for b in range(B):
                act.wait_ge(s("a_q_ps"), b + 1)
                A(QT[:, b, :], ps[:, 4 + b, :], ACT.Identity, bias=col("a_bq")).then_inc(s("a_q"), 1)
                act.wait_ge(s("a_q"), b + 1)
                A(Qh[:, b, :], QT[:, b, :], ACT.Copy).then_inc(s("a_qh"), 1)
            act.wait_ge(s("in_first"), 16 * 3)

            def key_blocks(m):
                act.wait_ge(s("a_kp_ps"), m + 1)
                for v in range(2):
                    u = 2 * m + v
                    if u >= 4:
                        act.wait_ge(s("as_ps"), CB * (u - 3))
                    for j in range(4):
                        i = A(bda[:, u % 4, j, :], ps[:, 7, v * NS:(v + 1) * NS], ACT.Copy, scale=quad[:, j:j + 1])
                    i.then_inc(s("a_bd"), 1)

            def query_rows(m):
                act.wait_ge(s("a_pk_ps"), m + 1)
                A(Qp[:, m % G, (m // G) * S:(m // G + 1) * S], ps[:, 4 + m % 2, :], ACT.Copy).then_inc(s("a_qp"), 1)

            key_blocks(0)
            query_rows(0)
            query_rows(1)
            for b in range(B):
                act.wait_ge(s("a_k_ps"), b + 1)
                A(KT[:, b, :], ps[:, b, :], ACT.Identity, bias=col("a_bk")).then_inc(s("a_k"), 1)
            for m in range(2, 2 * G):
                query_rows(m)
            key_blocks(1)
            act.wait_ge(s("in_ctx"), 16 * 5)
            A(lamr[:, :], tdr[:, :], ACT.Exp).then_inc(s("lam"), 1)
            A(lamc[:, 0:1], col("td"), ACT.Exp).then_inc(s("lam"), 1)

            def pre_copies(l, banks):
                n0, nb = 9 * l, len(banks)
                act.wait_ge(s("pre_ps"), n0 + 1)
                A(Kx[:, :], ps[:, banks[0], 0:B * NCP], ACT.Identity, bias=col(f"x{l}_bk")).then_inc(s("pre"), 1)
                yield
                order = [("v", r) for r in range(nb - 1)] + [("k", 0), ("k", 1)] + [("v", r) for r in range(nb - 1, 6)]
                for m, (kind, r) in enumerate(order):
                    bank = banks[(m + 1) % nb]
                    act.wait_ge(s("pre_ps"), n0 + m + 2)
                    if kind == "k":
                        for j in range(4):
                            i = A(Kbp[:, 2 * r:2 * r + 2, j, :], ps[:, bank, 0:2 * B * NCP].rearrange("p (g n) -> p g n", g=2),
                                  ACT.Copy, scale=quad[:, j:j + 1])
                    else:
                        b, q = r // 3, r % 3
                        n = min(4, NB - 4 * q)
                        i = A(Vbdx[:, b, 4 * q:4 * q + n, 0:P],
                              ps[:, bank, 0:n * P].rearrange("p (n d) -> p n d", d=P), ACT.Copy)
                    i.then_inc(s("pre"), 1)
                    yield

            pre = pre_copies(0, (6,))
            for _ in range(4):
                next(pre)
            key_blocks(2)
            for _ in pre:
                pass
            key_blocks(3)
            act.wait_ge(s("lam_ok"), 4)
            A(rpow[:, :], trow, ACT.Exp, scale=lamc[:, 1:2]).then_inc(s("tabs"), 1)
            A(kpow[:, :], lamr[:, :], ACT.Exp, scale=ncol).then_inc(s("tabs"), 1)
            A(w128, lamc[:, 1:2], ACT.Exp, scale=float(P)).then_inc(s("tabs"), 1)
            act.wait_ge(s("gap"), 1)
            A(Wtab[:, :, :], Wtab[:, :, :], ACT.Exp, scale=-1.0).then_inc(s("wexp"), 1)
            act.wait_ge(s("mT_ps"), 1)
            A(MT[:, 0, :], ps[0:32, 6, :], ACT.Copy).then_inc(s("mT"), 1)
            act.wait_ge(s("vm_ps"), B)
            A(Vmb[:, :, :].rearrange("p b d -> p (b d)"), ps[:, 2, 0:2 * P], ACT.Copy).then_inc(s("vm"), 1)
            A(Vmc[:, :], ps[:, 2, 256:256 + B], ACT.Copy).then_inc(s("vm"), 1)
            for b in range(B):
                act.wait_ge(s("xsel_ps"), b + 1)
                A(xsel[:, b, :], ps[:, 2 + b, :], ACT.Copy).then_inc(s("xsel"), 1)
            for n in range(B * G + 1):
                if n < B * G:
                    act.wait_ge(s("nb"), n + 1)
                    if n >= 2:
                        act.wait_ge(s("pta_ps"), n - 1)
                    A(Pa[:, n % 2, :], ps[:, n % 2, :], ACT.Exp, bias=nb[:, n:n + 1], scale=ASCALE,
                      accum_out=rsum[:, n:n + 1]).then_inc(s("a_exp"), 1)
                m = n - 1
                if m >= 0:
                    act.wait_ge(s("pta_ps"), m + 1)
                    if m >= 2:
                        act.wait_ge(s("pva_ps"), m - 1)
                    A(PTa[:, m % 2, :], ps[:, 2 + m % 2, :], ACT.Copy).then_inc(s("pta"), 1)
            for b in range(B):
                act.wait_ge(s("ao_ps"), b + 1)
                A(attnT[:, b, :], ps[:, 6 + b, :], ACT.Identity, bias=Vmc[:, b:b + 1]).then_inc(s("a_at"), 1)

            def context(l, k):
                L = f"x{l}"
                ln_copy(k)
                for b in range(B):
                    act.wait_ge(s("x_q_ps"), 2 * l + b + 1)
                    A(Qh[:, b, :], ps[:, 4 + b, :], ACT.Identity, bias=col(f"{L}_bq")).then_inc(s("x_qh"), 1)
                for m in range(0, 2 * G, 2):
                    act.wait_ge(s("x_pk_ps"), 8 * l + m + 1)
                    A(Qp[:, m % G, (m // G) * S:(m // G + 1) * S], ps[:, m % 4, :], ACT.Copy).then_inc(s("x_qp_a"), 1)
                for n in range(NT + 3):
                    c = n - 1
                    if 0 <= c < NT:
                        for q in range(3):
                            r = 3 * c + q
                            act.wait_ge(s("x_pt_ps"), 24 * l + r + 1)
                            if c >= 2 and q == 0:
                                act.wait_ge(s("x_pv_ps"), 8 * l + c - 1)
                            t0, t1 = 4 * q, min(4 * q + 4, NB)
                            if q < 2:
                                A(PTx[:, c % 2, t0 * P:t1 * P], ps[:, 4 + r % 2, :], ACT.Copy).then_inc(s("x_pt"), 1)
                            else:
                                A(PTx[:, c % 2, t0 * P:(t1 - 1) * P], ps[:, 4 + r % 2, 0:P], ACT.Copy)
                                A(PTx[0:LB, c % 2, (t1 - 1) * P:t1 * P], ps[0:LB, 4 + r % 2, P:2 * P],
                                  ACT.Copy).then_inc(s("x_pt"), 1)
                    if n < NT:
                        for u in range(2):
                            act.wait_ge(s("x_sub"), 16 * l + 2 * n + u + 1)
                            v = Ssb[:, n % 2, u * 8 * NC:(u + 1) * 8 * NC]
                            A(v, v, ACT.Exp, scale=ASCALE).then_inc(s("x_exp"), 1)
                    c = n - 3
                    if c >= 0:
                        act.wait_ge(s("x_at_ps"), 8 * l + c + 1)
                        A(xchunk(c, attnT), ps[:, 6 + c % 2, 256:384], ACT.Copy).then_inc(s("x_at"), 1)

            context(0, 1)

            ln_copy(2)
            act.wait_ge(s("rl_ps"), 1)
            A(sg[:, :, :].rearrange("p c e -> p (c e)"), ps[:, 4, 0:NT * E], ACT.Exp, scale=-1.0).then_inc(s("m_en"), 1)

            for _ in pre_copies(1, (5, 6, 7)):
                pass

            def silu(n):
                act.wait_ge(s("g_ps"), n + 1)
                if n >= NHS:
                    act.wait_ge(s("dn_ps"), n - NHS + 1)
                A(hs[:, n % NHS, :], ps[:, n % 2, :], ACT.Silu).then_inc(s("m_silu"), 1)

            for n in range(B * NM):
                silu(n)

            ln_copy(3)
            for b in range(B):
                act.wait_ge(s("r_pj_ps"), 5 * b + 1)
                A(RT[:, b, :], ps[:, 0, :], ACT.Copy).then_inc(s("r_pj"), 1)
                act.wait_ge(s("r_pj_ps"), 5 * b + 2)
                A(Kh[:, b, :], ps[:, 1, :], ACT.Copy).then_inc(s("r_kh"), 1)
                act.wait_ge(s("r_pj_ps"), 5 * b + 5)
                A(GT[:, b, :], ps[:, 4, :], ACT.Silu).then_inc(s("r_g"), 1)
            for m in range(2 * G):
                act.wait_ge(s("r_pk_ps"), m + 1)
                A(Qp[:, m % G, (m // G) * S:(m // G + 1) * S], ps[:, 2 + m % 2, :], ACT.Copy).then_inc(s("r_kp"), 1)
            act.wait_ge(s("r_pj"), B)
            for b in range(B):
                A(Qh[:, b, :], RT[:, b, :], ACT.Copy).then_inc(s("r_rh"), 1)
            for c in range(NT):
                act.wait_ge(s("r_rows_ps"), c + 1)
                if c >= 2:
                    act.wait_ge(s("r_s_ps"), 4 * (c - 1))
                for j in range(4):
                    i = A(Rbd[:, c % 2, :, j, :], ps[:, 4, :].rearrange("p (g t) -> p g t", g=G), ACT.Copy,
                          scale=quad[:, j:j + 1])
                i.then_inc(s("rbd"), 1)
            for b in range(B):
                act.wait_ge(s("y_ps"), CB * (b + 1))
                A(yc[:, b, :], ps[:, 6 + b, :], ACT.Copy).then_inc(s("r_y"), 1)
            for b in range(B):
                act.wait_ge(s("r_yc"), b + 1)
                A(sq[:, b, :], yc[:, b, :], ACT.Square).then_inc(s("r_sq"), 1)
            for b in range(B):
                act.wait_ge(s("r_var"), b + 1)
                A(gn[:, b, :], gv[:, b, :], ACT.Sqrt).then_inc(s("r_sd"), 1)

            context(1, 4)

            ln_copy(5)
            for b in range(B):
                act.wait_ge(s("hnT_ps"), b + 1)
                A(hnT[:, b, :], ps[:, 4 + b, :], ACT.Identity, scale=col("rn_g"), bias=col("rn_b")).then_inc(s("hnT"), 1)

            def f_norm(c):
                act.wait_ge(s("f_st"), c + 1)
                for e in range(FE - 1):
                    if e == 2:
                        act.wait_ge(s("f_hv"), c + 1)
                    A(hn[c][:, e * FH:(e + 1) * FH], ps[:, 2 * (c % 2) + e // 2, (e % 2) * FH:(e % 2 + 1) * FH],
                      ACT.Identity, scale=frs[:, c, e:e + 1], bias=fnm[:, c, e:e + 1]).then_inc(s("f_hn"), 1)

            def f_relu(b, q):
                act.wait_ge(s("f_hT_ps"), 8 * b + q + 1)
                if b == 1 and q == 0:
                    act.wait_ge(s("f_o_ps"), CB)
                A(hidT[:, q, :], ps[:, 4 + (8 * b + q) % 2, :], ACT.Relu, scale=colsb[:, len(COLS) + q:len(COLS) + q + 1],
                  bias=colsb[:, len(COLS) + 8 + q:len(COLS) + 9 + q]).then_inc(s("f_hT"), 1)

            f_norm(0)
            f_norm(1)
            act.wait_ge(s("fsub"), 1)
            A(fsm[:, :, :], fsm[:, :, :], ACT.Exp).then_inc(s("fexp"), 1)
            f_norm(2)
            f_norm(3)
            for j in range(CB):
                f_relu(0, 2 * j)
                f_relu(0, 2 * j + 1)
                f_norm(CB + j)
            for q in range(8):
                f_relu(1, q)

        @block.vector
        def _(dve):
            V = nc.vector
            chain = [0]

            def link(ins):
                chain[0] += 1
                ins.then_inc(s("dve_chain"), 1)
                dve.wait_ge(s("dve_chain"), chain[0])

            def layernorm(k):
                for b in range(B):
                    cs = range(CB * b, CB * b + CB)
                    for c in cs:
                        wait_x(dve, k, c)
                        i = V.bn_stats(st[:, c, :], x_tm[:, c, :])
                    link(i)
                    for c in cs:
                        i = V.bn_aggr(mv[:, c, :], st[:, c, :])
                    link(i)
                    V.tensor_scalar(veps[:, CB * b:CB * b + CB], mv[:, CB * b:CB * b + CB, 1], 1e-5, None,
                                    ALU.add).then_inc(s("veps"), 1)
                for b in range(B):
                    dve.wait_ge(s("rstd"), 2 * k + b + 1)
                    for c in range(CB * b, CB * b + CB):
                        V.tensor_scalar(xn_tm[:, c, :], x_tm[:, c, :], mv[:, c, 0:1], rstd[:, c:c + 1],
                                        ALU.subtract, ALU.mult).then_inc(s("xn"), 1)

            def add_residual(bank, b, sem, ops):
                dve.wait_ge(s(ops), b + 1)
                cs = slice(CB * b, CB * b + CB)
                V.tensor_tensor(x_tm[:, cs, :], ps[:, bank, :].rearrange("p (c d) -> p c d", c=CB), x_tm[:, cs, :],
                                ALU.add).then_inc(s(sem), CB)

            dve.wait_ge(s("in_first"), 16 * 3)
            dve.wait_ge(s("in_first"), 16 * 3)
            link(V.tensor_copy(sidx_f, sidx_i))
            for c in range(CB):
                i = V.tensor_scalar(ohs[:, c, :], sidx_f, iota_pc[:, c:c + 1], None, ALU.is_equal)
            i.then_inc(s("ohs"), 1)
            layernorm(0)
            for b in range(B):
                dve.wait_ge(s("ksh"), b + 1)
                V.tensor_tensor(Ksl[:, b, :], KsT[:, b, :], Ksh[:, b, :].bitcast(F32), ALU.subtract).then_inc(s("ksl"), 1)
            for b in range(B):
                dve.wait_ge(s("a_qh"), b + 1)
                V.tensor_tensor(Ql[:, b, :], QT[:, b, :], Qh[:, b, :].bitcast(F32), ALU.subtract).then_inc(s("a_ql"), 1)
            dve.wait_ge(s("in_attn"), 16 * 3)
            for b in range(B):
                dve.wait_ge(s("a_v_ps"), b + 1)
                V.tensor_tensor(V_tm[:, CB * b:CB * b + CB, :], ps[:, 2 + b, :].rearrange("p (c d) -> p c d", c=CB),
                                row("a_bv").unsqueeze(1).broadcast_to([P, CB, D]), ALU.add).then_inc(s("a_v"), 1)
            for b in range(B):
                link(V.reduce_sum(kbar[:, b:b + 1], KsT[:, b, :], AXX))
                V.tensor_scalar(kbarbd[:, b, :], hmask, kbar[:, b:b + 1], 1.0 / NS, ALU.mult, ALU.mult).then_inc(s("kbar"), 1)
            for n in range(B * G * CB):
                m, j = n // CB, n % CB
                b, g = m // G, m % G
                pair = 2 * (n % 3)
                dve.wait_ge(s("as_ps"), n + 1)
                V.tensor_reduce(Mx[:, j, b, 4 * g:4 * g + 4],
                                ps[:, pair:pair + 2, :].rearrange("p v (h n) -> p (v h) n", n=NS),
                                AXX, ALU.max).then_inc(s("mx"), 1)
            dve.wait_ge(s("mx"), 4 * NT)
            dve.wait_ge(s("mean_ps"), 1)
            V.tensor_tensor(Mx[:, :, :, :], Mx[:, :, :, :],
                            ps[:, 7, 0:NT * H].rearrange("p (b c h) -> p c b h", b=B, c=CB), ALU.subtract).then_inc(s("m"), 1)
            dve.wait_ge(s("mT"), 1)
            for r in range(4):
                cur, nxt = MT[:, r % 2, :], MT[:, 1 - r % 2, :]
                v = v8[:, 8 * r:8 * r + 8]
                link(V.max(v, cur))
                link(V.max_index(idx[:, 8 * r:8 * r + 8], v, cur))
                if r < 3:
                    link(V.match_replace(nxt, v, cur, NEG))
            link(V.tensor_copy(idxf[:, :], idx[:, :]))
            V.tensor_tensor(diag[:, :, :], idxf[:, :].unsqueeze(1).broadcast_to([32, 32, SLOTS]),
                            ident[0:32, 0:32].unsqueeze(2).broadcast_to([32, 32, SLOTS]), ALU.mult).then_inc(s("diag"), 1)
            link(V.transpose(idxT[:, :], idxf[:, :]))
            for j in range(4):
                i = V.tensor_copy(idxcol[32 * j:32 * j + 32, :], idxT[:, j::4])
            link(i)
            for b in range(B):
                dve.wait_ge(s("ib_ps"), b + 1)
                dve.wait_ge(s("vbdx"), B)
                for c in range(CB):
                    i = V.tensor_scalar(OH[:, CB * b + c, :], ps[:, b, :], iota_pc[:, c:c + 1], None, ALU.is_equal)
                i.then_inc(s("oh"), 1)
            for b in range(B):
                dve.wait_ge(s("qs_ps"), b + 1)
                V.scalar_tensor_tensor(out=Qbd[:, b, :, :], in0=ps[:, 4 + b, :].rearrange("p (h n) -> p h n", h=H),
                                       scalar=col("a_bq"), in1=hmask.unsqueeze(2).broadcast_to([P, H, SLOTS]),
                                       op0=ALU.add, op1=ALU.mult).then_inc(s("qbd"), 1)

            def place(n):
                V.tensor_scalar(OHT[:, n, :], iota_row, idxcol[:, n:n + 1], None, ALU.is_equal).then_inc(s("oht"), 1)

            place(0)
            place(1)
            for n in range(B * G + 2):
                if n < B * G:
                    dve.wait_ge(s("ag_ps"), n + 1)
                    link(V.tensor_reduce(nmx[:, n:n + 1], ps[:, n % 2, :], AXX, ALU.max))
                    V.tensor_scalar(nb[:, n:n + 1], nmx[:, n:n + 1], -ASCALE, None, ALU.mult).then_inc(s("nb"), 1)
                if n + 2 < B * G:
                    place(n + 2)
                m = n - 2
                if m >= 0:
                    b, g = m // G, m % G
                    dve.wait_ge(s("a_exp"), m + 1)
                    link(V.reciprocal(rinv[:, m:m + 1], rsum[:, m:m + 1]))
                    dve.wait_ge(s("pva_ps"), m + 1)
                    dve.wait_ge(s("vm"), B)
                    link(V.scalar_tensor_tensor(out=dgt[:, m, :], in0=ps[:, 4 + m % 2, 0:32], scalar=rinv[:, m:m + 1],
                                                in1=Vmb[:, b, 32 * g:32 * g + 32], op0=ALU.mult, op1=ALU.subtract))
                    V.tensor_tensor(dg[:, m, :], dgt[:, m, :], slotmask, ALU.mult).then_inc(s("dg"), 1)
            for b in range(B):
                dve.wait_ge(s("xb"), b + 1)
                add_residual(b, b, "x_up", "a_op_ps")

            def context(l, k, xbk):
                L = f"x{l}"
                layernorm(k)
                for b in range(B):
                    dve.wait_ge(s("x_qh"), 2 * l + b + 1)
                    V.scalar_tensor_tensor(out=Ql[:, b, :], in0=ps[:, 4 + b, :], scalar=col(f"{L}_bq"), in1=Qh[:, b, :].bitcast(F32),
                                           op0=ALU.add, op1=ALU.subtract).then_inc(s("x_ql"), 1)
                for m in range(1, 2 * G, 2):
                    dve.wait_ge(s("x_pk_ps"), 8 * l + m + 1)
                    V.tensor_copy(Qp[:, m % G, (m // G) * S:(m // G + 1) * S], ps[:, m % 4, :]).then_inc(s("x_qp_v"), 1)
                for n in range(NT + 4):
                    if n < NT:
                        for u in range(2):
                            dve.wait_ge(s("x_s_ps"), 16 * l + 2 * n + u + 1)
                            src = ps[:, 2 * u:2 * u + 2, 0:4 * NCP].rearrange("p v (h n) -> p v h n", n=NCP)[:, :, :, 0:NC]
                            m8 = mxx[:, n % 2, 8 * u:8 * u + 8]
                            link(V.tensor_reduce(m8.rearrange("p (v h) -> p v h", v=2), src, AXX, ALU.max))
                            if n >= 2 and u == 0:
                                dve.wait_ge(s("x_pt_ps"), 24 * l + 3 * (n - 1))
                            V.tensor_tensor(Ssb[:, n % 2, u * 8 * NC:(u + 1) * 8 * NC].rearrange("p (v h n) -> p v h n", v=2, h=4),
                                            src, m8.rearrange("p (v h) -> p v h", v=2).unsqueeze(3).broadcast_to([P, 2, 4, NC]),
                                            ALU.subtract).then_inc(s("x_sub"), 1)
                    c = n - 4
                    if c >= 0:
                        dve.wait_ge(s("x_op_ps"), 8 * l + c + 1)
                        dve.wait_ge(s("xb"), xbk + c // CB + 1)
                        V.tensor_tensor(x_tm[:, c, :], ps[:, 6 + c % 2, 384:512], x_tm[:, c, :], ALU.add).then_inc(s("x_up"), 1)
                    c = n - 2
                    if 0 <= c < NT:
                        dve.wait_ge(s("x_pv_ps"), 8 * l + c + 1)
                        bank = ps[:, 6 + c % 2, :]
                        link(V.tensor_scalar(rsx[:, 0, :], bank[:, D:VW], 1e-9 if l == 0 else 0.0, None, ALU.add))
                        link(V.reciprocal(rsx[:, 1, :], rsx[:, 0, :]))
                        V.tensor_tensor(atm[:, c % 4, :].rearrange("p (h d) -> p h d", h=H),
                                        bank[:, 0:D].rearrange("p (h d) -> p h d", h=H),
                                        rsx[:, 1, :].unsqueeze(2).broadcast_to([P, H, HD]), ALU.mult).then_inc(s("x_atm"), 1)

            context(0, 1, 2)

            layernorm(2)
            dve.wait_ge(s("wmask"), 1)
            dve.wait_ge(s("in_ctx"), 16 * 5)
            for h in range(H):
                V.scalar_tensor_tensor(out=Wtab[:, h, :], in0=ident, scalar=ur[:, h:h + 1], in1=Wtab[:, h, :],
                                       op0=ALU.mult, op1=ALU.add)
            dve.wait_ge(s("m_en"), 1)
            dve.wait_ge(s("in_moe"), 16 * 3)
            link(V.tensor_scalar(sg[:, :, :], sg[:, :, :], 1.0, None, ALU.add))
            link(V.reciprocal(sg[:, :, :], sg[:, :, :]))
            link(V.tensor_tensor(sc[:, :, :], sg[:, :, :], eb_sb[:, :].unsqueeze(1).broadcast_to([P, NT, E]), ALU.add))
            s4 = sc[:, :, :].rearrange("p c (g e) -> p c g e", g=EG)

            def r4(i):
                return rt[:, :, 4 * i:4 * i + 4]

            V.tensor_tensor(r4(0), s4[:, :, :, 0], s4[:, :, :, 1], ALU.max)
            V.tensor_tensor(r4(1), s4[:, :, :, 0], s4[:, :, :, 1], ALU.min)
            V.tensor_tensor(r4(2), s4[:, :, :, 2], s4[:, :, :, 3], ALU.max)
            link(V.tensor_tensor(r4(3), s4[:, :, :, 2], s4[:, :, :, 3], ALU.min))
            V.tensor_tensor(r4(4), r4(0), r4(2), ALU.max)
            V.tensor_tensor(r4(5), r4(0), r4(2), ALU.min)
            link(V.tensor_tensor(r4(6), r4(1), r4(3), ALU.max))
            link(V.tensor_tensor(r4(5), r4(5), r4(6), ALU.max))
            link(V.tensor_tensor(r4(7), r4(4), r4(5), ALU.add))

            def rank_of(vals, cnt, dst, before, t1, t2):
                me = vals.unsqueeze(3).broadcast_to([P, NT, cnt, cnt])
                other = vals.unsqueeze(2).broadcast_to([P, NT, cnt, cnt])
                bm = before.unsqueeze(1).broadcast_to([P, NT, cnt, cnt])
                V.tensor_tensor(t1, other, me, ALU.is_gt)
                link(V.tensor_tensor(t2, other, me, ALU.is_equal))
                link(V.tensor_tensor(t2, t2, bm, ALU.mult))
                link(V.tensor_tensor(t1, t1, t2, ALU.add))
                link(V.reduce_sum(dst, t1, AXX))

            c1 = rt[:, :, 32:48].rearrange("p c (a b) -> p c a b", a=4)
            c2 = rt[:, :, 48:64].rearrange("p c (a b) -> p c a b", a=4)
            rank_of(r4(7), 4, r4(0), before4, c1, c2)
            link(V.tensor_scalar(r4(1), r4(0), 1.5, None, ALU.is_lt))
            link(V.memset(masked[:, :, E:E + 4], NEG))
            link(V.tensor_tensor(masked[:, :, 0:E].rearrange("p c (g e) -> p c g e", g=EG), s4,
                                 r4(1).unsqueeze(3).broadcast_to([P, NT, EG, 4]), ALU.mult))
            for c in range(NT):
                i = V.max(top8[:, c, :], masked[:, c, :])
            link(i)
            link(V.memset(top8[:, :, 4:8], NEG))
            for c in range(NT):
                i = V.match_replace(struck[:, c, :], top8[:, c, :], masked[:, c, :], RB)
            link(i)
            link(V.tensor_scalar(rank[:, :, :], struck[:, :, 0:E], RB, None, ALU.is_equal))
            link(V.tensor_tensor(rank[:, :, :], rank[:, :, :], sg[:, :, :], ALU.mult))
            link(V.reduce_sum(den[:, :], rank[:, :, :], AXX))
            link(V.tensor_scalar(den[:, :], den[:, :], 1e-20, None, ALU.add))
            link(V.reciprocal(den[:, :], den[:, :]))
            link(V.tensor_scalar(den[:, :], den[:, :], 2.5, None, ALU.mult))
            V.tensor_tensor(comb[:, :, :], rank[:, :, :], den[:, :].unsqueeze(2).broadcast_to([P, NT, E]),
                            ALU.mult).then_inc(s("comb"), 2)
            dve.wait_ge(s("filled"), 4)
            for b in range(B):
                src, bs = ps[0:E, 5, :], slice(b * S, (b + 1) * S)
                dve.wait_ge(s("cT_ps"), b + 1)
                V.tensor_copy(combr[0:E, bs], src).then_inc(s("combT"), 1)
                dve.wait_ge(s("combT"), 3 * b + 1)
                link(V.tensor_tensor(cr[0:E, :], src, combr[0:E, bs], ALU.subtract))
                V.tensor_copy(combr[32:32 + E, bs], cr[0:E, :]).then_inc(s("combT"), 1)
                link(V.tensor_copy(crb[0:E, :], cr[0:E, :]))
                V.tensor_tensor(combr[64:64 + E, bs], cr[0:E, :], crb[0:E, :], ALU.subtract).then_inc(s("combT"), 1)
            for n in range(B * NM):
                b, i = n // NM, n % NM
                dve.wait_ge(s("m_silu"), n + 1)
                dve.wait_ge(s("u_ps"), n + 1)
                V.tensor_tensor(hs[:, n % NHS, :], hs[:, n % NHS, :], ps[:, 2 + n % 2, :], ALU.mult).then_inc(s("m_h1"), 1)
                if i < NM - 1:
                    m = b * (NM - 1) + i
                    dve.wait_ge(s("m_h1"), n + 1)
                    dve.wait_ge(s("w_ps"), m + 1)
                    V.tensor_tensor(hs[:, n % NHS, :], hs[:, n % NHS, :], ps[:, 4 + m % 2, :], ALU.mult).then_inc(s("m_h2"), 1)
            for b in range(B):
                dve.wait_ge(s("dn_ps"), NM * (b + 1))
                cs = slice(CB * b, CB * b + CB)
                V.tensor_tensor(x_tm[:, cs, :], ps[:, 6 + b, :].rearrange("p (c d) -> p c d", c=CB), x_tm[:, cs, :],
                                ALU.add).then_inc(s("x_up"), CB)

            layernorm(3)
            for b in range(B):
                dve.wait_ge(s("xnT"), 2 * 3 + b + 1)
                link(V.tensor_tensor(xx[:, b, :], xnT[:, b, 0:S], xnT[:, b, 1:S + 1], ALU.subtract))
                for i, n in enumerate(("maa_k", "maa_v", "maa_r", "maa_g")):
                    V.scalar_tensor_tensor(out=mixes[:, i, b, :], in0=xx[:, b, :], scalar=col(n), in1=xnT[:, b, 1:S + 1],
                                           op0=ALU.mult, op1=ALU.add).then_inc(s("mix"), 1)
            dve.wait_ge(s("tabs"), 3)
            for b in range(B):
                cs = slice(CB * b, CB * b + CB)
                dve.wait_ge(s("r_kh"), b + 1)
                V.tensor_tensor(Kl[:, b, :], ps[:, 1, :], Kh[:, b, :].bitcast(F32), ALU.subtract).then_inc(s("r_kv"), 1)
                dve.wait_ge(s("r_pj_ps"), 5 * b + 3)
                V.tensor_tensor(Ktm[:, cs, :], ps[:, 2, :].rearrange("p (c d) -> p c d", c=CB),
                                kpow[:, :].unsqueeze(1).broadcast_to([P, CB, D]), ALU.mult).then_inc(s("r_kv"), 1)
                dve.wait_ge(s("r_pj_ps"), 5 * b + 4)
                V.tensor_copy(V_tm[:, cs, :], ps[:, 3, :].rearrange("p (c d) -> p c d", c=CB)).then_inc(s("r_kv"), 1)
                dve.wait_ge(s("r_pj"), b + 1)
                V.tensor_tensor(Rw[:, b, :].rearrange("p (c t) -> p c t", c=CB), RT[:, b, :].rearrange("p (c t) -> p c t", c=CB),
                                rpow[:, :].unsqueeze(1).broadcast_to([P, CB, P]), ALU.mult)
            for b in range(B):
                dve.wait_ge(s("r_rh"), b + 1)
                V.tensor_tensor(Ql[:, b, :], RT[:, b, :], Qh[:, b, :].bitcast(F32), ALU.subtract).then_inc(s("r_rl"), 1)
            for m in range(NT):
                b, j = m // CB, m % CB
                for q in range(4):
                    dve.wait_ge(s("r_s_ps"), 4 * m + q + 1)
                    if m >= 2 and q == 0:
                        dve.wait_ge(s("y_ps"), m - 1)
                    V.tensor_tensor(Pr[:, m % 2, 4 * q:4 * q + 4, :], ps[:, q, :].rearrange("p (h t) -> p h t", h=4),
                                    Wtab[:, 4 * q:4 * q + 4, :], ALU.mult).then_inc(s("r_p"), 1)
                if j < CB - 1:
                    k = b * (CB - 1) + j
                    dve.wait_ge(s("u_st_ps"), k + 1)
                    if k >= 2:
                        dve.wait_ge(s("y_ps"), m)
                    if k:
                        dve.wait_ge(s("state"), k)
                    V.tensor_tensor(Um[:, :], ps[:, 5, 0:P], bdiag, ALU.mult).then_inc(s("um"), 1)
                    dve.wait_ge(s("um"), k + 1)
                    if j == 0:
                        V.tensor_copy(St[:, k % 2, :], Um[:, :]).then_inc(s("state"), 1)
                    else:
                        dve.wait_ge(s("state"), k)
                        V.scalar_tensor_tensor(out=St[:, k % 2, :], in0=St[:, (k - 1) % 2, :], scalar=w128, in1=Um[:, :],
                                               op0=ALU.mult, op1=ALU.add).then_inc(s("state"), 1)
            for b in range(B):
                dve.wait_ge(s("r_mean_ps"), b + 1)
                V.scalar_tensor_tensor(out=yc[:, b, :], in0=ps[:, b, :], scalar=-1.0 / HD, in1=yc[:, b, :],
                                       op0=ALU.mult, op1=ALU.add).then_inc(s("r_yc"), 1)
            for b in range(B):
                dve.wait_ge(s("r_var_ps"), b + 1)
                V.tensor_scalar(gv[:, b, :], ps[:, 2 + b, :], 1.0 / HD, 64e-5, ALU.mult, ALU.add).then_inc(s("r_var"), 1)
            for b in range(B):
                y, r, t = yc[:, b, :], gy[:, b, :], gn[:, b, :]
                dve.wait_ge(s("r_sd"), b + 1)
                link(V.reciprocal(r, t))
                link(V.tensor_tensor(t, r, gv[:, b, :], ALU.mult))
                link(V.scalar_tensor_tensor(out=t, in0=t, scalar=-0.5, in1=r, op0=ALU.mult, op1=ALU.mult))
                link(V.scalar_tensor_tensor(out=r, in0=t, scalar=1.5, in1=r, op0=ALU.add, op1=ALU.mult))
                link(V.tensor_tensor(y, y, r, ALU.mult))
                link(V.tensor_scalar(y, y, col("hn_g"), col("hn_b"), ALU.mult, ALU.add))
                V.tensor_tensor(y, y, GT[:, b, :], ALU.mult).then_inc(s("r_yg"), 1)
            for b in range(B):
                dve.wait_ge(s("r_op_ps"), b + 1)
                cs = slice(CB * b, CB * b + CB)
                V.tensor_tensor(x_tm[:, cs, :], ps[:, 4 + b, :].rearrange("p (c d) -> p c d", c=CB), x_tm[:, cs, :],
                                ALU.add).then_inc(s("x_up"), CB)

            context(1, 4, 4)

            layernorm(5)
            for b in range(B):
                cs = range(CB * b, CB * b + CB)
                dve.wait_ge(s("xn"), 5 * NT + CB * (b + 1))
                for c in cs:
                    i = V.bn_stats(st[:, c, :], xn_tm[:, c, :])
                link(i)
                for c in cs:
                    i = V.bn_aggr(mv[:, c, :], st[:, c, :])
                link(i)
                V.tensor_scalar(veps[:, CB * b:CB * b + CB], mv[:, CB * b:CB * b + CB, 1], 1e-5, None,
                                ALU.add).then_inc(s("veps"), 1)
            dve.wait_ge(s("xnT_ps"), 12)
            for b in range(B):
                dve.wait_ge(s("rstd"), 2 * 6 + b + 1)
                for c in range(CB * b, CB * b + CB):
                    V.tensor_scalar(xn_tm[:, c, :], xn_tm[:, c, :], mv[:, c, 0:1], rstd[:, c:c + 1],
                                    ALU.subtract, ALU.mult).then_inc(s("hn2"), 1)
            def f_stats(c):
                dve.wait_ge(s("f_h_ps"), c + 1)
                for e in range(FE):
                    i = V.bn_stats(fst[:, e, :], ps[:, 2 * (c % 2) + e // 2, (e % 2) * FH:(e % 2 + 1) * FH])
                link(i)
                for e in range(FE):
                    i = V.bn_aggr(fmv[:, c, e, :], fst[:, e, :])
                link(i)
                V.tensor_scalar(fve[:, c, :], fmv[:, c, :, 1], 1e-5, None, ALU.add).then_inc(s("f_ve"), 1)

            def f_shift(c):
                dve.wait_ge(s("f_rs"), c + 1)
                V.scalar_tensor_tensor(out=fnm[:, c, :], in0=fmv[:, c, :, 0], scalar=-1.0, in1=frs[:, c, :],
                                       op0=ALU.mult, op1=ALU.mult).then_inc(s("f_st"), 1)
                e = FE - 1
                V.tensor_scalar(hn[c][:, e * FH:(e + 1) * FH], ps[:, 2 * (c % 2) + 1, FH:2 * FH], fmv[:, c, e, 0:1],
                                frs[:, c, e:e + 1], ALU.subtract, ALU.mult).then_inc(s("f_hv"), 1)

            def f_combine(c):
                dve.wait_ge(s("f_o_ps"), c + 1)
                bank = ps[:, 6 + c % 2, :]
                link(V.tensor_scalar(otm[:, c, :], bank[:, 0:P], fw[:, c, 0:1], None, ALU.mult))
                for e in range(1, FE):
                    i = V.scalar_tensor_tensor(out=otm[:, c, :], in0=bank[:, e * P:(e + 1) * P], scalar=fw[:, c, e:e + 1],
                                               in1=otm[:, c, :], op0=ALU.mult, op1=ALU.add)
                    if e < FE - 1:
                        link(i)
                i.then_inc(s("f_cmb"), 1)

            f_stats(0)
            f_stats(1)
            f_shift(0)
            f_shift(1)
            dve.wait_ge(s("fl_ps"), 1)
            lg = ps[:, 6, 0:NT * FE].rearrange("p (c e) -> p c e", e=FE)
            link(V.tensor_reduce(f1[:, :], lg, AXX, ALU.max))
            V.tensor_tensor(fsm[:, :, :], lg, f1[:, :].unsqueeze(2).broadcast_to([P, NT, FE]),
                            ALU.subtract).then_inc(s("fsub"), 1)
            f_stats(2)
            f_stats(3)
            f_shift(2)
            f_shift(3)
            dve.wait_ge(s("fexp"), 1)
            link(V.reduce_sum(f1[:, :], fsm[:, :, :], AXX))
            link(V.reciprocal(f1[:, :], f1[:, :]))
            link(V.tensor_tensor(fsm[:, :, :], fsm[:, :, :], f1[:, :].unsqueeze(2).broadcast_to([P, NT, FE]), ALU.mult))
            rank_of(fsm[:, :, :], FE, fw[:, :, :], before4, c1, c2)
            link(V.tensor_scalar(fw[:, :, :], fw[:, :, :], 1.5, None, ALU.is_lt))
            link(V.tensor_tensor(fw[:, :, :], fw[:, :, :], fsm[:, :, :], ALU.mult))
            link(V.reduce_sum(f1[:, :], fw[:, :, :], AXX))
            link(V.tensor_scalar(f1[:, :], f1[:, :], 1e-8, None, ALU.add))
            link(V.reciprocal(f1[:, :], f1[:, :]))
            link(V.tensor_tensor(fw[:, :, :], fw[:, :, :], f1[:, :].unsqueeze(2).broadcast_to([P, NT, FE]), ALU.mult))
            for c in range(CB, NT, 2):
                f_stats(c)
                f_stats(c + 1)
                f_shift(c)
                f_shift(c + 1)

            def last_layernorm(b):
                cs = range(CB * b, CB * b + CB)
                sl = slice(CB * b, CB * b + CB)
                dve.wait_ge(s("f_cmb"), CB * (b + 1))
                for c in cs:
                    i = V.bn_stats(st[:, c, :], otm[:, c, :])
                link(i)
                for c in cs:
                    i = V.bn_aggr(mv[:, c, :], st[:, c, :])
                link(i)
                V.tensor_scalar(veps[:, sl], mv[:, sl, 1], 1e-5, None, ALU.add).then_inc(s("veps"), 1)
                dve.wait_ge(s("rstd"), 2 * 7 + b + 1)
                for c in cs:
                    i = V.tensor_scalar(otm[:, c, :], otm[:, c, :], mv[:, c, 0:1], rstd[:, c:c + 1], ALU.subtract, ALU.mult)
                link(i)
                link(V.tensor_tensor(otm[:, sl, :], otm[:, sl, :], row("on_g").unsqueeze(1).broadcast_to([P, CB, D]), ALU.mult))
                dve.wait_ge(s("xb"), 6 + b + 1)
                V.tensor_tensor(otm[:, sl, :], otm[:, sl, :], x_tm[:, sl, :], ALU.add).then_inc(s("final"), 1)

            for b in range(B):
                for j in range(CB):
                    f_combine(CB * b + j)
                last_layernorm(b)

        @block.gpsimd
        def _(pool):
            Gp = nc.gpsimd

            def inv_std(k):
                for b in range(B):
                    pool.wait_ge(s("veps"), 2 * k + b + 1)
                    sl = slice(CB * b, CB * b + CB)
                    Gp.tensor_tensor(rstd[:, sl], veps[:, sl], half[:, 0:CB], ALU.pow).then_inc(s("rstd"), 1)

            def with_bias(k, name):
                for b in range(B):
                    pool.wait_ge(s("xn"), NT * k + CB * (b + 1))
                    sl = slice(CB * b, CB * b + CB)
                    Gp.tensor_tensor(x_tm[:, sl, :], x_tm[:, sl, :], row(name).unsqueeze(1).broadcast_to([P, CB, D]),
                                     ALU.add).then_inc(s("xb"), 1)

            def repeat_context(l):
                for b in range(B):
                    Gp.tensor_copy(ctxrep[:, b * NB * P:b * NB * P + HK].rearrange("p (h n) -> p h n", h=H),
                                   ctxT[:, b, 0:NC].unsqueeze(1).broadcast_to([P, H, NC]))
                    i = Gp.memset(ctxrep[:, b * NB * P + HK:(b + 1) * NB * P], 0.0)
                i.then_inc(s("ctxrep"), 1)

            def split_keys(l):
                pool.wait_ge(s("pre"), 9 * l + 1)
                Gp.tensor_copy(Kxh[:, :], Kx[:, :]).then_inc(s("kxh"), 1)
                pool.wait_ge(s("kxh"), l + 1)
                Gp.tensor_tensor(Kxl[:, :], Kx[:, :], Kxh[:, :].bitcast(F32), ALU.subtract).then_inc(s("kx"), 1)

            def value_blocks(l):
                for b in range(B):
                    pool.wait_ge(s("pre"), 9 * l + 3 + 3 * (b + 1))
                    v = Vbdx[:, b, :, :]
                    Gp.tensor_tensor(v[:, :, 0:P], v[:, :, 0:P], row(f"x{l}_bv").unsqueeze(1).broadcast_to([P, NB, P]),
                                     ALU.add).then_inc(s("vb"), 1)
                    Gp.tensor_copy(v[:, :, P:VW], bdx_sb[:, :, P:VW])
                    pool.wait_ge(s("vb"), 2 * l + b + 1)
                    Gp.tensor_tensor(v[:, :, 0:P], v[:, :, 0:P], bdx_sb[:, :, 0:P], ALU.mult).then_inc(s("vbdx"), 1)

            Gp.memset(half[:, :], -0.5).then_inc(s("filled"), 1)
            Gp.memset(xnT[:, :, 0:1], 0.0).then_inc(s("filled"), 1)
            Gp.memset(sel4[:, :, :].bitcast(F32), 0.0).then_inc(s("filled"), 1)
            pool.wait_ge(s("filled"), 1)
            inv_std(0)
            pool.wait_ge(s("in_first"), 16 * 3)
            pool.wait_ge(s("filled"), 3)
            for t, where in terms.items():
                i = Gp.tensor_copy(sel4[:, t, :].rearrange("p (h t d) -> p h t d", t=4, d=HD)[:, :, where, :],
                                   ident.rearrange("p (h d) -> p h d", d=HD).unsqueeze(2).broadcast_to([P, H, 2, HD]))
            i.then_inc(s("sel"), 1)
            pool.wait_ge(s("in_ctx"), 16 * 5)
            repeat_context(0)
            pool.wait_ge(s("in_attn"), 16 * 3)
            with_bias(0, "a_bo")
            pool.wait_ge(s("lam"), 2)
            Gp.tensor_scalar(lamr[:, :], lamr[:, :], 3.0e38, None, ALU.min).then_inc(s("lam_ok"), 1)
            Gp.tensor_scalar(lamc[:, 0:1], lamc[:, 0:1], 3.0e38, None, ALU.min).then_inc(s("lam_ok"), 1)
            pool.wait_ge(s("lam_ok"), 2)
            Gp.tensor_scalar(lamc[:, 1:2], lamc[:, 0:1], -1.0, None, ALU.mult).then_inc(s("lam_ok"), 2)

            split_keys(0)
            value_blocks(0)
            Gp.tensor_tensor(Wtab[:, :, :], gapT.unsqueeze(1).broadcast_to([P, H, P]),
                             lamr[:, ::HD].unsqueeze(2).broadcast_to([P, H, P]), ALU.mult).then_inc(s("gap"), 1)
            pool.wait_ge(s("wexp"), 1)
            Gp.tensor_tensor(Wtab[:, :, :], Wtab[:, :, :], causal.unsqueeze(1).broadcast_to([P, H, P]),
                             ALU.mult).then_inc(s("wmask"), 1)
            inv_std(1)
            with_bias(1, "x0_bo")
            repeat_context(1)
            inv_std(2)
            Gp.memset(combr, 0.0).then_inc(s("filled"), 1)
            split_keys(1)
            pool.wait_ge(s("in_sel"), 16 * 2)
            value_blocks(1)
            inv_std(3)
            pool.wait_ge(s("r_pj_ps"), 5 * B)
            Gp.memset(Vx[:, :, :, :], 0.0).then_inc(s("filled"), 1)
            pool.wait_ge(s("filled"), 5)
            for c in range(NT):
                pool.wait_ge(s("r_kv"), 3 * (c // CB + 1))
                if c >= 2:
                    pool.wait_ge(s("y_ps"), c - 1)
                o = 2048 * (c % 2)
                Gp.tensor_copy(big[:, o:o + H * (P + HD)].rearrange("p (h n) -> p h n", h=H)[:, :, 0:HD],
                               V_tm[:, c, :].rearrange("p (h d) -> p h d", h=H)).then_inc(s("vx"), 1)
            inv_std(4)
            with_bias(4, "x1_bo")
            inv_std(5)
            inv_std(6)
            with_bias(5, "on_b")
            for c in range(NT):
                pool.wait_ge(s("f_ve"), c + 1)
                Gp.tensor_tensor(frs[:, c, :], fve[:, c, :], half[:, 0:FE], ALU.pow).then_inc(s("f_rs"), 1)
            inv_std(7)


def kernel(**inputs):
    import numpy as np
    import ml_dtypes
    import concourse.bacc as bacc
    from concourse.bass_utils import run_bass_kernel_spmd

    a = {n: np.asarray(v) for n, v in inputs.items()}
    f = np.float32
    p = np.arange(P)

    def every(v):
        return np.broadcast_to(v, (P,) + v.shape)

    def side(parts):
        return np.concatenate(parts, axis=1)

    same_head = (p[:, None] // HD == p[None, :] // HD).astype(f)
    gap = np.maximum(p[None, :] - p[:, None] - 1, 0).astype(f)
    causal = (p[None, :] > p[:, None]).astype(f)
    consts = side([np.eye(P, dtype=f), np.ones((P, P), f), np.full((P, P), 1.0 / S, f), gap, causal, same_head,
                   every(np.arange(S, dtype=f))])
    before16 = (np.arange(E)[None, :] < np.arange(E)[:, None]).astype(f).reshape(-1)
    before4 = (np.arange(4)[None, :] < np.arange(4)[:, None]).astype(f).reshape(-1)
    small = side([(p[:, None] // HD == np.arange(H)[None, :]).astype(f),
                  (p[:, None] + P * np.arange(CB)[None, :]).astype(f),
                  ((p[:, None] // SLOTS == np.arange(32)[None, :] // HD) & (p[:, None] % SLOTS < TOPK)).astype(f),
                  every(before16), every(before4), every(np.arange(P, dtype=f)),
                  (p[:, None] - (P - 1)).astype(f), np.zeros((P, 1), f),
                  (p[:, None] // 32 == np.arange(4)[None, :]).astype(f)])
    r = p[:, None] + P * np.arange(NB)[None, :]
    cols_v = np.arange(VW)
    bdx = ((r[:, :, None] < HK) & (r[:, :, None] // NC == np.where(cols_v < D, cols_v // HD, cols_v - D))).astype(f)
    unit = np.arange(P)
    selx = np.zeros((P, 8, P), f)
    for m in range(8):
        for part in range(3):
            selx[32 * part + 2 * m + unit // 64, m, unit] = 1
    selx = selx.reshape(P, -1).astype(ml_dtypes.bfloat16)

    A0, X0, F0, R1, X1, F1 = "L0_attn_", "L0_xattn_", "L0_ffn_", "L1_attn_", "L1_xattn_", "L1_ffn_"
    td_row = np.repeat(a[R1 + "time_decay"], HD)
    cols = np.stack([a[A0 + "bq"], a[A0 + "bk"], a[X0 + "bq"], a[X0 + "bk"], a[X1 + "b_q"], a[X1 + "b_k"],
                     a[R1 + "time_maa_k"], a[R1 + "time_maa_v"], a[R1 + "time_maa_r"], a[R1 + "time_maa_g"],
                     td_row, a[F1 + "rn_g"], a[F1 + "rn_b"], a[R1 + "ln_g"], a[R1 + "ln_b"]], axis=1)
    cols = side([cols, a[F1 + "ln_g"].reshape(8, P).T, a[F1 + "ln_b"].reshape(8, P).T])
    rows = every(np.concatenate([a[A0 + "bv"], a[A0 + "bo"], a[X0 + "bv"], a[X0 + "bo"], a[X1 + "b_v"], a[X1 + "b_o"],
                                 a[F1 + "on_g"], a[F1 + "on_b"]]))
    wa = side([a[A0 + n] for n in ("Wq", "Wk", "Wv", "Wo")])
    wb = side([a[X0 + n].T for n in ("Wq", "Wk", "Wv", "Wo")] + [a[X1 + n].T for n in ("W_q", "W_k", "W_v", "W_o")])
    wr = side([a[R1 + n].T for n in ("w_r", "w_k", "w_v", "w_g", "w_o")])
    wm = side([a[F0 + "gate_w"].reshape(-1, D).T, a[F0 + "sh_gate_w"].T, a[F0 + "up_w"].reshape(-1, D).T,
               a[F0 + "sh_up_w"].T,
               a[F0 + "down_w"].transpose(0, 2, 1).reshape(8, P, D).transpose(1, 0, 2).reshape(P, -1),
               a[F0 + "sh_down_w"].T])
    w1 = a[F1 + "w1"].transpose(1, 0, 2).reshape(D, -1)
    w2 = a[F1 + "w2"].reshape(8, P, D).transpose(1, 0, 2).reshape(P, -1)
    given = {
        "x": a["x"], "sidx": every(a[A0 + "sample_idx"]), "consts": consts, "small": small, "selx": selx, "bdx": bdx,
        "cols": cols, "rows": rows, "wa": wa, "wb": wb, "ctxt": np.pad(a["ctx_1024"].transpose(2, 0, 1), ((0, 0), (0, 0), (0, NCP - NC))), "wm": wm,
        "rw": a[F0 + "router_weight"].T, "wr": wr, "tdrow": every(td_row), "urow": every(a[R1 + "time_faaaa"]),
        "w1": w1, "w2": w2, "rwf": a[F1 + "router_w"].T, "ebias": every(a[F0 + "e_bias"]),
    }
    nc = bacc.Bacc("TRN2", target_bir_lowering=False, num_devices=1)
    arrays, args = {}, []
    for n, v in given.items():
        arrays[f"{n}_dram"] = np.ascontiguousarray(v)
        args.append(nc.dram_tensor(f"{n}_dram", v.shape, mybir.dt.from_np(v.dtype), kind="ExternalInput").ap())
    args.append(nc.dram_tensor("out_dram", (B, S, D), F32, kind="ExternalOutput").ap())
    build(nc, *args)
    return run_bass_kernel_spmd(nc, [arrays], core_ids=[0]).results[0]["out_dram"]
```

```python
from contextlib import ExitStack

import concourse.bass as bass
from concourse import mybir

ALU = mybir.AluOpType
ACT = mybir.ActivationFunctionType
AXX = mybir.AxisListType.X
F32 = mybir.dt.float32
BF16 = mybir.dt.bfloat16
F32R = mybir.dt.float32r
I32 = mybir.dt.int32
U32 = mybir.dt.uint32

P = 128
D = 128
B, S = 2, 512
T = B * S
NT = T // P
CB = S // P
H, HD = 16, 8
NS = 256
TOPK = 31
SLOTS = 32
G = H // 4
NC = 77
NCP = NC + 1
HK = H * NC
NB = -(-HK // P)
LB = HK - (NB - 1) * P
VW = D + H
E, EG = 16, 4
NM = 9
FE, FH = 4, 256
NEG = -3.0e38
AHEAD = 7
BEFORE = 5
NHS = 8
STRUCK = 2 * NEG / 3
ASCALE = HD ** -0.5

COLS = ["a_bq", "a_bk", "x0_bq", "x0_bk", "x1_bq", "x1_bk", "maa_k", "maa_v", "maa_r", "maa_g",
        "td", "rn_g", "rn_b", "hn_g", "hn_b"]
COL = {n: i for i, n in enumerate(COLS)}
NCOL = len(COLS) + 16
ROWS = ["a_bv", "a_bo", "x0_bv", "x0_bo", "x1_bv", "x1_bo", "on_g", "on_b"]
ROW = {n: i for i, n in enumerate(ROWS)}
WA = ["a_q", "a_k", "a_v", "a_o"]
WB = ["x0_q", "x0_k", "x0_v", "x0_o", "x1_q", "x1_k", "x1_v", "x1_o"]
WR = ["w_r", "w_k", "w_v", "w_g", "w_o"]


def build(nc, x, sidx, consts, small, selx, bdx, cols, rows, wa, wb, ctxt, wm, rw, wr, tdrow, urow, w1, w2, rwf, ebias, out):
    with ExitStack() as ctx:
        def sb(name, shape, dt=F32):
            return ctx.enter_context(nc.sbuf_tensor(name, shape, dt))

        made = {}

        def s(name):
            if name not in made:
                made[name] = ctx.enter_context(nc.semaphore(name))
            return made[name]

        ps = ctx.enter_context(nc.psum_tensor("ps", [P, 8, 512], F32))

        cst = sb("cst", [P, 6 * P + 512])
        ident, ones, inv_s = cst[:, 0:P], cst[:, P:2 * P], cst[:, 2 * P:3 * P]
        gapT, causal, bdiag = cst[:, 3 * P:4 * P], cst[:, 4 * P:5 * P], cst[:, 5 * P:6 * P]
        iota_row = cst[:, 6 * P:6 * P + 512]
        sm = sb("sm", [P, 16 + 4 + 32 + 16 + P + 2 + 4])
        hmask = sm[:, 0:16]
        iota_pc = sm[:, 16:20]
        slotmask = sm[:, 20:52]
        before4 = sm[:, 52:68].rearrange("p (a b) -> p a b", a=4)
        trow = sm[:, 68:68 + P]
        ncol = sm[:, 68 + P:69 + P]
        quad = sm[:, 70 + P:74 + P]
        colsb = sb("colsb", [P, NCOL])
        rowsb = sb("rowsb", [P, len(ROWS) * P])
        wa_sb = sb("wa_sb", [P, len(WA) * P])
        wb_sb = sb("wb_sb", [P, len(WB) * P])
        wm_sb = sb("wm_sb", [P, 3 * NM * P])
        wr_sb = sb("wr_sb", [P, len(WR) * P])
        w1_sb = wm_sb[:, 0:FE * FH]
        w2_sb = wm_sb[:, FE * FH:FE * FH + 8 * P]
        rw_sb = sb("rw_sb", [P, E + FE])
        eb_sb = sb("eb_sb", [P, E])
        ctxT = sb("ctxT", [P, B, NCP])
        tdr = sb("tdr", [P, P])
        ur = sb("ur", [P, H])
        half = sb("half", [P, 256])
        const16 = half[:, :].bitcast(BF16)

        def col(n):
            return colsb[:, COL[n]:COL[n] + 1]

        def row(n):
            return rowsb[:, ROW[n] * P:(ROW[n] + 1) * P]

        def w(n):
            for names, t in ((WA, wa_sb), (WB, wb_sb), (WR, wr_sb)):
                if n in names:
                    i = names.index(n)
                    return t[:, i * P:(i + 1) * P]

        x_tm = sb("x_tm", [P, NT, D])
        xn_tm = sb("xn_tm", [P, NT, D])
        xnT = sb("xnT", [P, B, S + 1])
        KT = sb("KT", [P, B, S])
        V_tm = sb("V_tm", [P, NT, D])
        attnT = sb("attnT", [P, B, S])
        big = sb("big", [P, 8192])
        sel_sb = KT[:, 0, :].bitcast(BF16)
        QT = big[:, 7168:8192].rearrange("p (b n) -> p b n", b=B)
        aux = sb("aux", [P, 4096])
        st = sb("st", [P, NT, 6])
        mv = sb("mv", [P, NT, 2])
        veps = sb("veps", [P, NT])
        rstd = sb("rstd", [P, NT])
        Qh = sb("Qh", [P, B, S], F32R)
        Ql = sb("Ql", [P, B, S], F32R)
        Qp = sb("Qp", [P, G, T], F32R)
        bd = sb("bd", [P, 4096], F32R)
        sel4 = sb("sel4", [P, 4, G * P], F32R)
        QH, QL, KH, KL = range(4)
        terms = {QH: slice(0, 2), QL: slice(2, 4), KH: slice(0, 4, 2), KL: slice(1, 4, 2)}
        Kx = sb("Kx", [P, B * NCP])
        Kxh = sb("Kxh", [P, B * NCP], F32R)
        Kxl = sb("Kxl", [P, B * NCP], F32R)
        Kxh2 = sb("Kxh2", [P, B * NS], F32R)
        Kxl2 = sb("Kxl2", [P, B * NS], F32R)
        Kbp = sb("Kbp", [P, G, 4, B * NCP], F32R)
        Kpk = sb("Kpk", [P, G, B * NCP])
        Vbdx = sb("Vbdx", [P, B, NB, VW])
        ctxrep = big[:, 0:B * NB * P]
        Vraw = ctxrep.rearrange("p (b n d) -> p b n d", b=B, n=NB)
        bdx_sb = big[:, B * NB * P:B * NB * P + NB * VW].rearrange("p (n v) -> p n v", n=NB)
        Wtab = sb("Wtab", [P, H, P])
        rpow = sb("rpow", [P, P])
        kpow = sb("kpow", [P, P])
        lamr = sb("lamr", [P, P])
        lamc = sb("lamc", [P, 4])

        def xchunk(c, src):
            return src[:, c // CB, (c % CB) * P:(c % CB + 1) * P]

        def xnchunk(c):
            return xnT[:, c // CB, 1 + (c % CB) * P:1 + (c % CB + 1) * P]

        block = ctx.enter_context(nc.Block())
        x_v = x.rearrange("b (c p) d -> p (b c) d", p=P)
        out_v = out.rearrange("b (c p) d -> p (b c) d", p=P)

        PRE_ORDER = [("v", 0), ("v", 1), ("k", 0), ("k", 1), ("v", 2), ("v", 3), ("v", 4), ("v", 5)]
        PRE_FIRST = 6
        KEYS_AT, PRE_AT, QROWS_AT = (1, 9, 17), (2, 6, 10, 11, 14, 18, 19, 22, 23), (26, 29)

        bda = bd[:, :].rearrange("p (i j n) -> p i j n", i=4, j=4)
        Ksh = Kxh2[:, :].rearrange("p (b n) -> p b n", b=B)
        Ksl = Kxl2[:, :].rearrange("p (b n) -> p b n", b=B)
        OH = bd[:, :].rearrange("p (c n) -> p c n", c=NT)
        OHT = big[:, 4096:8192].rearrange("p (c n) -> p c n", c=NT)
        ohs = aux[:, 0:1024].rearrange("p (c n) -> p c n", c=CB)
        xsamp = aux[:, 1024:1536].rearrange("p (b n) -> p b n", b=B)
        KsT = aux[:, 1536:2048].rearrange("p (b n) -> p b n", b=B)
        Qbd = aux[:, 1024:2048].rearrange("p (b h n) -> p b h n", b=B, h=H)
        Pa = aux[:, 2048:3072].rearrange("p (i n) -> p i n", i=2)
        PTa = aux[:, 3072:4096].rearrange("p (i n) -> p i n", i=2)
        sidx_i = aux[:, 3072:3072 + NS].bitcast(I32)
        sidx_f = aux[:, 3072 + NS:3072 + 2 * NS]
        kbar = sb("kbar", [P, B])
        kbarbd = sb("kbarbd", [P, B, H])
        Mx = sb("Mx", [P, CB, B, H])
        MT = attnT[0:32, :, :]
        v8 = sb("v8", [32, SLOTS])
        idx = sb("idx", [32, SLOTS], U32)
        idxf = sb("idxf", [32, SLOTS])
        idxT = sb("idxT", [32, 32])
        idxcol = sb("idxcol", [P, 8])
        diag = [Kxh2[0:32, :], Kxl2[0:32, :]]
        ones_r = sb("ones_r", [32, P], F32R)
        Vmb = sb("Vmb", [P, B, D])
        Vmc = sb("Vmc", [P, B])
        nmx = sb("nmx", [P, 8])
        nb = sb("nb", [P, 8])
        rsum = sb("rsum", [P, 8])
        rinv = sb("rinv", [P, 8])
        dgt = attnT[:, 1, 0:256].rearrange("p (n d) -> p n d", n=8)
        dg = attnT[:, 1, 256:512].rearrange("p (n d) -> p n d", n=8)
        Ssb = aux[:, 0:2 * HK].rearrange("p (i n) -> p i n", i=2)
        PTx = big[:, 8192 - NHS * S:8192 - NHS * S + 2 * NB * P].rearrange("p (i n) -> p i n", i=2)
        mxx = sb("mxx", [P, 2, H])
        rsx = sb("rsx", [P, 2, H])
        atm = big[:, 7424:7936].rearrange("p (c n) -> p c n", c=4)
        sg = sb("sg", [P, NT, E])
        sc = sb("sc", [P, NT, E])
        rt = aux[:, 2048:2560].rearrange("p (c n) -> p c n", c=NT)
        masked = sb("masked", [P, NT, E + 4])
        struck = sb("struck", [P, NT, E + 4])
        top8 = sb("top8", [P, NT, 8])
        rank = sb("rank", [P, NT, E])
        den = sb("den", [P, NT])
        comb = sb("comb", [P, NT, E])
        combr = aux[:, 2560:3072].bitcast(BF16)
        cr = aux[0:E, 0:S]
        crb = sb("crb", [E, S], BF16)
        hs = big[:, 8192 - NHS * S:8192].rearrange("p (i n) -> p i n", i=NHS)
        xx = big[:, 0:1024].rearrange("p (b n) -> p b n", b=B)
        mixes = big[:, 1024:5120].rearrange("p (m b n) -> p m b n", m=4, b=B)
        Rbd = bd[:, :].rearrange("p (i g j t) -> p i g j t", i=2, g=G, j=4)
        Pr = big[:, 4096:8192].rearrange("p (i h t) -> p i h t", i=2, h=H)
        Rw = aux[:, 0:1024].rearrange("p (b n) -> p b n", b=B)
        Ktm = aux[:, 1024:2048].rearrange("p (c n) -> p c n", c=NT)
        GT = aux[:, 2048:3072].rearrange("p (b n) -> p b n", b=B)
        Vx = big[:, 0:4096].rearrange("p (i h n) -> p i h n", i=2, h=H)
        Kh, Kl = Qh, Ql
        Rh = [Kxh2[:, :], Qh[:, 0, :]]
        Rl = [Kxl2[:, :], Ql[:, 0, :]]
        gv = sb("gv", [P, B, CB * H])
        gn = sb("gn", [P, B, CB * H])
        gy = sb("gy", [P, B, CB * H])
        gx = [attnT[:, 0, :], KT[:, 0, :]]
        yc = aux[:, 3072:4096].rearrange("p (b n) -> p b n", b=B)
        St = sb("St", [P, 2, D])
        Um = sb("Um", [P, D])
        PACK_BANK = (5, 6, 7, 5, 6, 7, 7, 7)
        w128 = lamc[:, 2:3]
        sq = xn_tm[:, :, :].rearrange("p (b c) d -> p b (c d)", b=B)
        hn = [t.rearrange("p (c n) -> p c n", n=FE * FH) for t in
              (big[:, 0:4096], Wtab[:, :, :].rearrange("p h n -> p (h n)"),
               Vbdx[:, :, :, :].rearrange("p b n v -> p (b n v)")[:, 0:2 * FE * FH])]
        hn = [hn[0][:, c, :] for c in range(CB)] + [hn[1 + c // 2][:, c % 2, :] for c in range(CB)]
        hidT = big[:, 4096:8192].rearrange("p (k n) -> p k n", k=8)
        hnT = aux[:, 0:1024].rearrange("p (b n) -> p b n", b=B)
        otm = aux[:, 1024:2048].rearrange("p (c n) -> p c n", c=NT)
        HB = (0, 2, 6)
        fsm = sb("fsm", [P, NT, FE])
        fw = sb("fw", [P, NT, FE])
        f1 = sb("f1", [P, NT])
        fst = sb("fst", [P, FE, 6])
        fmv = sb("fmv", [P, NT, FE, 2])
        fve = sb("fve", [P, NT, FE])
        frs = sb("frs", [P, NT, FE])
        fnm = sb("fnm", [P, NT, FE])

        @block.sync
        def _(sp):
            for b in range(B):
                sp.dma_start(x_tm[:, b * CB:(b + 1) * CB, :], x_v[:, b * CB:(b + 1) * CB, :]).then_inc(s(f"x_in{b}"), 16)
                if b == 0:
                    sp.dma_start(cst[:, :], consts).then_inc(s("in_first"), 16)
                    sp.dma_start(sidx_i, sidx).then_inc(s("in_first"), 16)
                    sp.dma_start(sm[:, :], small).then_inc(s("in_first"), 16)
            sp.dma_start(wa_sb[:, :], wa).then_inc(s("in_attn"), 16)
            sp.dma_start(colsb[:, :], cols).then_inc(s("in_attn"), 16)
            sp.dma_start(rowsb[:, :], rows).then_inc(s("in_attn"), 16)
            sp.dma_start(ctxT[:, :, :], ctxt).then_inc(s("in_ctx"), 16)
            sp.dma_start(wb_sb[:, :], wb).then_inc(s("in_ctx"), 16)
            sp.dma_start(bdx_sb, bdx).then_inc(s("in_ctx"), 16)
            sp.dma_start(tdr[:, :], tdrow).then_inc(s("in_ctx"), 16)
            sp.dma_start(ur[:, :], urow).then_inc(s("in_ctx"), 16)
            sp.dma_start(rw_sb[:, 0:E], rw).then_inc(s("in_moe"), 16)
            sp.dma_start(eb_sb[:, :], ebias).then_inc(s("in_moe"), 16)
            sp.dma_start(wm_sb[:, :], wm).then_inc(s("in_moe"), 16)
            sp.dma_start(wr_sb[:, :], wr).then_inc(s("in_last"), 16)
            sp.dma_start(rw_sb[:, E:E + FE], rwf).then_inc(s("in_last"), 16)
            sp.wait_ge(s("x_up"), NT)
            sp.dma_start(sel_sb, selx).then_inc(s("in_sel"), 16)
            sp.wait_ge(s("dn_ps"), B * NM)
            sp.dma_start(w1_sb, w1).then_inc(s("in_late"), 16)
            sp.dma_start(w2_sb, w2).then_inc(s("in_late"), 16)
            for b in range(B):
                sp.wait_ge(s("final"), b + 1)
                sp.dma_start(out_v[:, b * CB:(b + 1) * CB, :], otm[:, b * CB:(b + 1) * CB, :]).then_inc(s("stored"), 16)
            sp.wait_ge(s("stored"), 16 * B)

        def wait_x(eng, k, c):
            if k == 0:
                eng.wait_ge(s(f"x_in{c // CB}"), 16)
            else:
                eng.wait_ge(s("x_up"), NT * (k - 1) + c + 1)

        @block.tensor
        def _(pe):
            mm, tr = nc.tensor.matmul, nc.tensor.transpose

            def keep_warm(n, bank):
                for _ in range(n):
                    mm(ps[:, bank, :], const16[:, 0:P], const16[:, 0:512], start=True, stop=True)

            def ln_transpose(k, sem="xn", out_sem="xnT_ps", bank=6):
                for b in range(B):
                    for j in range(CB):
                        pe.wait_ge(s(sem), NT * k + CB * b + j + 1)
                        i = tr(ps[:, bank + b, j * P:(j + 1) * P], xn_tm[:, CB * b + j, :], ident)
                    i.then_inc(s(out_sem), 1)

            pe.wait_ge(s("filled"), 1)
            keep_warm(24, 0)
            pe.wait_ge(s("in_first"), 16 * 3)
            ln_transpose(0)
            pe.wait_ge(s("ohs"), 1)
            for b in range(B):
                for c in range(CB):
                    i = mm(ps[:, b, 0:NS], xn_tm[:, CB * b + c, :], ohs[:, c, :], start=(c == 0), stop=(c == CB - 1))
                i.then_inc(s("xsamp_ps"), 1)
            pe.wait_ge(s("in_attn"), 16 * 3)
            for b in range(B):
                pe.wait_ge(s("xsamp"), b + 1)
                mm(ps[:, 2 + b, 0:NS], w("a_k"), xsamp[:, b, :], start=True, stop=True).then_inc(s("ks_ps"), 1)
            for b in range(B):
                pe.wait_ge(s("xnT"), b + 1)
                mm(ps[:, 4 + b, :], w("a_q"), xnT[:, b, 1:S + 1], start=True, stop=True).then_inc(s("a_q_ps"), 1)
            for b in range(B):
                mm(ps[:, b, :], w("a_k"), xnT[:, b, 1:S + 1], start=True, stop=True).then_inc(s("a_k_ps"), 1)
            for b in range(B):
                pe.wait_ge(s("ks"), b + 1)
                for j in range(CB):
                    i = mm(ps[:, 2 + b, j * P:(j + 1) * P], xnchunk(CB * b + j), w("a_v"), start=True, stop=True)
                i.then_inc(s("a_v_ps"), 1)

            def pre_groups(l, banks):
                n0, nb = 9 * l, len(banks)
                mm(ps[:, banks[0], 0:B * NCP], w(f"x{l}_k"), ctxT[:, :, :].rearrange("p b n -> p (b n)"),
                   start=True, stop=True).then_inc(s("pre_ps"), 1)
                yield
                pe.wait_ge(s("ctxrep"), 1)
                for m, (kind, r) in enumerate(PRE_ORDER):
                    bank = banks[(m + 1) % nb]
                    if m + 1 >= nb:
                        pe.wait_ge(s("pre"), n0 + m + 2 - nb)
                    if kind == "k":
                        pe.wait_ge(s("kx"), l + 1)
                        for v in range(2):
                            o = ps[:, bank, v * B * NCP:(v + 1) * B * NCP]
                            q = 2 * r + v
                            mm(o, sel4[:, KH, q * P:(q + 1) * P], Kxh[:, :], start=True, stop=False)
                            i = mm(o, sel4[:, KL, q * P:(q + 1) * P], Kxl[:, :], start=False, stop=True)
                    else:
                        b, q = r // 3, r % 3
                        for n in range(4 * q, min(4 * q + 4, NB)):
                            i = mm(ps[:, bank, (n - 4 * q) * P:(n - 4 * q + 1) * P],
                                   ctxrep[:, b * NB * P + n * P:b * NB * P + (n + 1) * P], w(f"x{l}_v"), start=True, stop=True)
                    i.then_inc(s("pre_ps"), 1)
                    yield

            pre = pre_groups(0, (6,))

            def a_pack(m):
                b, g = m // G, m % G
                mm(ps[:, 6, :], sel4[:, QH, g * P:(g + 1) * P], Qh[:, b, :], start=True, stop=False)
                mm(ps[:, 6, :], sel4[:, QL, g * P:(g + 1) * P], Ql[:, b, :], start=False, stop=True).then_inc(s("a_pk_ps"), 1)

            def q_rows(b):
                for j in range(CB):
                    i = mm(ps[:, 6, j * P:(j + 1) * P], xnchunk(CB * b + j), w("a_q"), start=True, stop=True)
                i.then_inc(s("a_qt_ps"), 1)

            def a_keys(m):
                b, gg = m // 2, m % 2
                if m:
                    pe.wait_ge(s("a_bd"), 2 * m)
                for g in (2 * gg, 2 * gg + 1):
                    o = ps[:, 7, (g % 2) * NS:(g % 2 + 1) * NS]
                    mm(o, sel4[:, KH, g * P:(g + 1) * P], Ksh[:, b, :], start=True, stop=False)
                    i = mm(o, sel4[:, KL, g * P:(g + 1) * P], Ksl[:, b, :], start=False, stop=True)
                i.then_inc(s("a_kp_ps"), 1)

            pe.wait_ge(s("sel"), 1)
            pe.wait_ge(s("ksl"), B)
            a_keys(0)
            pe.wait_ge(s("a_ql"), B)
            a_pack(0)
            pe.wait_ge(s("a_q"), 2)
            pe.wait_ge(s("in_ctx"), 16 * 5)
            groups = 0
            for n in range(B * G * CB):
                m, j = n // CB, n % CB
                b, g = m // G, m % G
                pair = 4 - 2 * (n % 3)
                if j == 0:
                    pe.wait_ge(s("a_bd"), m + 1)
                    pe.wait_ge(s("a_qp"), m + 1)
                if n == 1:
                    pe.wait_ge(s("a_v"), 2)
                if n == 2:
                    pe.wait_ge(s("a_k"), 2)
                if n >= 3:
                    pe.wait_ge(s("mx"), n - 2)
                for v in range(2):
                    i = mm(ps[:, pair + v, :], Qp[:, g, b * S + j * P:b * S + (j + 1) * P],
                           bda[:, m % 4, 2 * v:2 * v + 2, :], start=True, stop=True)
                i.then_inc(s("as_ps"), 1)
                if n % 4 == 0 and m + 1 < B * G:
                    if groups:
                        pe.wait_ge(s("pre"), groups)
                    a_pack(m + 1)
                elif n in KEYS_AT:
                    a_keys(1 + KEYS_AT.index(n))
                elif n in PRE_AT:
                    pe.wait_ge(s("a_qp"), m + 2)
                    next(pre)
                    groups += 1
                elif n in QROWS_AT:
                    b = QROWS_AT.index(n)
                    if b == 0:
                        pe.wait_ge(s("a_qp"), B * G)
                        pe.wait_ge(s("pre"), 9)
                    else:
                        pe.wait_ge(s("a_qtl"), b)
                    q_rows(b)
            for _ in pre:
                pass
            pe.wait_ge(s("a_bd"), 2 * G)
            pe.wait_ge(s("kbar"), B)
            for c in range(NT):
                i = mm(ps[:, 7, c * H:(c + 1) * H], xchunk(c, QT), kbarbd[:, c // CB, :], start=True, stop=True)
            i.then_inc(s("mean_ps"), 1)
            pe.wait_ge(s("m"), 1)
            pe.wait_ge(s("a_qtl"), B)
            for c in range(CB):
                i = tr(ps[0:32, 6, c * P:(c + 1) * P], Mx[:, c, :, :].rearrange("p b h -> p (b h)"), ident)
            i.then_inc(s("mT_ps"), 1)
            for b in range(B):
                for c in range(CB):
                    mm(ps[:, 2, b * P:(b + 1) * P], inv_s, V_tm[:, CB * b + c, :], start=(c == 0), stop=(c == CB - 1))
                for c in range(CB):
                    i = mm(ps[:, 2, 256 + b:257 + b], V_tm[:, CB * b + c, :], inv_s[:, 0:1], start=(c == 0),
                           stop=(c == CB - 1))
                i.then_inc(s("vm_ps"), 1)
            pre = pre_groups(1, (3, 4, 5))
            for _ in range(PRE_FIRST):
                next(pre)
            for b in range(B):
                pe.wait_ge(s("diag"), b + 1)
                mm(ps[:, b, :], ones_r[:, :], diag[b], start=True, stop=True).then_inc(s("ib_ps"), 1)
            for _ in pre:
                pass
            pe.wait_ge(s("vm"), B)
            for b in range(B):
                pe.wait_ge(s("oh"), b + 1)
                if b == 1:
                    pe.wait_ge(s("pre"), 18)
                for c in range(CB):
                    mm(ps[:, 2 + b, :], Qh[:, b, c * P:(c + 1) * P], OH[:, CB * b + c, :], start=(c == 0), stop=False)
                    i = mm(ps[:, 2 + b, :], Ql[:, b, c * P:(c + 1) * P], OH[:, CB * b + c, :], start=False, stop=(c == CB - 1))
                i.then_inc(s("qs_ps"), 1)
            NG = B * G
            for n in range(NG + 3):
                if n < NG:
                    b, g = n // G, n % G
                    pe.wait_ge(s("qbd"), b + 1)
                    pe.wait_ge(s("a_exp"), n - 1) if n >= 2 else pe.wait_ge(s("oh"), B)
                    mm(ps[:, n % 2, :], Qbd[:, b, 4 * g:4 * g + 4, :].rearrange("p h n -> p (h n)"), KT[:, b, :],
                       start=True, stop=True).then_inc(s("ag_ps"), 1)
                m = n - 1
                if 0 <= m < NG:
                    b, g = m // G, m % G
                    pe.wait_ge(s("a_exp"), m + 1)
                    pe.wait_ge(s("pta"), m - 1) if m >= 2 else pe.wait_ge(s("qbd"), B)
                    for c in range(CB):
                        i = tr(ps[:, 2 + m % 2, c * P:(c + 1) * P], Pa[:, m % 2, c * P:(c + 1) * P], ident)
                    i.then_inc(s("pta_ps"), 1)
                m = n - 2
                if 0 <= m < NG:
                    b, g = m // G, m % G
                    pe.wait_ge(s("pta"), m + 1)
                    pe.wait_ge(s("dg"), m - 1) if m >= 2 else pe.wait_ge(s("qbd"), B)
                    for c in range(CB):
                        i = mm(ps[:, 4 + m % 2, 0:32], PTa[:, m % 2, c * P:(c + 1) * P],
                               V_tm[:, CB * b + c, 32 * g:32 * g + 32], start=(c == 0), stop=(c == CB - 1))
                    i.then_inc(s("pva_ps"), 1)
                m = n - 3
                if m >= 0:
                    b, g = m // G, m % G
                    pe.wait_ge(s("dg"), m + 1)
                    pe.wait_ge(s("oht"), m + 1)
                    i = mm(ps[32 * g:32 * g + 32, 6 + b, :], dg[:, m, :], OHT[:, m, :], start=True, stop=True)
                    if g == G - 1:
                        i.then_inc(s("ao_ps"), 1)
            for b in range(B):
                pe.wait_ge(s("a_at"), b + 1)
                for c in range(CB * b, CB * b + CB):
                    i = mm(ps[:, b, (c % CB) * P:(c % CB + 1) * P], xchunk(c, attnT), w("a_o"), start=True, stop=True)
                i.then_inc(s("a_op_ps"), 1)

            def context(l, k):
                L = f"x{l}"
                keep_warm(8, 2)
                ln_transpose(k)
                keep_warm(3, 2)
                for b in range(B):
                    pe.wait_ge(s("xnT"), 2 * k + b + 1)
                    mm(ps[:, 4 + b, :], w(f"{L}_q"), xnT[:, b, 1:S + 1], start=True, stop=True).then_inc(s("x_q_ps"), 1)

                def pack(m):
                    b, g = m // G, m % G
                    pe.wait_ge(s("x_ql"), 2 * l + b + 1)
                    if m >= G + 2:
                        pe.wait_ge(s(("x_qp_a", "x_qp_v")[m % 2]), 4 * l + m // 2)
                    o = ps[:, m if b == 0 else 6 + m % 2, :]
                    mm(o, sel4[:, QH, g * P:(g + 1) * P], Qh[:, b, :], start=True, stop=False)
                    mm(o, sel4[:, QL, g * P:(g + 1) * P], Ql[:, b, :], start=False, stop=True).then_inc(s("x_pk_ps"), 1)

                for m in range(G):
                    pack(m)
                pe.wait_ge(s("x_qp_a"), 4 * l + 2)
                pe.wait_ge(s("x_qp_v"), 4 * l + 2)
                if l == 0:
                    pe.wait_ge(s("pre"), 9)
                else:
                    pe.wait_ge(s("x1_keys"), 4)
                for n in range(NT + 4):
                    if n < NT:
                        for u in range(2):
                            m = 2 * n + u
                            if m >= 2:
                                pe.wait_ge(s("x_sub"), 16 * l + m - 1)
                            for v in range(2):
                                g, b = 2 * u + v, n // CB
                                i = mm(ps[:, g, 0:4 * NCP], Qp[:, g, n * P:(n + 1) * P],
                                       Kbp[:, g, :, b * NCP:(b + 1) * NCP], start=True, stop=True)
                            i.then_inc(s("x_s_ps"), 1)
                    if n < 2:
                        pack(G + 2 * n)
                        pack(G + 2 * n + 1)
                    if n == 2:
                        pe.wait_ge(s("x_qp_a"), 4 * l + 4)
                        pe.wait_ge(s("x_qp_v"), 4 * l + 4)
                        pe.wait_ge(s("vbdx"), 2 * l + 2)
                    c = n - 4
                    if c >= 0:
                        pe.wait_ge(s("x_at"), 8 * l + c + 1)
                        mm(ps[:, 6 + c % 2, 384:512], xchunk(c, attnT), w(f"{L}_o"), start=True,
                           stop=True).then_inc(s("x_op_ps"), 1)
                    c = n - 1
                    if 0 <= c < NT:
                        pe.wait_ge(s("x_exp"), 16 * l + 2 * c + 2)
                        for q in range(3):
                            r = 3 * c + q
                            if r >= 2:
                                pe.wait_ge(s("x_pt"), 24 * l + r - 1)
                            for t in range(4 * q, min(4 * q + 4, NB)):
                                wd = P if t < NB - 1 else LB
                                i = tr(ps[0:wd, 4 + r % 2, (t - 4 * q) * P:(t - 4 * q + 1) * P],
                                       Ssb[:, c % 2, t * P:t * P + wd], ident)
                            i.then_inc(s("x_pt_ps"), 1)
                    c = n - 2
                    if 0 <= c < NT:
                        pe.wait_ge(s("x_pt"), 24 * l + 3 * c + 3)
                        if c >= 2:
                            pe.wait_ge(s("x_up"), (1 + 3 * l) * NT + c - 1)
                        for t in range(NB):
                            wd = P if t < NB - 1 else LB
                            i = mm(ps[:, 6 + c % 2, 0:VW], PTx[0:wd, c % 2, t * P:(t + 1) * P],
                                   Vbdx[0:wd, c // CB, t, :], start=(t == 0), stop=(t == NB - 1))
                        i.then_inc(s("x_pv_ps"), 1)
                    c = n - 3
                    if 0 <= c < NT:
                        pe.wait_ge(s("x_atm"), 8 * l + c + 1)
                        tr(ps[:, 6 + c % 2, 256:384], atm[:, c % 4, :], ident).then_inc(s("x_at_ps"), 1)

            context(0, 1)

            keep_warm(8, 0)
            pe.wait_ge(s("x_up"), 2 * NT)
            ln_transpose(2)
            keep_warm(3, 0)
            pe.wait_ge(s("in_moe"), 16 * 3)
            for b in range(B):
                pe.wait_ge(s("xnT"), 2 * 2 + b + 1)
                for c in range(CB * b, CB * b + CB):
                    i = mm(ps[:, 4, c * E:(c + 1) * E], xnchunk(c), rw_sb[:, 0:E], start=True, stop=True)
            i.then_inc(s("rl_ps"), 1)

            def gate_up(n):
                b, i = n // NM, n % NM
                if n >= 2:
                    pe.wait_ge(s("m_h1"), n - 1)
                mm(ps[:, n % 2, :], wm_sb[:, i * P:(i + 1) * P], xnT[:, b, 1:S + 1], start=True,
                   stop=True).then_inc(s("g_ps"), 1)
                mm(ps[:, 2 + n % 2, :], wm_sb[:, (NM + i) * P:(NM + i + 1) * P], xnT[:, b, 1:S + 1], start=True,
                   stop=True).then_inc(s("u_ps"), 1)

            def expand(n):
                b, i = n // NM, n % NM
                if i < NM - 1:
                    m = b * (NM - 1) + i
                    pe.wait_ge(s("combT"), 3 * b + 3)
                    if m >= 2:
                        pe.wait_ge(s("m_h2"), m - 1)
                    mm(ps[:, 4 + m % 2, :], sel_sb[:, i * P:(i + 1) * P], combr[:, b * S:(b + 1) * S], start=True,
                       stop=True).then_inc(s("w_ps"), 1)

            def down(n):
                b, i = n // NM, n % NM
                if i < NM - 1:
                    pe.wait_ge(s("m_h2"), b * (NM - 1) + i + 1)
                else:
                    pe.wait_ge(s("m_h1"), n + 1)
                for c in range(CB):
                    r = mm(ps[:, 6 + b, c * P:(c + 1) * P], hs[:, n % NHS, c * P:(c + 1) * P],
                           wm_sb[:, (2 * NM + i) * P:(2 * NM + i + 1) * P], start=(i == 0 and c == 0),
                           stop=(i == NM - 1), skip_group_check=True)
                r.then_inc(s("dn_ps"), 1)

            NN = B * NM
            for n in range(BEFORE):
                gate_up(n)
            pe.wait_ge(s("xnT"), 2 * 2 + B)
            for b in range(B):
                pe.wait_ge(s("comb"), b + 1)
                for c in range(CB):
                    i = tr(ps[0:E, 5 + 2 * b, c * P:(c + 1) * P], comb[:, CB * b + c, :], ident)
                i.then_inc(s("cT_ps"), 1)
            for n in range(BEFORE, AHEAD):
                gate_up(n)
            pe.wait_ge(s("in_sel"), 16)
            for n in range(NN + 1):
                if n < NN:
                    expand(n)
                if n >= 1:
                    down(n - 1)
                if 1 <= n <= NN - AHEAD:
                    gate_up(n + AHEAD - 1)

            keep_warm(8, 4)
            pe.wait_ge(s("x_up"), 3 * NT)
            ln_transpose(3)
            keep_warm(3, 4)
            pe.wait_ge(s("in_last"), 16 * 2)

            def r_project(b):
                mk, mv_, mr, mg = (mixes[:, i, b, :] for i in range(4))
                pe.wait_ge(s("mix"), 4 * b + 2)
                if b:
                    pe.wait_ge(s("r_kv"), 3)
                mm(ps[:, 0, :], w("w_r"), mr, start=True, stop=True).then_inc(s("r_pj_ps"), 1)
                pe.wait_ge(s("mix"), 4 * b + 3)
                mm(ps[:, 1, :], w("w_k"), mk, start=True, stop=True).then_inc(s("r_pj_ps"), 1)
                if b:
                    pe.wait_ge(s("r_kv"), 4)
                for j in range(CB):
                    i = mm(ps[:, 2, j * P:(j + 1) * P], mk[:, j * P:(j + 1) * P], w("w_k"), start=True, stop=True)
                i.then_inc(s("r_pj_ps"), 1)
                pe.wait_ge(s("mix"), 4 * b + 4)
                if b:
                    pe.wait_ge(s("r_kv"), 5)
                for j in range(CB):
                    i = mm(ps[:, 3, j * P:(j + 1) * P], mv_[:, j * P:(j + 1) * P], w("w_v"), start=True, stop=True)
                i.then_inc(s("r_pj_ps"), 1)
                pe.wait_ge(s("mix_g"), b + 1)
                if b:
                    pe.wait_ge(s("r_g"), 1)
                mm(ps[:, 4, :], w("w_g"), mg, start=True, stop=True).then_inc(s("r_pj_ps"), 1)

            def r_pack(m):
                b, g = m // G, m % G
                pe.wait_ge(s("r_kv"), 5 * b + 2)
                bank = PACK_BANK[m]
                before = [k for k in range(m) if PACK_BANK[k] == bank]
                if before:
                    pe.wait_ge(s("r_kp"), before[-1] + 1)
                mm(ps[:, bank, :], sel4[:, KH, g * P:(g + 1) * P], Kh[:, b, :], start=True, stop=False)
                mm(ps[:, bank, :], sel4[:, KL, g * P:(g + 1) * P], Kl[:, b, :], start=False, stop=True).then_inc(s("r_pk_ps"), 1)

            def r_rows(c):
                b, cs = c // CB, slice((c % CB) * P, (c % CB + 1) * P)
                pe.wait_ge(s("r_kv"), 5 * b + 1)
                if c:
                    pe.wait_ge(s("rbd"), c)
                for g in range(G):
                    o = ps[:, 4, g * P:(g + 1) * P]
                    mm(o, sel4[:, QH, g * P:(g + 1) * P], Rh[b][:, cs], start=True, stop=False)
                    i = mm(o, sel4[:, QL, g * P:(g + 1) * P], Rl[b][:, cs], start=False, stop=True)
                i.then_inc(s("r_rows_ps"), 1)

            def r_scores(c):
                pe.wait_ge(s("rbd"), c + 1)
                pe.wait_ge(s("r_kp"), G * (c // CB + 1))
                for q in range(4):
                    if c >= 1:
                        pe.wait_ge(s("r_p"), 4 * (c - 1) + q + 1)
                    mm(ps[:, q, :], Qp[:, q, c * P:(c + 1) * P], Rbd[:, c % 2, q, :, :], start=True,
                       stop=True).then_inc(s("r_s_ps"), 1)
                if c % CB < CB - 1:
                    if c >= 1:
                        pe.wait_ge(s("um"), c - c // CB)
                    mm(ps[:, 5, 0:P], Ktm[:, c, :], V_tm[:, c, :], start=True, stop=True).then_inc(s("u_st_ps"), 1)

            def r_out(c):
                b, j = c // CB, c % CB
                y = ps[:, 6 + b, j * P:(j + 1) * P]
                if j:
                    pe.wait_ge(s("state"), b * (CB - 1) + j)
                    mm(y, St[:, (b * (CB - 1) + j - 1) % 2, :], xchunk(c, Rw), start=False, stop=False, skip_group_check=True)
                pe.wait_ge(s("vx"), c + 1)
                for h in range(H):
                    if h % 4 == 0:
                        pe.wait_ge(s("r_p"), 4 * c + h // 4 + 1)
                    i = mm(y, Vx[:, c % 2, h, :], Pr[:, c % 2, h, :], start=(j == 0 and h == 0), stop=(h == H - 1),
                           skip_group_check=True)
                i.then_inc(s("y_ps"), 1)

            def r_mean(b):
                pe.wait_ge(s("r_y"), b + 1)
                mm(ps[:, 6 + b, :], bdiag, yc[:, b, :], start=True, stop=True).then_inc(s("r_mean_ps"), 1)

            def r_variance(b):
                pe.wait_ge(s("r_sq"), b + 1)
                for j in range(CB):
                    i = mm(ps[:, 6 + b, j * H:(j + 1) * H], sq[:, b, j * P:(j + 1) * P], hmask, start=True, stop=True)
                i.then_inc(s("r_var_ps"), 1)

            def r_spread(b):
                pe.wait_ge(s("r_rs"), b + 1)
                for j in range(CB):
                    i = mm(ps[:, 6 + b, j * P:(j + 1) * P], gx[b][:, j * P:(j + 1) * P],
                           ident, start=True, stop=True)
                i.then_inc(s("r_sp_ps"), 1)

            def r_output(b):
                pe.wait_ge(s("r_yg"), b + 1)
                for c in range(CB * b, CB * b + CB):
                    i = mm(ps[:, 4 + b, (c % CB) * P:(c % CB + 1) * P], xchunk(c, yc), w("w_o"), start=True, stop=True)
                i.then_inc(s("r_op_ps"), 1)

            r_project(0)
            pe.wait_ge(s("xnT"), 8)
            for m in range(G):
                r_pack(m)
            r_project(1)
            pe.wait_ge(s("r_g"), B)
            r_rows(0)
            pe.wait_ge(s("r_kv"), 5 * B)
            for c in range(NT + 1):
                if c < NT:
                    r_scores(c)
                if c + 1 < NT:
                    r_rows(c + 1)
                if c == 1:
                    pe.wait_ge(s("r_kp"), 5)
                if c >= 1:
                    r_out(c - 1)
                if c < 3:
                    for m in ((4, 5), (6,), (7,))[c]:
                        r_pack(m)
                if c == CB + 1:
                    r_mean(0)
                if c == CB + 2:
                    r_variance(0)
            r_spread(0)
            r_mean(1)
            r_variance(1)
            r_output(0)
            r_spread(1)
            r_output(1)

            context(1, 4)

            keep_warm(8, 0)
            pe.wait_ge(s("x_up"), 5 * NT)
            ln_transpose(5)
            keep_warm(3, 0)
            pe.wait_ge(s("in_late"), 16 * 2)
            pe.wait_ge(s("xnT"), 12)

            def f_hidden(c):
                if c >= 3:
                    pe.wait_ge(s("f_hn"), 3 * (c - 2))
                    pe.wait_ge(s("f_hv"), c - 2)
                for v in range(2):
                    i = mm(ps[:, HB[c % 3] + v, :], xnchunk(c), w1_sb[:, v * 512:(v + 1) * 512], start=True, stop=True)
                i.then_inc(s("f_h_ps"), 1)

            def f_turn(b, qs):
                pe.wait_ge(s("f_hn"), 3 * CB * (b + 1))
                pe.wait_ge(s("f_hv"), CB * (b + 1))
                for q in qs:
                    r = 8 * b + q
                    if r >= 2:
                        pe.wait_ge(s("f_hT"), r - 1)
                    for j in range(CB):
                        i = tr(ps[:, 4 + r % 2, j * P:(j + 1) * P], hn[CB * b + j][:, q * P:(q + 1) * P], ident)
                    i.then_inc(s("f_hT_ps"), 1)

            def f_down(b):
                pe.wait_ge(s("f_hT"), 8 * (b + 1))
                for j in range(CB):
                    c = CB * b + j
                    if c == 0:
                        pe.wait_ge(s("f_hn"), 3 * 6)
                        pe.wait_ge(s("f_hv"), 6)
                    if c >= 2:
                        pe.wait_ge(s("f_cmb"), c - 1)
                    for e in range(FE):
                        for v in range(2):
                            i = mm(ps[:, 6 + c % 2, e * P:(e + 1) * P], hidT[:, 2 * e + v, j * P:(j + 1) * P],
                                   w2_sb[:, (2 * e + v) * P:(2 * e + v + 1) * P], start=(v == 0), stop=(v == 1))
                    i.then_inc(s("f_o_ps"), 1)

            f_hidden(0)
            f_hidden(1)
            ln_transpose(0, sem="hn2", out_sem="hnT_ps", bank=4)
            f_hidden(2)
            pe.wait_ge(s("in_last"), 16 * 2)
            pe.wait_ge(s("hnT"), 2)
            for c in range(NT):
                i = mm(ps[:, 5, c * FE:(c + 1) * FE], hnT[:, c // CB, (c % CB) * P:(c % CB + 1) * P],
                       rw_sb[:, E:E + FE], start=True, stop=True)
            i.then_inc(s("fl_ps"), 1)
            f_hidden(3)
            f_hidden(4)
            pe.wait_ge(s("fsub"), 1)
            f_turn(0, range(4))
            f_hidden(5)
            f_hidden(6)
            f_turn(0, range(4, 8))
            f_hidden(7)
            f_down(0)
            f_turn(1, range(8))
            f_down(1)

        @block.scalar
        def _(act):
            A = nc.scalar.activation

            def ln_copy(k):
                for b in range(B):
                    if k == 0 and b == 0:
                        act.wait_ge(s("filled"), 2)
                    act.wait_ge(s("xnT_ps"), 2 * k + b + 1)
                    A(xnT[:, b, 1:S + 1], ps[:, 6 + b, :], ACT.Copy).then_inc(s("xnT"), 1)

            ln_copy(0)
            for b in range(B):
                act.wait_ge(s("xsamp_ps"), b + 1)
                A(xsamp[:, b, :], ps[:, b, 0:NS], ACT.Copy).then_inc(s("xsamp"), 1)
            act.wait_ge(s("in_attn"), 16 * 3)
            for b in range(B):
                act.wait_ge(s("ks_ps"), b + 1)
                A(KsT[:, b, :], ps[:, 2 + b, 0:NS], ACT.Identity, bias=col("a_bk")).then_inc(s("ks"), 1)
            for b in range(B):
                act.wait_ge(s("ks"), b + 1)
                A(Ksh[:, b, :], KsT[:, b, :], ACT.Copy).then_inc(s("ksh"), 1)
            for b in range(B):
                act.wait_ge(s("a_q_ps"), b + 1)
                A(QT[:, b, :], ps[:, 4 + b, :], ACT.Identity, bias=col("a_bq")).then_inc(s("a_q"), 1)
                act.wait_ge(s("a_q"), b + 1)
                A(Qh[:, b, :], QT[:, b, :], ACT.Copy).then_inc(s("a_qh"), 1)
            act.wait_ge(s("in_first"), 16 * 3)

            def key_blocks(m):
                act.wait_ge(s("a_kp_ps"), m + 1)
                for v in range(2):
                    u = 2 * m + v
                    if u >= 4:
                        act.wait_ge(s("as_ps"), CB * (u - 3))
                    for j in range(4):
                        i = A(bda[:, u % 4, j, :], ps[:, 7, v * NS:(v + 1) * NS], ACT.Copy, scale=quad[:, j:j + 1])
                    i.then_inc(s("a_bd"), 1)

            def query_rows(m):
                act.wait_ge(s("a_pk_ps"), m + 1)
                A(Qp[:, m % G, (m // G) * S:(m // G + 1) * S], ps[:, 6, :], ACT.Copy).then_inc(s("a_qp"), 1)

            key_blocks(0)
            query_rows(0)
            for b in range(B):
                act.wait_ge(s("a_k_ps"), b + 1)
                A(KT[:, b, :], ps[:, b, :], ACT.Identity, bias=col("a_bk")).then_inc(s("a_k"), 1)

            def pre_copies(l, banks):
                n0, nb = 9 * l, len(banks)
                act.wait_ge(s("pre_ps"), n0 + 1)
                A(Kx[:, :], ps[:, banks[0], 0:B * NCP], ACT.Identity, bias=col(f"x{l}_bk")).then_inc(s("pre"), 1)
                yield
                for m, (kind, r) in enumerate(PRE_ORDER):
                    bank = banks[(m + 1) % nb]
                    act.wait_ge(s("pre_ps"), n0 + m + 2)
                    if kind == "k" and l == 1:
                        i = A(Kpk[:, 2 * r:2 * r + 2, :], ps[:, bank, 0:2 * B * NCP].rearrange("p (g n) -> p g n", g=2), ACT.Copy)
                    elif kind == "k":
                        for j in range(4):
                            i = A(Kbp[:, 2 * r:2 * r + 2, j, :], ps[:, bank, 0:2 * B * NCP].rearrange("p (g n) -> p g n", g=2),
                                  ACT.Copy, scale=quad[:, j:j + 1])
                    else:
                        b, q = r // 3, r % 3
                        n = min(4, NB - 4 * q)
                        i = A(Vbdx[:, b, 4 * q:4 * q + n, 0:P] if l == 0 else Vraw[:, b, 4 * q:4 * q + n, :],
                              ps[:, bank, 0:n * P].rearrange("p (n d) -> p n d", d=P), ACT.Copy)
                    i.then_inc(s("pre"), 1)
                    yield

            pre = pre_copies(0, (6,))
            for n in range(B * G * CB):
                m = n // CB
                if n % 4 == 0 and m + 1 < B * G:
                    query_rows(m + 1)
                elif n in KEYS_AT:
                    key_blocks(1 + KEYS_AT.index(n))
                elif n in PRE_AT:
                    next(pre)
                elif n in QROWS_AT:
                    b = QROWS_AT.index(n)
                    act.wait_ge(s("a_qt_ps"), b + 1)
                    A(Qh[:, b, :], ps[:, 6, :], ACT.Copy).then_inc(s("a_qth"), 1)
                if n == 5:
                    act.wait_ge(s("in_ctx"), 16 * 5)
                    A(lamr[:, :], tdr[:, :], ACT.Exp).then_inc(s("lam"), 1)
                    A(lamc[:, 0:1], col("td"), ACT.Exp).then_inc(s("lam"), 1)
            act.wait_ge(s("lam_ok"), 4)
            A(rpow[:, :], trow, ACT.Exp, scale=lamc[:, 1:2]).then_inc(s("tabs"), 1)
            A(kpow[:, :], lamr[:, :], ACT.Exp, scale=ncol).then_inc(s("tabs"), 1)
            A(w128, lamc[:, 1:2], ACT.Exp, scale=float(P)).then_inc(s("tabs"), 1)
            act.wait_ge(s("gap"), 1)
            A(Wtab[:, :, :], Wtab[:, :, :], ACT.Exp, scale=-1.0).then_inc(s("wexp"), 1)
            act.wait_ge(s("mT_ps"), 1)
            A(MT[:, 0, :], ps[0:32, 6, :], ACT.Copy).then_inc(s("mT"), 1)
            act.wait_ge(s("vm_ps"), B)
            A(Vmb[:, :, :].rearrange("p b d -> p (b d)"), ps[:, 2, 0:2 * P], ACT.Copy).then_inc(s("vm"), 1)
            A(Vmc[:, :], ps[:, 2, 256:256 + B], ACT.Copy).then_inc(s("vm"), 1)
            for _ in pre_copies(1, (3, 4, 5)):
                pass
            for n in range(B * G + 1):
                if n < B * G:
                    act.wait_ge(s("nb"), n + 1)
                    if n >= 2:
                        act.wait_ge(s("pta_ps"), n - 1)
                    A(Pa[:, n % 2, :], ps[:, n % 2, :], ACT.Exp, bias=nb[:, n:n + 1], scale=ASCALE,
                      accum_out=rsum[:, n:n + 1]).then_inc(s("a_exp"), 1)
                m = n - 1
                if m >= 0:
                    act.wait_ge(s("pta_ps"), m + 1)
                    if m >= 2:
                        act.wait_ge(s("pva_ps"), m - 1)
                    A(PTa[:, m % 2, :], ps[:, 2 + m % 2, :], ACT.Copy).then_inc(s("pta"), 1)
            for b in range(B):
                act.wait_ge(s("ao_ps"), b + 1)
                A(attnT[:, b, :], ps[:, 6 + b, :], ACT.Identity, bias=Vmc[:, b:b + 1]).then_inc(s("a_at"), 1)

            def context(l, k):
                L = f"x{l}"
                ln_copy(k)
                for b in range(B):
                    act.wait_ge(s("x_q_ps"), 2 * l + b + 1)
                    A(Qh[:, b, :], ps[:, 4 + b, :], ACT.Identity, bias=col(f"{L}_bq")).then_inc(s("x_qh"), 1)

                def packed(m):
                    act.wait_ge(s("x_pk_ps"), 8 * l + m + 1)
                    A(Qp[:, m % G, (m // G) * S:(m // G + 1) * S], ps[:, m if m < G else 6 + m % 2, :],
                      ACT.Copy).then_inc(s("x_qp_a"), 1)

                packed(0)
                packed(2)
                for n in range(NT + 3):
                    if n < 2:
                        packed(G + 2 * n)
                    c = n - 1
                    if 0 <= c < NT:
                        for q in range(3):
                            r = 3 * c + q
                            act.wait_ge(s("x_pt_ps"), 24 * l + r + 1)
                            if c >= 2 and q == 0:
                                act.wait_ge(s("x_pv_ps"), 8 * l + c - 1)
                            t0, t1 = 4 * q, min(4 * q + 4, NB)
                            if q < 2:
                                A(PTx[:, c % 2, t0 * P:t1 * P], ps[:, 4 + r % 2, :], ACT.Copy).then_inc(s("x_pt"), 1)
                            else:
                                A(PTx[:, c % 2, t0 * P:(t1 - 1) * P], ps[:, 4 + r % 2, 0:P], ACT.Copy)
                                A(PTx[0:LB, c % 2, (t1 - 1) * P:t1 * P], ps[0:LB, 4 + r % 2, P:2 * P],
                                  ACT.Copy).then_inc(s("x_pt"), 1)
                    if n < NT:
                        for u in range(2):
                            act.wait_ge(s("x_sub"), 16 * l + 2 * n + u + 1)
                            v = Ssb[:, n % 2, u * 8 * NC:(u + 1) * 8 * NC]
                            A(v, v, ACT.Exp, scale=ASCALE).then_inc(s("x_exp"), 1)
                    c = n - 3
                    if c >= 0:
                        act.wait_ge(s("x_at_ps"), 8 * l + c + 1)
                        A(xchunk(c, attnT), ps[:, 6 + c % 2, 256:384], ACT.Copy).then_inc(s("x_at"), 1)

            context(0, 1)

            ln_copy(2)
            act.wait_ge(s("rl_ps"), 1)
            A(sg[:, :, :].rearrange("p c e -> p (c e)"), ps[:, 4, 0:NT * E], ACT.Exp, scale=-1.0).then_inc(s("m_en"), 1)

            def silu(n):
                act.wait_ge(s("g_ps"), n + 1)
                if n >= NHS:
                    act.wait_ge(s("dn_ps"), n - NHS + 1)
                A(hs[:, n % NHS, :], ps[:, n % 2, :], ACT.Silu).then_inc(s("m_silu"), 1)

            for n in range(B * NM):
                silu(n)

            ln_copy(3)
            def r_copies(b):
                act.wait_ge(s("r_pj_ps"), 5 * b + 1)
                if b:
                    act.wait_ge(s("r_pk_ps"), G)
                A(Rh[b], ps[:, 0, :], ACT.Copy).then_inc(s("r_rh"), 1)
                act.wait_ge(s("r_pj_ps"), 5 * b + 2)
                A(Kh[:, b, :], ps[:, 1, :], ACT.Copy).then_inc(s("r_kh"), 1)
                act.wait_ge(s("r_pj_ps"), 5 * b + 5)
                A(GT[:, b, :], ps[:, 4, :], ACT.Silu).then_inc(s("r_g"), 1)

            def r_packed(m):
                act.wait_ge(s("r_pk_ps"), m + 1)
                A(Qp[:, m % G, (m // G) * S:(m // G + 1) * S], ps[:, PACK_BANK[m], :],
                  ACT.Copy).then_inc(s("r_kp"), 1)

            def r_sum(b):
                act.wait_ge(s("y_ps"), CB * (b + 1))
                A(yc[:, b, :], ps[:, 6 + b, :], ACT.Copy).then_inc(s("r_y"), 1)

            def r_deviation(b):
                act.wait_ge(s("r_var"), b + 1)
                A(gn[:, b, :], gv[:, b, :], ACT.Sqrt).then_inc(s("r_sd"), 1)

            r_copies(0)
            for m in range(G):
                r_packed(m)
            r_copies(1)
            for c in range(NT):
                act.wait_ge(s("r_rows_ps"), c + 1)
                if c >= 2:
                    act.wait_ge(s("r_s_ps"), 4 * (c - 1))
                for j in range(4):
                    i = A(Rbd[:, c % 2, :, j, :], ps[:, 4, :].rearrange("p (g t) -> p g t", g=G), ACT.Copy,
                          scale=quad[:, j:j + 1])
                i.then_inc(s("rbd"), 1)
                if 1 <= c <= 3:
                    for m in ((4, 5), (6,), (7,))[c - 1]:
                        r_packed(m)
                if c == CB + 1:
                    r_sum(0)
            r_deviation(0)
            r_sum(1)
            r_deviation(1)

            context(1, 4)

            ln_copy(5)
            for b in range(B):
                act.wait_ge(s("hnT_ps"), b + 1)
                A(hnT[:, b, :], ps[:, 4 + b, :], ACT.Identity, scale=col("rn_g"), bias=col("rn_b")).then_inc(s("hnT"), 1)

            def f_norm(c):
                act.wait_ge(s("f_st"), c + 1)
                for e in range(FE - 1):
                    if e == 2:
                        act.wait_ge(s("f_hv"), c + 1)
                    A(hn[c][:, e * FH:(e + 1) * FH], ps[:, HB[c % 3] + e // 2, (e % 2) * FH:(e % 2 + 1) * FH],
                      ACT.Identity, scale=frs[:, c, e:e + 1], bias=fnm[:, c, e:e + 1]).then_inc(s("f_hn"), 1)

            def f_relu(b, q):
                act.wait_ge(s("f_hT_ps"), 8 * b + q + 1)
                if b == 1 and q == 0:
                    act.wait_ge(s("f_o_ps"), CB)
                A(hidT[:, q, :], ps[:, 4 + (8 * b + q) % 2, :], ACT.Relu, scale=colsb[:, len(COLS) + q:len(COLS) + q + 1],
                  bias=colsb[:, len(COLS) + 8 + q:len(COLS) + 9 + q]).then_inc(s("f_hT"), 1)

            f_norm(0)
            f_norm(1)
            act.wait_ge(s("fsub"), 1)
            A(fsm[:, :, :], fsm[:, :, :], ACT.Exp).then_inc(s("fexp"), 1)
            f_norm(2)
            f_norm(3)
            for j in range(CB):
                f_relu(0, 2 * j)
                f_relu(0, 2 * j + 1)
                f_norm(CB + j)
            for q in range(8):
                f_relu(1, q)

        @block.vector
        def _(dve):
            V = nc.vector
            chain = [0]

            def link(ins):
                chain[0] += 1
                ins.then_inc(s("dve_chain"), 1)
                dve.wait_ge(s("dve_chain"), chain[0])

            def ln_stats(k, b):
                cs = range(CB * b, CB * b + CB)
                for c in cs:
                    wait_x(dve, k, c)
                    i = V.bn_stats(st[:, c, :], x_tm[:, c, :])
                link(i)
                for c in cs:
                    i = V.bn_aggr(mv[:, c, :], st[:, c, :])
                link(i)
                V.tensor_scalar(veps[:, CB * b:CB * b + CB], mv[:, CB * b:CB * b + CB, 1], 1e-5, None,
                                ALU.add).then_inc(s("veps"), 1)

            def ln_norm(k, b):
                dve.wait_ge(s("rstd"), 2 * k + b + 1)
                for c in range(CB * b, CB * b + CB):
                    V.tensor_scalar(xn_tm[:, c, :], x_tm[:, c, :], mv[:, c, 0:1], rstd[:, c:c + 1],
                                    ALU.subtract, ALU.mult).then_inc(s("xn"), 1)

            def add_residual(bank, b, sem, ops):
                dve.wait_ge(s(ops), b + 1)
                cs = slice(CB * b, CB * b + CB)
                V.tensor_tensor(x_tm[:, cs, :], ps[:, bank, :].rearrange("p (c d) -> p c d", c=CB), x_tm[:, cs, :],
                                ALU.add).then_inc(s(sem), CB)

            ln_stats(0, 0)
            dve.wait_ge(s("in_first"), 16 * 3)
            link(V.tensor_copy(sidx_f, sidx_i))
            for c in range(CB):
                i = V.tensor_scalar(ohs[:, c, :], sidx_f, iota_pc[:, c:c + 1], None, ALU.is_equal)
            i.then_inc(s("ohs"), 1)
            ln_stats(0, 1)
            ln_norm(0, 0)
            ln_norm(0, 1)
            for b in range(B):
                dve.wait_ge(s("ksh"), b + 1)
                V.tensor_tensor(Ksl[:, b, :], KsT[:, b, :], Ksh[:, b, :].bitcast(F32), ALU.subtract).then_inc(s("ksl"), 1)
            for b in range(B):
                dve.wait_ge(s("a_qh"), b + 1)
                V.tensor_tensor(Ql[:, b, :], QT[:, b, :], Qh[:, b, :].bitcast(F32), ALU.subtract).then_inc(s("a_ql"), 1)
            dve.wait_ge(s("in_attn"), 16 * 3)
            for b in range(B):
                dve.wait_ge(s("a_v_ps"), b + 1)
                V.tensor_tensor(V_tm[:, CB * b:CB * b + CB, :], ps[:, 2 + b, :].rearrange("p (c d) -> p c d", c=CB),
                                row("a_bv").unsqueeze(1).broadcast_to([P, CB, D]), ALU.add).then_inc(s("a_v"), 1)
            for b in range(B):
                link(V.reduce_sum(kbar[:, b:b + 1], KsT[:, b, :], AXX))
                V.tensor_scalar(kbarbd[:, b, :], hmask, kbar[:, b:b + 1], 1.0 / NS, ALU.mult, ALU.mult).then_inc(s("kbar"), 1)
            for n in range(B * G * CB):
                m, j = n // CB, n % CB
                b, g = m // G, m % G
                pair = 4 - 2 * (n % 3)
                dve.wait_ge(s("as_ps"), n + 1)
                V.tensor_reduce(Mx[:, j, b, 4 * g:4 * g + 4],
                                ps[:, pair:pair + 2, :].rearrange("p v (h n) -> p (v h) n", n=NS),
                                AXX, ALU.max).then_inc(s("mx"), 1)
                if n - 2 in QROWS_AT:
                    q = QROWS_AT.index(n - 2)
                    dve.wait_ge(s("a_qth"), q + 1)
                    V.tensor_tensor(Ql[:, q, :], ps[:, 6, :], Qh[:, q, :].bitcast(F32), ALU.subtract).then_inc(s("a_qtl"), 1)
            dve.wait_ge(s("mx"), 4 * NT)
            dve.wait_ge(s("mean_ps"), 1)
            V.tensor_tensor(Mx[:, :, :, :], Mx[:, :, :, :],
                            ps[:, 7, 0:NT * H].rearrange("p (b c h) -> p c b h", b=B, c=CB), ALU.subtract).then_inc(s("m"), 1)
            dve.wait_ge(s("mT"), 1)
            for r in range(4):
                cur, nxt = MT[:, r % 2, :], MT[:, 1 - r % 2, :]
                v = v8[:, 8 * r:8 * r + 8]
                link(V.max(v, cur))
                i = V.max_index(idx[:, 8 * r:8 * r + 8], v, cur)
                if r == 3:
                    link(i)
                else:
                    link(V.match_replace(nxt, v, cur, NEG))
            link(V.tensor_copy(idxf[:, :], idx[:, :]))
            for b in range(B):
                V.tensor_tensor(diag[b].rearrange("p (h n) -> p h n", h=H), idxf[:, :].unsqueeze(1).broadcast_to([32, H, SLOTS]),
                                ident[0:32, H * b:H * (b + 1)].unsqueeze(2).broadcast_to([32, H, SLOTS]),
                                ALU.mult).then_inc(s("diag"), 1)
            link(V.transpose(idxT[:, :], idxf[:, :]))
            for j in range(4):
                i = V.tensor_copy(idxcol[32 * j:32 * j + 32, :], idxT[:, j::4])
            link(i)
            for b in range(B):
                dve.wait_ge(s("ib_ps"), b + 1)
                for c in range(CB):
                    i = V.tensor_scalar(OH[:, CB * b + c, :], ps[:, b, :], iota_pc[:, c:c + 1], None, ALU.is_equal)
                i.then_inc(s("oh"), 1)

            def place(n):
                V.tensor_scalar(OHT[:, n, :], iota_row, idxcol[:, n:n + 1], None, ALU.is_equal).then_inc(s("oht"), 1)

            for b in range(B):
                place(2 * b)
                place(2 * b + 1)
                dve.wait_ge(s("qs_ps"), b + 1)
                V.scalar_tensor_tensor(out=Qbd[:, b, :, :], in0=ps[:, 2 + b, :].rearrange("p (h n) -> p h n", h=H),
                                       scalar=col("a_bq"), in1=hmask.unsqueeze(2).broadcast_to([P, H, SLOTS]),
                                       op0=ALU.add, op1=ALU.mult).then_inc(s("qbd"), 1)
            for n in range(B * G + 2):
                if n < B * G:
                    dve.wait_ge(s("ag_ps"), n + 1)
                    link(V.tensor_reduce(nmx[:, n:n + 1], ps[:, n % 2, :], AXX, ALU.max))
                    V.tensor_scalar(nb[:, n:n + 1], nmx[:, n:n + 1], -ASCALE, None, ALU.mult).then_inc(s("nb"), 1)
                if n < B * G - 4:
                    place(n + 4)
                m = n - 2
                if m >= 0:
                    b, g = m // G, m % G
                    dve.wait_ge(s("a_exp"), m + 1)
                    link(V.reciprocal(rinv[:, m:m + 1], rsum[:, m:m + 1]))
                    dve.wait_ge(s("pva_ps"), m + 1)
                    dve.wait_ge(s("vm"), B)
                    link(V.scalar_tensor_tensor(out=dgt[:, m, :], in0=ps[:, 4 + m % 2, 0:32], scalar=rinv[:, m:m + 1],
                                                in1=Vmb[:, b, 32 * g:32 * g + 32], op0=ALU.mult, op1=ALU.subtract))
                    V.tensor_tensor(dg[:, m, :], dgt[:, m, :], slotmask, ALU.mult).then_inc(s("dg"), 1)
            for b in range(B):
                dve.wait_ge(s("xb"), b + 1)
                add_residual(b, b, "x_up", "a_op_ps")
                ln_stats(1, b)
            ln_norm(1, 0)
            ln_norm(1, 1)

            def context(l, xbk, after):
                L = f"x{l}"
                for b in range(B):
                    dve.wait_ge(s("x_qh"), 2 * l + b + 1)
                    V.scalar_tensor_tensor(out=Ql[:, b, :], in0=ps[:, 4 + b, :], scalar=col(f"{L}_bq"), in1=Qh[:, b, :].bitcast(F32),
                                           op0=ALU.add, op1=ALU.subtract).then_inc(s("x_ql"), 1)

                def packed(m):
                    dve.wait_ge(s("x_pk_ps"), 8 * l + m + 1)
                    V.tensor_copy(Qp[:, m % G, (m // G) * S:(m // G + 1) * S],
                                  ps[:, m if m < G else 6 + m % 2, :]).then_inc(s("x_qp_v"), 1)

                packed(1)
                packed(3)
                def add_output(c):
                    dve.wait_ge(s("x_op_ps"), 8 * l + c + 1)
                    dve.wait_ge(s("xb"), xbk + c // CB + 1)
                    V.tensor_tensor(x_tm[:, c, :], ps[:, 6 + c % 2, 384:512], x_tm[:, c, :], ALU.add).then_inc(s("x_up"), 1)

                for n in range(NT + 4):
                    if n >= NT:
                        add_output(n - 4)
                    if 1 <= n <= 2:
                        packed(G + 2 * n - 1)
                    if n < NT:
                        for u in range(2):
                            if u == 1 and n >= 4:
                                add_output(n - 4)
                            dve.wait_ge(s("x_s_ps"), 16 * l + 2 * n + u + 1)
                            src = ps[:, 2 * u:2 * u + 2, 0:4 * NCP].rearrange("p v (h n) -> p v h n", n=NCP)[:, :, :, 0:NC]
                            m8 = mxx[:, n % 2, 8 * u:8 * u + 8]
                            link(V.tensor_reduce(m8.rearrange("p (v h) -> p v h", v=2), src, AXX, ALU.max))
                            if n >= 2 and u == 0:
                                dve.wait_ge(s("x_pt_ps"), 24 * l + 3 * (n - 1))
                            V.tensor_tensor(Ssb[:, n % 2, u * 8 * NC:(u + 1) * 8 * NC].rearrange("p (v h n) -> p v h n", v=2, h=4),
                                            src, m8.rearrange("p (v h) -> p v h", v=2).unsqueeze(3).broadcast_to([P, 2, 4, NC]),
                                            ALU.subtract).then_inc(s("x_sub"), 1)
                    c = n - 2
                    if 0 <= c < NT:
                        dve.wait_ge(s("x_pv_ps"), 8 * l + c + 1)
                        bank = ps[:, 6 + c % 2, :]
                        link(V.tensor_scalar(rsx[:, 0, :], bank[:, D:VW], 1e-9 if l == 0 else 0.0, None, ALU.add))
                        link(V.reciprocal(rsx[:, 1, :], rsx[:, 0, :]))
                        V.tensor_tensor(atm[:, c % 4, :].rearrange("p (h d) -> p h d", h=H),
                                        bank[:, 0:D].rearrange("p (h d) -> p h d", h=H),
                                        rsx[:, 1, :].unsqueeze(2).broadcast_to([P, H, HD]), ALU.mult).then_inc(s("x_atm"), 1)
                    if n == NT + 2:
                        ln_stats(after, 0)
                ln_stats(after, 1)
                ln_norm(after, 0)
                ln_norm(after, 1)

            context(0, 2, 2)

            dve.wait_ge(s("wmask"), 1)
            dve.wait_ge(s("in_ctx"), 16 * 5)
            for h in range(H):
                V.scalar_tensor_tensor(out=Wtab[:, h, :], in0=ident, scalar=ur[:, h:h + 1], in1=Wtab[:, h, :],
                                       op0=ALU.mult, op1=ALU.add)
            dve.wait_ge(s("m_en"), 1)
            dve.wait_ge(s("in_moe"), 16 * 3)
            link(V.tensor_scalar(sg[:, :, :], sg[:, :, :], 1.0, None, ALU.add))
            link(V.reciprocal(sg[:, :, :], sg[:, :, :]))
            link(V.tensor_tensor(sc[:, :, :], sg[:, :, :], eb_sb[:, :].unsqueeze(1).broadcast_to([P, NT, E]), ALU.add))
            s4 = sc[:, :, :].rearrange("p c (g e) -> p c g e", g=EG)

            def r4(i):
                return rt[:, :, 4 * i:4 * i + 4]

            V.tensor_tensor(r4(0), s4[:, :, :, 0], s4[:, :, :, 1], ALU.max)
            V.tensor_tensor(r4(1), s4[:, :, :, 0], s4[:, :, :, 1], ALU.min)
            V.tensor_tensor(r4(2), s4[:, :, :, 2], s4[:, :, :, 3], ALU.max)
            link(V.tensor_tensor(r4(3), s4[:, :, :, 2], s4[:, :, :, 3], ALU.min))
            V.tensor_tensor(r4(4), r4(0), r4(2), ALU.max)
            V.tensor_tensor(r4(5), r4(0), r4(2), ALU.min)
            link(V.tensor_tensor(r4(6), r4(1), r4(3), ALU.max))
            link(V.tensor_tensor(r4(5), r4(5), r4(6), ALU.max))
            V.tensor_tensor(r4(7), r4(4), r4(5), ALU.add).then_inc(s("pair_sum"), 1)

            def product(n):
                dve.wait_ge(s("m_silu"), n + 1)
                dve.wait_ge(s("u_ps"), n + 1)
                V.tensor_tensor(hs[:, n % NHS, :], hs[:, n % NHS, :], ps[:, 2 + n % 2, :], ALU.mult).then_inc(s("m_h1"), 1)

            product(0)
            dve.wait_ge(s("pair_sum"), 1)

            def rank_of(vals, cnt, dst, before, t1, t2):
                me = vals.unsqueeze(3).broadcast_to([P, NT, cnt, cnt])
                other = vals.unsqueeze(2).broadcast_to([P, NT, cnt, cnt])
                bm = before.unsqueeze(1).broadcast_to([P, NT, cnt, cnt])
                V.tensor_tensor(t1, other, me, ALU.is_gt)
                link(V.tensor_tensor(t2, other, me, ALU.is_equal))
                link(V.tensor_tensor(t2, t2, bm, ALU.mult))
                link(V.tensor_tensor(t1, t1, t2, ALU.add))
                link(V.reduce_sum(dst, t1, AXX))

            c1 = rt[:, :, 32:48].rearrange("p c (a b) -> p c a b", a=4)
            c2 = rt[:, :, 48:64].rearrange("p c (a b) -> p c a b", a=4)
            rank_of(r4(7), 4, r4(0), before4, c1, c2)
            product(1)
            link(V.tensor_scalar(r4(1), r4(0), 1.5, None, ALU.is_lt))
            link(V.memset(masked[:, :, E:E + 4], NEG))
            link(V.tensor_tensor(masked[:, :, 0:E].rearrange("p c (g e) -> p c g e", g=EG), s4,
                                 r4(1).unsqueeze(3).broadcast_to([P, NT, EG, 4]), ALU.mult))
            for c in range(NT):
                i = V.max(top8[:, c, :], masked[:, c, :])
            link(i)
            product(2)
            link(V.memset(top8[:, :, 4:8], NEG))
            for c in range(NT):
                i = V.match_replace(struck[:, c, :], top8[:, c, :], masked[:, c, :], STRUCK)
            link(i)
            product(3)
            link(V.tensor_scalar(rank[:, :, :], struck[:, :, 0:E], STRUCK, None, ALU.is_equal))
            link(V.tensor_tensor(rank[:, :, :], rank[:, :, :], sg[:, :, :], ALU.mult))
            link(V.reduce_sum(den[:, :], rank[:, :, :], AXX))
            link(V.tensor_scalar(den[:, :], den[:, :], 1e-20, None, ALU.add))
            link(V.reciprocal(den[:, :], den[:, :]))
            link(V.tensor_scalar(den[:, :], den[:, :], 2.5, None, ALU.mult))
            V.tensor_tensor(comb[:, :, :], rank[:, :, :], den[:, :].unsqueeze(2).broadcast_to([P, NT, E]),
                            ALU.mult).then_inc(s("comb"), 2)
            dve.wait_ge(s("filled"), 4)

            def split_weights(b):
                src, bs = ps[0:E, 5 + 2 * b, :], slice(b * S, (b + 1) * S)
                dve.wait_ge(s("cT_ps"), b + 1)
                V.tensor_copy(combr[0:E, bs], src).then_inc(s("combT"), 1)
                dve.wait_ge(s("combT"), 3 * b + 1)
                link(V.tensor_tensor(cr[0:E, :], src, combr[0:E, bs], ALU.subtract))
                V.tensor_copy(combr[32:32 + E, bs], cr[0:E, :]).then_inc(s("combT"), 1)
                link(V.tensor_copy(crb[0:E, :], cr[0:E, :]))
                V.tensor_tensor(combr[64:64 + E, bs], cr[0:E, :], crb[0:E, :], ALU.subtract).then_inc(s("combT"), 1)

            product(4)
            split_weights(0)
            for n in range(5, AHEAD - 2):
                product(n)
            for n in range(B * NM):
                b, i = n // NM, n % NM
                if n == 4:
                    split_weights(1)
                if n + AHEAD - 2 < B * NM:
                    product(n + AHEAD - 2)
                if i < NM - 1:
                    m = b * (NM - 1) + i
                    dve.wait_ge(s("m_h1"), n + 1)
                    dve.wait_ge(s("w_ps"), m + 1)
                    V.tensor_tensor(hs[:, n % NHS, :], hs[:, n % NHS, :], ps[:, 4 + m % 2, :], ALU.mult).then_inc(s("m_h2"), 1)
            for b in range(B):
                dve.wait_ge(s("dn_ps"), NM * (b + 1))
                cs = slice(CB * b, CB * b + CB)
                V.tensor_tensor(x_tm[:, cs, :], ps[:, 6 + b, :].rearrange("p (c d) -> p c d", c=CB), x_tm[:, cs, :],
                                ALU.add).then_inc(s("x_up"), CB)
                ln_stats(3, b)
            ln_norm(3, 0)
            ln_norm(3, 1)

            for b in range(B):
                dve.wait_ge(s("xnT"), 2 * 3 + b + 1)
                V.tensor_tensor(xx[:, b, :], xnT[:, b, 0:S], xnT[:, b, 1:S + 1], ALU.subtract).then_inc(s("mix"), 1)
                dve.wait_ge(s("mix"), 4 * b + 1)
                for i, n in ((2, "maa_r"), (0, "maa_k"), (1, "maa_v")):
                    V.scalar_tensor_tensor(out=mixes[:, i, b, :], in0=xx[:, b, :], scalar=col(n), in1=xnT[:, b, 1:S + 1],
                                           op0=ALU.mult, op1=ALU.add).then_inc(s("mix"), 1)
            dve.wait_ge(s("tabs"), 3)
            for b in range(B):
                cs = slice(CB * b, CB * b + CB)
                dve.wait_ge(s("r_rh"), b + 1)
                V.tensor_tensor(Rl[b], ps[:, 0, :], Rh[b].bitcast(F32), ALU.subtract).then_inc(s("r_kv"), 1)
                dve.wait_ge(s("r_kh"), b + 1)
                V.tensor_tensor(Kl[:, b, :], ps[:, 1, :], Kh[:, b, :].bitcast(F32), ALU.subtract).then_inc(s("r_kv"), 1)
                V.tensor_tensor(Rw[:, b, :].rearrange("p (c t) -> p c t", c=CB), ps[:, 0, :].rearrange("p (c t) -> p c t", c=CB),
                                rpow[:, :].unsqueeze(1).broadcast_to([P, CB, P]), ALU.mult).then_inc(s("r_kv"), 1)
                dve.wait_ge(s("r_pj_ps"), 5 * b + 3)
                V.tensor_tensor(Ktm[:, cs, :], ps[:, 2, :].rearrange("p (c d) -> p c d", c=CB),
                                kpow[:, :].unsqueeze(1).broadcast_to([P, CB, D]), ALU.mult).then_inc(s("r_kv"), 1)
                dve.wait_ge(s("r_pj_ps"), 5 * b + 4)
                V.tensor_copy(V_tm[:, cs, :], ps[:, 3, :].rearrange("p (c d) -> p c d", c=CB)).then_inc(s("r_kv"), 1)

            def r_centre(b):
                dve.wait_ge(s("r_mean_ps"), b + 1)
                V.scalar_tensor_tensor(out=yc[:, b, :], in0=ps[:, 6 + b, :], scalar=-1.0 / HD, in1=yc[:, b, :],
                                       op0=ALU.mult, op1=ALU.add).then_inc(s("r_yc"), 1)
                dve.wait_ge(s("r_yc"), b + 1)
                V.tensor_tensor(sq[:, b, :], yc[:, b, :], yc[:, b, :], ALU.mult).then_inc(s("r_sq"), 1)

            def r_variance(b):
                dve.wait_ge(s("r_var_ps"), b + 1)
                V.tensor_scalar(gv[:, b, :], ps[:, 6 + b, 0:CB * H], 1.0 / HD, 64e-5, ALU.mult, ALU.add).then_inc(s("r_var"), 1)

            def r_scale(b):
                r, t = gy[:, b, :], gn[:, b, :]
                dve.wait_ge(s("r_sd"), b + 1)
                link(V.reciprocal(r, t))
                link(V.tensor_tensor(t, r, gv[:, b, :], ALU.mult))
                link(V.scalar_tensor_tensor(out=t, in0=t, scalar=-0.5, in1=r, op0=ALU.mult, op1=ALU.mult))
                wide = [P, CB * H, HD]
                V.scalar_tensor_tensor(out=gx[b].rearrange("p (g d) -> p g d", d=HD), in0=t.unsqueeze(2).broadcast_to(wide),
                                       scalar=1.5, in1=r.unsqueeze(2).broadcast_to(wide), op0=ALU.add,
                                       op1=ALU.mult).then_inc(s("r_rs"), 1)

            def r_gate(b):
                y = yc[:, b, :]
                dve.wait_ge(s("r_sp_ps"), b + 1)
                link(V.tensor_tensor(y, y, ps[:, 6 + b, :], ALU.mult))
                link(V.tensor_scalar(y, y, col("hn_g"), col("hn_b"), ALU.mult, ALU.add))
                V.tensor_tensor(y, y, GT[:, b, :], ALU.mult).then_inc(s("r_yg"), 1)

            for m in range(NT):
                b, j = m // CB, m % CB
                for q in range(4):
                    dve.wait_ge(s("r_s_ps"), 4 * m + q + 1)
                    if m >= 2 and q == 0:
                        dve.wait_ge(s("y_ps"), m - 1)
                    V.tensor_tensor(Pr[:, m % 2, 4 * q:4 * q + 4, :], ps[:, q, :].rearrange("p (h t) -> p h t", h=4),
                                    Wtab[:, 4 * q:4 * q + 4, :], ALU.mult).then_inc(s("r_p"), 1)
                if j < CB - 1:
                    k = b * (CB - 1) + j
                    dve.wait_ge(s("u_st_ps"), k + 1)
                    if k >= 2:
                        dve.wait_ge(s("y_ps"), m)
                    if k:
                        dve.wait_ge(s("state"), k)
                    V.tensor_tensor(Um[:, :], ps[:, 5, 0:P], bdiag, ALU.mult).then_inc(s("um"), 1)
                    dve.wait_ge(s("um"), k + 1)
                    if j == 0:
                        V.tensor_copy(St[:, k % 2, :], Um[:, :]).then_inc(s("state"), 1)
                    else:
                        dve.wait_ge(s("state"), k)
                        V.scalar_tensor_tensor(out=St[:, k % 2, :], in0=St[:, (k - 1) % 2, :], scalar=w128, in1=Um[:, :],
                                               op0=ALU.mult, op1=ALU.add).then_inc(s("state"), 1)
                if m == CB + 1:
                    r_centre(0)
                if m == CB + 2:
                    r_variance(0)
            r_scale(0)
            r_centre(1)
            r_gate(0)
            r_variance(1)
            r_scale(1)

            def add_recurrence(b):
                dve.wait_ge(s("r_op_ps"), b + 1)
                cs = slice(CB * b, CB * b + CB)
                V.tensor_tensor(x_tm[:, cs, :], ps[:, 4 + b, :].rearrange("p (c d) -> p c d", c=CB), x_tm[:, cs, :],
                                ALU.add).then_inc(s("x_up"), CB)

            add_recurrence(0)
            ln_stats(4, 0)
            r_gate(1)
            ln_norm(4, 0)
            add_recurrence(1)
            ln_stats(4, 1)
            ln_norm(4, 1)

            context(1, 4, 5)

            for b in range(B):
                cs = range(CB * b, CB * b + CB)
                dve.wait_ge(s("xn"), 5 * NT + CB * (b + 1))
                for c in cs:
                    i = V.bn_stats(st[:, c, :], xn_tm[:, c, :])
                link(i)
                for c in cs:
                    i = V.bn_aggr(mv[:, c, :], st[:, c, :])
                link(i)
                V.tensor_scalar(veps[:, CB * b:CB * b + CB], mv[:, CB * b:CB * b + CB, 1], 1e-5, None,
                                ALU.add).then_inc(s("veps"), 1)
            dve.wait_ge(s("xnT_ps"), 12)
            for b in range(B):
                dve.wait_ge(s("rstd"), 2 * 6 + b + 1)
                for c in range(CB * b, CB * b + CB):
                    V.tensor_scalar(xn_tm[:, c, :], xn_tm[:, c, :], mv[:, c, 0:1], rstd[:, c:c + 1],
                                    ALU.subtract, ALU.mult).then_inc(s("hn2"), 1)
            def f_stats(c):
                dve.wait_ge(s("f_h_ps"), c + 1)
                for e in range(FE):
                    i = V.bn_stats(fst[:, e, :], ps[:, HB[c % 3] + e // 2, (e % 2) * FH:(e % 2 + 1) * FH])
                link(i)
                for e in range(FE):
                    i = V.bn_aggr(fmv[:, c, e, :], fst[:, e, :])
                link(i)
                V.tensor_scalar(fve[:, c, :], fmv[:, c, :, 1], 1e-5, None, ALU.add).then_inc(s("f_ve"), 1)

            def f_shift(c):
                dve.wait_ge(s("f_rs"), c + 1)
                V.scalar_tensor_tensor(out=fnm[:, c, :], in0=fmv[:, c, :, 0], scalar=-1.0, in1=frs[:, c, :],
                                       op0=ALU.mult, op1=ALU.mult).then_inc(s("f_st"), 1)
                e = FE - 1
                V.tensor_scalar(hn[c][:, e * FH:(e + 1) * FH], ps[:, HB[c % 3] + 1, FH:2 * FH], fmv[:, c, e, 0:1],
                                frs[:, c, e:e + 1], ALU.subtract, ALU.mult).then_inc(s("f_hv"), 1)

            def f_combine(c):
                dve.wait_ge(s("f_o_ps"), c + 1)
                bank = ps[:, 6 + c % 2, :]
                link(V.tensor_scalar(otm[:, c, :], bank[:, 0:P], fw[:, c, 0:1], None, ALU.mult))
                for e in range(1, FE):
                    i = V.scalar_tensor_tensor(out=otm[:, c, :], in0=bank[:, e * P:(e + 1) * P], scalar=fw[:, c, e:e + 1],
                                               in1=otm[:, c, :], op0=ALU.mult, op1=ALU.add)
                    if e < FE - 1:
                        link(i)
                i.then_inc(s("f_cmb"), 1)

            f_stats(0)
            f_stats(1)
            f_shift(0)
            f_shift(1)
            dve.wait_ge(s("fl_ps"), 1)
            lg = ps[:, 5, 0:NT * FE].rearrange("p (c e) -> p c e", e=FE)
            link(V.tensor_reduce(f1[:, :], lg, AXX, ALU.max))
            V.tensor_tensor(fsm[:, :, :], lg, f1[:, :].unsqueeze(2).broadcast_to([P, NT, FE]),
                            ALU.subtract).then_inc(s("fsub"), 1)
            f_stats(2)
            f_stats(3)
            f_shift(2)
            f_shift(3)
            dve.wait_ge(s("fexp"), 1)
            link(V.reduce_sum(f1[:, :], fsm[:, :, :], AXX))
            link(V.reciprocal(f1[:, :], f1[:, :]))
            link(V.tensor_tensor(fsm[:, :, :], fsm[:, :, :], f1[:, :].unsqueeze(2).broadcast_to([P, NT, FE]), ALU.mult))
            rank_of(fsm[:, :, :], FE, fw[:, :, :], before4, c1, c2)
            link(V.tensor_scalar(fw[:, :, :], fw[:, :, :], 1.5, None, ALU.is_lt))
            link(V.tensor_tensor(fw[:, :, :], fw[:, :, :], fsm[:, :, :], ALU.mult))
            link(V.reduce_sum(f1[:, :], fw[:, :, :], AXX))
            link(V.tensor_scalar(f1[:, :], f1[:, :], 1e-8, None, ALU.add))
            link(V.reciprocal(f1[:, :], f1[:, :]))
            link(V.tensor_tensor(fw[:, :, :], fw[:, :, :], f1[:, :].unsqueeze(2).broadcast_to([P, NT, FE]), ALU.mult))
            for c in range(CB, NT):
                f_stats(c)
                f_shift(c)

            def last_layernorm(b):
                cs = range(CB * b, CB * b + CB)
                sl = slice(CB * b, CB * b + CB)
                dve.wait_ge(s("f_cmb"), CB * (b + 1))
                for c in cs:
                    i = V.bn_stats(st[:, c, :], otm[:, c, :])
                link(i)
                for c in cs:
                    i = V.bn_aggr(mv[:, c, :], st[:, c, :])
                link(i)
                V.tensor_scalar(veps[:, sl], mv[:, sl, 1], 1e-5, None, ALU.add).then_inc(s("veps"), 1)
                dve.wait_ge(s("rstd"), 2 * 7 + b + 1)
                for c in cs:
                    i = V.tensor_scalar(otm[:, c, :], otm[:, c, :], mv[:, c, 0:1], rstd[:, c:c + 1], ALU.subtract, ALU.mult)
                link(i)
                link(V.tensor_tensor(otm[:, sl, :], otm[:, sl, :], row("on_g").unsqueeze(1).broadcast_to([P, CB, D]), ALU.mult))
                dve.wait_ge(s("xb"), 6 + b + 1)
                V.tensor_tensor(otm[:, sl, :], otm[:, sl, :], x_tm[:, sl, :], ALU.add).then_inc(s("final"), 1)

            for b in range(B):
                for j in range(CB):
                    f_combine(CB * b + j)
                last_layernorm(b)

        @block.gpsimd
        def _(pool):
            Gp = nc.gpsimd

            def inv_std(k):
                for b in range(B):
                    pool.wait_ge(s("veps"), 2 * k + b + 1)
                    sl = slice(CB * b, CB * b + CB)
                    Gp.tensor_tensor(rstd[:, sl], veps[:, sl], half[:, 0:CB], ALU.pow).then_inc(s("rstd"), 1)

            def with_bias(k, name):
                for b in range(B):
                    pool.wait_ge(s("xn"), NT * k + CB * (b + 1))
                    sl = slice(CB * b, CB * b + CB)
                    Gp.tensor_tensor(x_tm[:, sl, :], x_tm[:, sl, :], row(name).unsqueeze(1).broadcast_to([P, CB, D]),
                                     ALU.add).then_inc(s("xb"), 1)

            def repeat_context():
                for b in range(B):
                    Gp.tensor_copy(ctxrep[:, b * NB * P:b * NB * P + HK].rearrange("p (h n) -> p h n", h=H),
                                   ctxT[:, b, 0:NC].unsqueeze(1).broadcast_to([P, H, NC]))
                    i = Gp.memset(ctxrep[:, b * NB * P + HK:(b + 1) * NB * P], 0.0)
                i.then_inc(s("ctxrep"), 1)

            def split_keys(l):
                pool.wait_ge(s("pre"), 9 * l + 1)
                Gp.tensor_copy(Kxh[:, :], Kx[:, :]).then_inc(s("kxh"), 1)
                pool.wait_ge(s("kxh"), l + 1)
                Gp.tensor_tensor(Kxl[:, :], Kx[:, :], Kxh[:, :].bitcast(F32), ALU.subtract).then_inc(s("kx"), 1)

            def value_blocks(l):
                for b in range(B):
                    pool.wait_ge(s("pre"), 9 * l + 3 + 3 * (b + 1))
                    v = Vbdx[:, b, :, :]
                    raw = v[:, :, 0:P] if l == 0 else Vraw[:, b, :, :]
                    Gp.tensor_tensor(v[:, :, 0:P], raw, row(f"x{l}_bv").unsqueeze(1).broadcast_to([P, NB, P]),
                                     ALU.add).then_inc(s("vb"), 1)
                    if l == 0:
                        Gp.tensor_copy(v[:, :, P:VW], bdx_sb[:, :, P:VW])
                    pool.wait_ge(s("vb"), 2 * l + b + 1)
                    Gp.tensor_tensor(v[:, :, 0:P], v[:, :, 0:P], bdx_sb[:, :, 0:P], ALU.mult).then_inc(s("vbdx"), 1)

            Gp.memset(half[:, :], -0.5).then_inc(s("filled"), 1)
            Gp.memset(xnT[:, :, 0:1], 0.0).then_inc(s("filled"), 1)
            Gp.memset(sel4[:, :, :].bitcast(F32), 0.0).then_inc(s("filled"), 1)
            pool.wait_ge(s("filled"), 1)
            inv_std(0)
            pool.wait_ge(s("in_first"), 16 * 3)
            pool.wait_ge(s("filled"), 3)
            for t, where in terms.items():
                i = Gp.tensor_copy(sel4[:, t, :].rearrange("p (h t d) -> p h t d", t=4, d=HD)[:, :, where, :],
                                   ident.rearrange("p (h d) -> p h d", d=HD).unsqueeze(2).broadcast_to([P, H, 2, HD]))
            i = Gp.tensor_copy(ones_r[:, :], ones[0:32, :])
            i.then_inc(s("sel"), 1)
            pool.wait_ge(s("in_ctx"), 16 * 5)
            repeat_context()
            pool.wait_ge(s("in_attn"), 16 * 3)
            with_bias(0, "a_bo")
            pool.wait_ge(s("lam"), 2)
            Gp.tensor_scalar(lamr[:, :], lamr[:, :], 3.0e38, None, ALU.min).then_inc(s("lam_ok"), 1)
            Gp.tensor_scalar(lamc[:, 0:1], lamc[:, 0:1], 3.0e38, None, ALU.min).then_inc(s("lam_ok"), 1)
            pool.wait_ge(s("lam_ok"), 2)
            Gp.tensor_scalar(lamc[:, 1:2], lamc[:, 0:1], -1.0, None, ALU.mult).then_inc(s("lam_ok"), 2)

            split_keys(0)
            value_blocks(0)
            Gp.tensor_tensor(Wtab[:, :, :], gapT.unsqueeze(1).broadcast_to([P, H, P]),
                             lamr[:, ::HD].unsqueeze(2).broadcast_to([P, H, P]), ALU.mult).then_inc(s("gap"), 1)
            pool.wait_ge(s("wexp"), 1)
            Gp.tensor_tensor(Wtab[:, :, :], Wtab[:, :, :], causal.unsqueeze(1).broadcast_to([P, H, P]),
                             ALU.mult).then_inc(s("wmask"), 1)
            split_keys(1)
            inv_std(1)
            with_bias(1, "x0_bo")
            inv_std(2)
            Gp.memset(combr, 0.0).then_inc(s("filled"), 1)
            pool.wait_ge(s("pre"), 18)
            pool.wait_ge(s("x_pv_ps"), NT)
            for j in range(4):
                Gp.tensor_scalar(Kbp[:, :, j, :], Kpk[:, :, :], quad[:, j:j + 1], None, ALU.mult).then_inc(s("x1_keys"), 1)
            value_blocks(1)
            inv_std(3)
            for b in range(B):
                pool.wait_ge(s("mix"), 4 * b + 1)
                Gp.tensor_scalar(mixes[:, 3, b, :], xx[:, b, :], col("maa_g"), None, ALU.mult).then_inc(s("mix_gx"), 1)
                pool.wait_ge(s("mix_gx"), b + 1)
                Gp.tensor_tensor(mixes[:, 3, b, :], mixes[:, 3, b, :], xnT[:, b, 1:S + 1], ALU.add).then_inc(s("mix_g"), 1)
            pool.wait_ge(s("r_pj_ps"), 5 * B)
            Gp.memset(Vx[:, :, :, :], 0.0).then_inc(s("filled"), 1)
            pool.wait_ge(s("filled"), 5)
            for c in range(NT):
                pool.wait_ge(s("r_kv"), 5 * (c // CB + 1))
                if c >= 2:
                    pool.wait_ge(s("y_ps"), c - 1)
                o = 2048 * (c % 2)
                Gp.tensor_copy(big[:, o:o + H * (P + HD)].rearrange("p (h n) -> p h n", h=H)[:, :, 0:HD],
                               V_tm[:, c, :].rearrange("p (h d) -> p h d", h=H)).then_inc(s("vx"), 1)
            inv_std(4)
            with_bias(4, "x1_bo")
            inv_std(5)
            inv_std(6)
            with_bias(5, "on_b")
            for c in range(NT):
                pool.wait_ge(s("f_ve"), c + 1)
                Gp.tensor_tensor(frs[:, c, :], fve[:, c, :], half[:, 0:FE], ALU.pow).then_inc(s("f_rs"), 1)
            inv_std(7)


def kernel(**inputs):
    import numpy as np
    import ml_dtypes
    import concourse.bacc as bacc
    from concourse.bass_utils import run_bass_kernel_spmd

    a = {n: np.asarray(v) for n, v in inputs.items()}
    f = np.float32
    p = np.arange(P)

    def every(v):
        return np.broadcast_to(v, (P,) + v.shape)

    def side(parts):
        return np.concatenate(parts, axis=1)

    same_head = (p[:, None] // HD == p[None, :] // HD).astype(f)
    gap = np.maximum(p[None, :] - p[:, None] - 1, 0).astype(f)
    causal = (p[None, :] > p[:, None]).astype(f)
    consts = side([np.eye(P, dtype=f), np.ones((P, P), f), np.full((P, P), 1.0 / S, f), gap, causal, same_head,
                   every(np.arange(S, dtype=f))])
    before4 = (np.arange(4)[None, :] < np.arange(4)[:, None]).astype(f).reshape(-1)
    small = side([(p[:, None] // HD == np.arange(H)[None, :]).astype(f),
                  (p[:, None] + P * np.arange(CB)[None, :]).astype(f),
                  ((p[:, None] // SLOTS == np.arange(32)[None, :] // HD) & (p[:, None] % SLOTS < TOPK)).astype(f),
                  every(before4), every(np.arange(P, dtype=f)),
                  (p[:, None] - (P - 1)).astype(f), np.zeros((P, 1), f),
                  (p[:, None] // 32 == np.arange(4)[None, :]).astype(f)])
    r = p[:, None] + P * np.arange(NB)[None, :]
    cols_v = np.arange(VW)
    bdx = ((r[:, :, None] < HK) & (r[:, :, None] // NC == np.where(cols_v < D, cols_v // HD, cols_v - D))).astype(f)
    unit = np.arange(P)
    selx = np.zeros((P, 8, P), f)
    for m in range(8):
        for part in range(3):
            selx[32 * part + 2 * m + unit // 64, m, unit] = 1
    selx = selx.reshape(P, -1).astype(ml_dtypes.bfloat16)

    A0, X0, F0, R1, X1, F1 = "L0_attn_", "L0_xattn_", "L0_ffn_", "L1_attn_", "L1_xattn_", "L1_ffn_"
    td_row = np.repeat(a[R1 + "time_decay"], HD)
    cols = np.stack([a[A0 + "bq"], a[A0 + "bk"], a[X0 + "bq"], a[X0 + "bk"], a[X1 + "b_q"], a[X1 + "b_k"],
                     a[R1 + "time_maa_k"], a[R1 + "time_maa_v"], a[R1 + "time_maa_r"], a[R1 + "time_maa_g"],
                     td_row, a[F1 + "rn_g"], a[F1 + "rn_b"], a[R1 + "ln_g"], a[R1 + "ln_b"]], axis=1)
    cols = side([cols, a[F1 + "ln_g"].reshape(8, P).T, a[F1 + "ln_b"].reshape(8, P).T])
    rows = every(np.concatenate([a[A0 + "bv"], a[A0 + "bo"], a[X0 + "bv"], a[X0 + "bo"], a[X1 + "b_v"], a[X1 + "b_o"],
                                 a[F1 + "on_g"], a[F1 + "on_b"]]))
    wa = side([a[A0 + n] for n in ("Wq", "Wk", "Wv", "Wo")])
    wb = side([a[X0 + n].T for n in ("Wq", "Wk", "Wv", "Wo")] + [a[X1 + n].T for n in ("W_q", "W_k", "W_v", "W_o")])
    wr = side([a[R1 + n].T for n in ("w_r", "w_k", "w_v", "w_g", "w_o")])
    wm = side([a[F0 + "gate_w"].reshape(-1, D).T, a[F0 + "sh_gate_w"].T, a[F0 + "up_w"].reshape(-1, D).T,
               a[F0 + "sh_up_w"].T,
               a[F0 + "down_w"].transpose(0, 2, 1).reshape(8, P, D).transpose(1, 0, 2).reshape(P, -1),
               a[F0 + "sh_down_w"].T])
    w1 = a[F1 + "w1"].transpose(1, 0, 2).reshape(D, -1)
    w2 = a[F1 + "w2"].reshape(8, P, D).transpose(1, 0, 2).reshape(P, -1)
    given = {
        "x": a["x"], "sidx": every(a[A0 + "sample_idx"]), "consts": consts, "small": small, "selx": selx, "bdx": bdx,
        "cols": cols, "rows": rows, "wa": wa, "wb": wb, "ctxt": np.pad(a["ctx_1024"].transpose(2, 0, 1), ((0, 0), (0, 0), (0, NCP - NC))), "wm": wm,
        "rw": a[F0 + "router_weight"].T, "wr": wr, "tdrow": every(td_row), "urow": every(a[R1 + "time_faaaa"]),
        "w1": w1, "w2": w2, "rwf": a[F1 + "router_w"].T, "ebias": every(a[F0 + "e_bias"]),
    }
    nc = bacc.Bacc("TRN2", target_bir_lowering=False, num_devices=1)
    arrays, args = {}, []
    for n, v in given.items():
        arrays[f"{n}_dram"] = np.ascontiguousarray(v)
        args.append(nc.dram_tensor(f"{n}_dram", v.shape, mybir.dt.from_np(v.dtype), kind="ExternalInput").ap())
    args.append(nc.dram_tensor("out_dram", (B, S, D), F32, kind="ExternalOutput").ap())
    build(nc, *args)
    return run_bass_kernel_spmd(nc, [arrays], core_ids=[0]).results[0]["out_dram"]
```
